# Optimizing a Trainium2 kernel written in Bass

```python
import numpy as np
import jax
import jax.numpy as jnp

def _softmax(x, axis=-1):
    return jax.nn.softmax(x, axis=axis)

def _gelu(x):
    return jax.nn.gelu(x, approximate=True)

def _silu(x):
    return jax.nn.silu(x)

def _sigmoid(x):
    return jax.nn.sigmoid(x)

def _layernorm(x, axis=-1, eps=1e-05):
    m = jnp.mean(x, axis=axis, keepdims=True)
    v = jnp.var(x, axis=axis, keepdims=True)
    return (x - m) / jnp.sqrt(v + eps)

def _scatter_add(tgt, idx, src, axis=0):
    return tgt.at[idx].add(src)

def _segment_sum(src, seg, n):
    return jax.ops.segment_sum(src, seg, n)
kernel_name = 'mk_adaln_attn_ffn_d2_seqx_r8_0881a5'

def setup_inputs(seed: int=0):
    np.random.seed(seed)
    _w = jnp.asarray

    def _rec_inputs():
        import jax
        import jax.numpy as jnp
        _rk = jax.random.key(seed)
        x = -0.000125 + 0.9999 * jax.random.normal(jax.random.fold_in(_rk, 1), (64, 32, 512), jnp.float32)
        _lenS = 32 - jax.random.randint(jax.random.fold_in(_rk, 7), (64,), 0, max(1, 32 // 4) + 1, jnp.int32)
        _lenS2 = 32 - jax.random.randint(jax.random.fold_in(_rk, 8), (64,), 0, max(1, 32 // 4) + 1, jnp.int32)
        cond_128 = 0.0061147 + 1.02565 * jax.random.normal(jax.random.fold_in(_rk, 11), (64, 128), jnp.float32)
        fside_S_0 = -0.022604 + 0.987366 * jax.random.normal(jax.random.fold_in(_rk, 12), (32,), jnp.float32)
        return (x, cond_128, fside_S_0)
    x, cond_128, fside_S_0 = _rec_inputs()

    def _L0_cond_setup():
        import jax, jax.numpy as jnp
        import numpy as np
        K = 8
        T = 1.0
        D_EMBD = 128
        IN_C = 32
        OUT_C = 32
        BS = 32
        H = 512
        HID = 128
        key = jax.random.key(seed)
        ks = jax.random.split(key, 10)
        s = lambda fan_in: 1.0 / np.sqrt(fan_in)
        return {'x': jax.random.normal(ks[0], (BS, IN_C, H), dtype=jnp.float32), 'embedding': jax.random.normal(ks[1], (BS, D_EMBD), dtype=jnp.float32), 'W0': jax.random.normal(ks[2], (D_EMBD, HID), dtype=jnp.float32) * s(D_EMBD), 'b0': jnp.zeros((HID,), dtype=jnp.float32), 'W1': jax.random.normal(ks[3], (HID, HID), dtype=jnp.float32) * s(HID), 'b1': jnp.zeros((HID,), dtype=jnp.float32), 'W2': jax.random.normal(ks[4], (HID, K), dtype=jnp.float32) * s(HID), 'b2': jnp.zeros((K,), dtype=jnp.float32), 'weight': jax.random.normal(ks[5], (K, OUT_C, IN_C, 1), dtype=jnp.float32) * s(IN_C), 'bias_k': jax.random.normal(ks[6], (K, OUT_C), dtype=jnp.float32) * 0.1}
    _L0_cond_all = _L0_cond_setup()
    _L0_cond_in = {k: v for k, v in _L0_cond_all.items() if k in ('W0', 'b0', 'W1', 'b1', 'W2', 'b2', 'weight', 'bias_k')}
    del _L0_cond_all

    def _L0_attn_setup():
        import jax, jax.numpy as jnp
        import numpy as np
        B, N, D = (8, 128, 512)
        H = 8
        HEAD_DIM = D // H
        E = HEAD_DIM // H
        key = jax.random.key(seed)
        ks = jax.random.split(key, 7)
        s = 0.02
        return {'x': jax.random.normal(ks[0], (B, N, D), dtype=jnp.float32), 'Wqk_w': jax.random.normal(ks[1], (2 * HEAD_DIM, D), dtype=jnp.float32) * s, 'Wqk_b': jnp.zeros((2 * HEAD_DIM,), dtype=jnp.float32), 'Wv_w': jax.random.normal(ks[2], (HEAD_DIM, D), dtype=jnp.float32) * s, 'Wv_b': jnp.zeros((HEAD_DIM,), dtype=jnp.float32), 'Wo_w': jax.random.normal(ks[3], (D, HEAD_DIM), dtype=jnp.float32) * s, 'Wo_b': jnp.zeros((D,), dtype=jnp.float32)}
    _L0_attn_all = _L0_attn_setup()
    _L0_attn_in = {k: v for k, v in _L0_attn_all.items() if k in ('Wqk_w', 'Wqk_b', 'Wv_w', 'Wv_b', 'Wo_w', 'Wo_b')}
    del _L0_attn_all

    def _L0_cond2_setup():
        import jax, jax.numpy as jnp
        import numpy as np
        from jax import lax
        N, C_IN, L = (32, 32, 512)
        C_OUT, K, GROUPS = (32, 9, 4)
        C_DIM, PAD, STRIDE = (128, 4, 1)
        key = jax.random.key(seed)
        k1, k2, k3, k4, k5 = jax.random.split(key, 5)
        x = jax.random.normal(k1, (N, C_IN, L), dtype=jnp.float32)
        c = jax.random.normal(k2, (N, C_DIM), dtype=jnp.float32)
        weight = jax.random.normal(k3, (C_OUT, C_IN // GROUPS, K), dtype=jnp.float32)
        c_weight = jax.random.normal(k4, (C_OUT, C_DIM), dtype=jnp.float32)
        bias = jax.random.normal(k5, (C_OUT,), dtype=jnp.float32)
        return {'x': x, 'c': c, 'weight': weight, 'c_weight': c_weight, 'bias': bias}
    _L0_cond2_all = _L0_cond2_setup()
    _L0_cond2_in = {k: v for k, v in _L0_cond2_all.items() if k in ('weight', 'c_weight')}
    del _L0_cond2_all

    def _L0_ffn_setup():
        import jax, jax.numpy as jnp
        import numpy as np
        HID, INT, LAT, NE, K = (512, 1024, 256, 8, 2)
        LN_EPS = 1e-05

        def _layernorm(x, gamma, beta):
            mu = jnp.mean(x, axis=-1, keepdims=True)
            var = jnp.var(x, axis=-1, keepdims=True)
            return (x - mu) * jax.lax.rsqrt(var + LN_EPS) * gamma + beta
        key = jax.random.key(seed)
        ks = jax.random.split(key, 8)
        s = lambda d: 1.0 / np.sqrt(d)
        return {'hidden_states': jax.random.normal(ks[0], (4, 256, HID), jnp.float32), 'gate_w': jax.random.normal(ks[1], (HID, NE), jnp.float32) * s(HID), 'up_w': jax.random.normal(ks[2], (HID, INT), jnp.float32) * s(HID), 'down_w': jax.random.normal(ks[3], (INT, HID), jnp.float32) * s(INT), 'fc1_w': jax.random.normal(ks[4], (HID, LAT), jnp.float32) * s(HID), 'fc2_w': jax.random.normal(ks[5], (LAT, HID), jnp.float32) * s(LAT), 'expert_w': jax.random.normal(ks[6], (LAT, LAT), jnp.float32), 'ln_gamma': jnp.ones((HID,), jnp.float32), 'ln_beta': jnp.zeros((HID,), jnp.float32)}
    _L0_ffn_all = _L0_ffn_setup()
    _L0_ffn_in = {k: v for k, v in _L0_ffn_all.items() if k in ('gate_w', 'up_w', 'down_w', 'fc1_w', 'fc2_w', 'expert_w', 'ln_gamma', 'ln_beta')}
    del _L0_ffn_all

    def _L1_cond_setup():
        import jax, jax.numpy as jnp
        import numpy as np
        K = 8
        T = 1.0
        D_EMBD = 128
        IN_C = 32
        OUT_C = 32
        BS = 32
        H = 512
        HID = 128
        key = jax.random.key(seed)
        ks = jax.random.split(key, 10)
        s = lambda fan_in: 1.0 / np.sqrt(fan_in)
        return {'x': jax.random.normal(ks[0], (BS, IN_C, H), dtype=jnp.float32), 'embedding': jax.random.normal(ks[1], (BS, D_EMBD), dtype=jnp.float32), 'W0': jax.random.normal(ks[2], (D_EMBD, HID), dtype=jnp.float32) * s(D_EMBD), 'b0': jnp.zeros((HID,), dtype=jnp.float32), 'W1': jax.random.normal(ks[3], (HID, HID), dtype=jnp.float32) * s(HID), 'b1': jnp.zeros((HID,), dtype=jnp.float32), 'W2': jax.random.normal(ks[4], (HID, K), dtype=jnp.float32) * s(HID), 'b2': jnp.zeros((K,), dtype=jnp.float32), 'weight': jax.random.normal(ks[5], (K, OUT_C, IN_C, 1), dtype=jnp.float32) * s(IN_C), 'bias_k': jax.random.normal(ks[6], (K, OUT_C), dtype=jnp.float32) * 0.1}
    _L1_cond_all = _L1_cond_setup()
    _L1_cond_in = {k: v for k, v in _L1_cond_all.items() if k in ('W0', 'b0', 'W1', 'b1', 'W2', 'b2', 'weight', 'bias_k')}
    del _L1_cond_all

    def _L1_attn_setup():
        import jax, jax.numpy as jnp
        import numpy as np
        HIDDEN = 512
        NUM_HEADS = 32
        NUM_KV_HEADS = 8
        HEAD_DIM = HIDDEN // NUM_HEADS
        N_REP = NUM_HEADS // NUM_KV_HEADS
        B, S = (1, 256)
        ACT_BITS = 8
        QB = 2 ** (ACT_BITS - 1) - 1
        ROPE_BASE = 10000.0
        LN_EPS = 1e-05

        def _act_quant(x):
            scale = QB / jnp.clip(jnp.max(jnp.abs(x), axis=-1, keepdims=True), 1e-05, None)
            q = jnp.clip(jnp.round(x * scale), -QB - 1, QB) / scale
            return x + jax.lax.stop_gradient(q - x)

        def _weight_quant(w):
            scale = 1.0 / jnp.clip(jnp.mean(jnp.abs(w)), 1e-05, None)
            q = jnp.clip(jnp.round(w * scale), -1.0, 1.0) / scale
            return w + jax.lax.stop_gradient(q - w)

        def _bitlinear(x, w):
            return jnp.einsum('...i,oi->...o', _act_quant(x), _weight_quant(w))

        def _layernorm(x, g, b):
            mu = jnp.mean(x, axis=-1, keepdims=True)
            var = jnp.mean(jnp.square(x - mu), axis=-1, keepdims=True)
            return (x - mu) * jax.lax.rsqrt(var + LN_EPS) * g + b

        def _rope(x):
            s, d = (x.shape[2], x.shape[3])
            inv_freq = 1.0 / ROPE_BASE ** (jnp.arange(0, d, 2, dtype=jnp.float32) / d)
            freqs = jnp.arange(s, dtype=jnp.float32)[:, None] * inv_freq[None, :]
            emb = jnp.concatenate([freqs, freqs], axis=-1)
            cos, sin = (jnp.cos(emb), jnp.sin(emb))
            x1, x2 = jnp.split(x, 2, axis=-1)
            rot = jnp.concatenate([-x2, x1], axis=-1)
            return x * cos + rot * sin
        key = jax.random.key(seed)
        ks = jax.random.split(key, 5)
        hidden_states = jax.random.normal(ks[0], (B, S, HIDDEN), dtype=jnp.float32)
        std = 0.02
        Wq = jax.random.normal(ks[1], (HIDDEN, HIDDEN), dtype=jnp.float32) * std
        Wk = jax.random.normal(ks[2], (NUM_KV_HEADS * HEAD_DIM, HIDDEN), dtype=jnp.float32) * std
        Wv = jax.random.normal(ks[3], (NUM_KV_HEADS * HEAD_DIM, HIDDEN), dtype=jnp.float32) * std
        Wo = jax.random.normal(ks[4], (HIDDEN, HIDDEN), dtype=jnp.float32) * std
        ln_w = jnp.ones((HIDDEN,), dtype=jnp.float32)
        ln_b = jnp.zeros((HIDDEN,), dtype=jnp.float32)
        return {'hidden_states': hidden_states, 'ln_w': ln_w, 'ln_b': ln_b, 'Wq': Wq, 'Wk': Wk, 'Wv': Wv, 'Wo': Wo}
    _L1_attn_all = _L1_attn_setup()
    _L1_attn_in = {k: v for k, v in _L1_attn_all.items() if k in ('ln_w', 'ln_b', 'Wq', 'Wk', 'Wv', 'Wo')}
    del _L1_attn_all

    def _L1_cond2_setup():
        import jax, jax.numpy as jnp
        import numpy as np
        K = 8
        T = 1.0
        D_EMBD = 128
        IN_C = 32
        OUT_C = 32
        BS = 32
        H = 512
        HID = 128
        key = jax.random.key(seed)
        ks = jax.random.split(key, 10)
        s = lambda fan_in: 1.0 / np.sqrt(fan_in)
        return {'x': jax.random.normal(ks[0], (BS, IN_C, H), dtype=jnp.float32), 'embedding': jax.random.normal(ks[1], (BS, D_EMBD), dtype=jnp.float32), 'W0': jax.random.normal(ks[2], (D_EMBD, HID), dtype=jnp.float32) * s(D_EMBD), 'b0': jnp.zeros((HID,), dtype=jnp.float32), 'W1': jax.random.normal(ks[3], (HID, HID), dtype=jnp.float32) * s(HID), 'b1': jnp.zeros((HID,), dtype=jnp.float32), 'W2': jax.random.normal(ks[4], (HID, K), dtype=jnp.float32) * s(HID), 'b2': jnp.zeros((K,), dtype=jnp.float32), 'weight': jax.random.normal(ks[5], (K, OUT_C, IN_C, 1), dtype=jnp.float32) * s(IN_C), 'bias_k': jax.random.normal(ks[6], (K, OUT_C), dtype=jnp.float32) * 0.1}
    _L1_cond2_all = _L1_cond2_setup()
    _L1_cond2_in = {k: v for k, v in _L1_cond2_all.items() if k in ('W0', 'b0', 'W1', 'b1', 'W2', 'b2', 'weight', 'bias_k')}
    del _L1_cond2_all

    def _L1_ffn_setup():
        import jax, jax.numpy as jnp
        import numpy as np
        NUM_EXPERTS = 16
        TOP_K = 2
        INTER = 56
        key = jax.random.key(seed)
        k1, k2, k3, k4, k5 = jax.random.split(key, 5)
        B, S, H = (4, 256, 512)
        scale = 0.02
        return {'hid': jax.random.normal(k1, (B, S, H), dtype=jnp.float32), 'gate_w': jax.random.normal(k2, (NUM_EXPERTS, H), dtype=jnp.float32) * scale, 'u': jax.random.normal(k3, (NUM_EXPERTS * INTER, H), dtype=jnp.float32) * scale, 'g': jax.random.normal(k4, (NUM_EXPERTS * INTER, H), dtype=jnp.float32) * scale, 'd': jax.random.normal(k5, (H, NUM_EXPERTS * INTER), dtype=jnp.float32) * scale}
    _L1_ffn_all = _L1_ffn_setup()
    _L1_ffn_in = {k: v for k, v in _L1_ffn_all.items() if k in ('gate_w', 'u', 'g', 'd')}
    del _L1_ffn_all
    return {'x': x, 'cond_128': cond_128, 'fside_S_0': fside_S_0, 'L0_cond_W0': _L0_cond_in['W0'], 'L0_cond_b0': _L0_cond_in['b0'], 'L0_cond_W1': _L0_cond_in['W1'], 'L0_cond_b1': _L0_cond_in['b1'], 'L0_cond_W2': _L0_cond_in['W2'], 'L0_cond_b2': _L0_cond_in['b2'], 'L0_cond_weight': _L0_cond_in['weight'], 'L0_cond_bias_k': _L0_cond_in['bias_k'], 'L0_attn_Wqk_w': _L0_attn_in['Wqk_w'], 'L0_attn_Wqk_b': _L0_attn_in['Wqk_b'], 'L0_attn_Wv_w': _L0_attn_in['Wv_w'], 'L0_attn_Wv_b': _L0_attn_in['Wv_b'], 'L0_attn_Wo_w': _L0_attn_in['Wo_w'], 'L0_attn_Wo_b': _L0_attn_in['Wo_b'], 'L0_cond2_weight': _L0_cond2_in['weight'], 'L0_cond2_c_weight': _L0_cond2_in['c_weight'], 'L0_ffn_gate_w': _L0_ffn_in['gate_w'], 'L0_ffn_up_w': _L0_ffn_in['up_w'], 'L0_ffn_down_w': _L0_ffn_in['down_w'], 'L0_ffn_fc1_w': _L0_ffn_in['fc1_w'], 'L0_ffn_fc2_w': _L0_ffn_in['fc2_w'], 'L0_ffn_expert_w': _L0_ffn_in['expert_w'], 'L0_ffn_ln_gamma': _L0_ffn_in['ln_gamma'], 'L0_ffn_ln_beta': _L0_ffn_in['ln_beta'], 'L1_cond_W0': _L1_cond_in['W0'], 'L1_cond_b0': _L1_cond_in['b0'], 'L1_cond_W1': _L1_cond_in['W1'], 'L1_cond_b1': _L1_cond_in['b1'], 'L1_cond_W2': _L1_cond_in['W2'], 'L1_cond_b2': _L1_cond_in['b2'], 'L1_cond_weight': _L1_cond_in['weight'], 'L1_cond_bias_k': _L1_cond_in['bias_k'], 'L1_attn_ln_w': _L1_attn_in['ln_w'], 'L1_attn_ln_b': _L1_attn_in['ln_b'], 'L1_attn_Wq': _L1_attn_in['Wq'], 'L1_attn_Wk': _L1_attn_in['Wk'], 'L1_attn_Wv': _L1_attn_in['Wv'], 'L1_attn_Wo': _L1_attn_in['Wo'], 'L1_cond2_W0': _L1_cond2_in['W0'], 'L1_cond2_b0': _L1_cond2_in['b0'], 'L1_cond2_W1': _L1_cond2_in['W1'], 'L1_cond2_b1': _L1_cond2_in['b1'], 'L1_cond2_W2': _L1_cond2_in['W2'], 'L1_cond2_b2': _L1_cond2_in['b2'], 'L1_cond2_weight': _L1_cond2_in['weight'], 'L1_cond2_bias_k': _L1_cond2_in['bias_k'], 'L1_ffn_gate_w': _L1_ffn_in['gate_w'], 'L1_ffn_u': _L1_ffn_in['u'], 'L1_ffn_g': _L1_ffn_in['g'], 'L1_ffn_d': _L1_ffn_in['d']}

def reference(x, cond_128, fside_S_0, L0_cond_W0, L0_cond_b0, L0_cond_W1, L0_cond_b1, L0_cond_W2, L0_cond_b2, L0_cond_weight, L0_cond_bias_k, L0_attn_Wqk_w, L0_attn_Wqk_b, L0_attn_Wv_w, L0_attn_Wv_b, L0_attn_Wo_w, L0_attn_Wo_b, L0_cond2_weight, L0_cond2_c_weight, L0_ffn_gate_w, L0_ffn_up_w, L0_ffn_down_w, L0_ffn_fc1_w, L0_ffn_fc2_w, L0_ffn_expert_w, L0_ffn_ln_gamma, L0_ffn_ln_beta, L1_cond_W0, L1_cond_b0, L1_cond_W1, L1_cond_b1, L1_cond_W2, L1_cond_b2, L1_cond_weight, L1_cond_bias_k, L1_attn_ln_w, L1_attn_ln_b, L1_attn_Wq, L1_attn_Wk, L1_attn_Wv, L1_attn_Wo, L1_cond2_W0, L1_cond2_b0, L1_cond2_W1, L1_cond2_b1, L1_cond2_W2, L1_cond2_b2, L1_cond2_weight, L1_cond2_bias_k, L1_ffn_gate_w, L1_ffn_u, L1_ffn_g, L1_ffn_d):
    import jax
    import jax.numpy as jnp

    def _L0_cond_ref(x, embedding, W0, b0, W1, b1, W2, b2, weight, bias_k):
        import jax, jax.numpy as jnp
        import numpy as np
        K = 8
        T = 1.0
        D_EMBD = 128
        IN_C = 32
        OUT_C = 32
        BS = 32
        H = 512
        HID = 128
        h = jax.nn.gelu(embedding @ W0 + b0, approximate=False)
        h = jax.nn.gelu(h @ W1 + b1, approximate=False)
        att = jax.nn.softmax((h @ W2 + b2) / T, axis=-1)
        agg_w = jnp.einsum('bk,koi->boi', att, weight[..., 0])
        agg_b = att @ bias_k
        out = jnp.einsum('boi,bih->boh', agg_w, x) + agg_b[:, :, None]
        return out

    def _L0_attn_ref(x, Wqk_w, Wqk_b, Wv_w, Wv_b, Wo_w, Wo_b):
        import jax, jax.numpy as jnp
        import numpy as np
        B, N, D = (8, 128, 512)
        H = 8
        HEAD_DIM = D // H
        E = HEAD_DIM // H
        b, n, _ = x.shape
        qk = (x @ Wqk_w.T + Wqk_b).reshape(b, n, H, E, 2)
        q = jnp.transpose(qk[..., 0], (0, 2, 1, 3))
        k = jnp.transpose(qk[..., 1], (0, 2, 1, 3))
        v = (x @ Wv_w.T + Wv_b).reshape(b, n, H, E)
        v = jnp.transpose(v, (0, 2, 1, 3))
        scores = jnp.einsum('bhqd,bhkd->bhqk', q, k)
        attn = jax.nn.softmax(scores, axis=-1) / jnp.asarray(HEAD_DIM ** 0.5, x.dtype)
        out = jnp.einsum('bhsl,bhlv->bhsv', attn, v)
        out = jnp.transpose(out, (0, 2, 1, 3)).reshape(b, n, H * E)
        return out @ Wo_w.T + Wo_b

    def _L0_cond2_ref(x, c, weight, c_weight, bias):
        import jax, jax.numpy as jnp
        import numpy as np
        from jax import lax
        N, C_IN, L = (32, 32, 512)
        C_OUT, K, GROUPS = (32, 9, 4)
        C_DIM, PAD, STRIDE = (128, 4, 1)
        out = lax.conv_general_dilated(x, weight, window_strides=(STRIDE,), padding=[(PAD, PAD)], dimension_numbers=('NCH', 'OIH', 'NCH'), feature_group_count=GROUPS)
        ctx = jnp.einsum('nd,od->no', c, c_weight)
        out = out + ctx[:, :, None] + bias[None, :, None]
        return out

    def _L0_ffn_ref(hidden_states, gate_w, up_w, down_w, fc1_w, fc2_w, expert_w, ln_gamma, ln_beta):
        import jax, jax.numpy as jnp
        import numpy as np
        HID, INT, LAT, NE, K = (512, 1024, 256, 8, 2)
        LN_EPS = 1e-05

        def _layernorm(x, gamma, beta):
            mu = jnp.mean(x, axis=-1, keepdims=True)
            var = jnp.var(x, axis=-1, keepdims=True)
            return (x - mu) * jax.lax.rsqrt(var + LN_EPS) * gamma + beta
        logits = jnp.einsum('bsh,he->bse', hidden_states, gate_w)
        routing_weights, selected_experts = jax.lax.top_k(logits, K)
        h = jax.nn.relu(jnp.einsum('bsh,hi->bsi', hidden_states, up_w)) ** 2
        shared_out = jnp.einsum('bsi,ih->bsh', h, down_w)
        x_latent = jnp.einsum('bsh,hl->bsl', hidden_states, fc1_w)
        expert_out = jnp.einsum('bsl,lm->bsm', x_latent, expert_w)
        moe_out = expert_out * jnp.sum(routing_weights, axis=-1, keepdims=True)
        routed_out = jnp.einsum('bsl,lh->bsh', moe_out, fc2_w)
        return _layernorm(shared_out + routed_out, ln_gamma, ln_beta)

    def _L1_cond_ref(x, embedding, W0, b0, W1, b1, W2, b2, weight, bias_k):
        import jax, jax.numpy as jnp
        import numpy as np
        K = 8
        T = 1.0
        D_EMBD = 128
        IN_C = 32
        OUT_C = 32
        BS = 32
        H = 512
        HID = 128
        h = jax.nn.gelu(embedding @ W0 + b0, approximate=False)
        h = jax.nn.gelu(h @ W1 + b1, approximate=False)
        att = jax.nn.softmax((h @ W2 + b2) / T, axis=-1)
        agg_w = jnp.einsum('bk,koi->boi', att, weight[..., 0])
        agg_b = att @ bias_k
        out = jnp.einsum('boi,bih->boh', agg_w, x) + agg_b[:, :, None]
        return out

    def _L1_attn_ref(hidden_states, ln_w, ln_b, Wq, Wk, Wv, Wo):
        import jax, jax.numpy as jnp
        import numpy as np
        HIDDEN = 512
        NUM_HEADS = 32
        NUM_KV_HEADS = 8
        HEAD_DIM = HIDDEN // NUM_HEADS
        N_REP = NUM_HEADS // NUM_KV_HEADS
        B, S = (1, 256)
        ACT_BITS = 8
        QB = 2 ** (ACT_BITS - 1) - 1
        ROPE_BASE = 10000.0
        LN_EPS = 1e-05

        def _act_quant(x):
            scale = QB / jnp.clip(jnp.max(jnp.abs(x), axis=-1, keepdims=True), 1e-05, None)
            q = jnp.clip(jnp.round(x * scale), -QB - 1, QB) / scale
            return x + jax.lax.stop_gradient(q - x)

        def _weight_quant(w):
            scale = 1.0 / jnp.clip(jnp.mean(jnp.abs(w)), 1e-05, None)
            q = jnp.clip(jnp.round(w * scale), -1.0, 1.0) / scale
            return w + jax.lax.stop_gradient(q - w)

        def _bitlinear(x, w):
            return jnp.einsum('...i,oi->...o', _act_quant(x), _weight_quant(w))

        def _layernorm(x, g, b):
            mu = jnp.mean(x, axis=-1, keepdims=True)
            var = jnp.mean(jnp.square(x - mu), axis=-1, keepdims=True)
            return (x - mu) * jax.lax.rsqrt(var + LN_EPS) * g + b

        def _rope(x):
            s, d = (x.shape[2], x.shape[3])
            inv_freq = 1.0 / ROPE_BASE ** (jnp.arange(0, d, 2, dtype=jnp.float32) / d)
            freqs = jnp.arange(s, dtype=jnp.float32)[:, None] * inv_freq[None, :]
            emb = jnp.concatenate([freqs, freqs], axis=-1)
            cos, sin = (jnp.cos(emb), jnp.sin(emb))
            x1, x2 = jnp.split(x, 2, axis=-1)
            rot = jnp.concatenate([-x2, x1], axis=-1)
            return x * cos + rot * sin
        b, s, _ = hidden_states.shape
        normed = _layernorm(hidden_states, ln_w, ln_b)
        q = _bitlinear(normed, Wq).reshape(b, s, NUM_HEADS, HEAD_DIM).transpose(0, 2, 1, 3)
        k = _bitlinear(normed, Wk).reshape(b, s, NUM_KV_HEADS, HEAD_DIM).transpose(0, 2, 1, 3)
        v = _bitlinear(normed, Wv).reshape(b, s, NUM_KV_HEADS, HEAD_DIM).transpose(0, 2, 1, 3)
        q = _rope(q)
        k = _rope(k)
        scale = 1.0 / np.sqrt(HEAD_DIM)
        qg = q.reshape(b, NUM_KV_HEADS, N_REP, s, HEAD_DIM)
        scores = jnp.einsum('bgrqd,bgkd->bgrqk', qg, k) * scale
        attn = jax.nn.softmax(scores, axis=-1)
        out = jnp.einsum('bgrqk,bgkd->bgrqd', attn, v)
        out = out.reshape(b, NUM_HEADS, s, HEAD_DIM).transpose(0, 2, 1, 3).reshape(b, s, HIDDEN)
        return _bitlinear(out, Wo)

    def _L1_cond2_ref(x, embedding, W0, b0, W1, b1, W2, b2, weight, bias_k):
        import jax, jax.numpy as jnp
        import numpy as np
        K = 8
        T = 1.0
        D_EMBD = 128
        IN_C = 32
        OUT_C = 32
        BS = 32
        H = 512
        HID = 128
        h = jax.nn.gelu(embedding @ W0 + b0, approximate=False)
        h = jax.nn.gelu(h @ W1 + b1, approximate=False)
        att = jax.nn.softmax((h @ W2 + b2) / T, axis=-1)
        agg_w = jnp.einsum('bk,koi->boi', att, weight[..., 0])
        agg_b = att @ bias_k
        out = jnp.einsum('boi,bih->boh', agg_w, x) + agg_b[:, :, None]
        return out

    def _L1_ffn_ref(hid, gate_w, u, g, d):
        import jax, jax.numpy as jnp
        import numpy as np
        NUM_EXPERTS = 16
        TOP_K = 2
        INTER = 56
        B, S, H = hid.shape
        x = hid.reshape(-1, H)
        bs = x.shape[0]
        logits = x @ gate_w.T
        probs = jax.nn.softmax(logits.astype(jnp.float32), axis=-1)
        vals, idx = jax.lax.top_k(probs, TOP_K)
        vals = vals / jnp.sum(vals, axis=-1, keepdims=True)
        rows = jnp.arange(bs)[:, None]
        w = jnp.zeros((bs, NUM_EXPERTS), dtype=jnp.float32).at[rows, idx].set(vals)
        w = w.astype(x.dtype)
        gate_out = (x @ g.T).reshape(bs, NUM_EXPERTS, INTER)
        up_out = (x @ u.T).reshape(bs, NUM_EXPERTS, INTER)
        h = jax.nn.silu(gate_out) * up_out
        d_r = d.reshape(H, NUM_EXPERTS, INTER)
        out = jnp.einsum('bei,hei,be->bh', h, d_r, w)
        return out.reshape(B, S, H)
    x = x + _L0_attn_ref(_L0_cond_ref(x, cond_128, L0_cond_W0, L0_cond_b0, L0_cond_W1, L0_cond_b1, L0_cond_W2, L0_cond_b2, L0_cond_weight, L0_cond_bias_k), L0_attn_Wqk_w, L0_attn_Wqk_b, L0_attn_Wv_w, L0_attn_Wv_b, L0_attn_Wo_w, L0_attn_Wo_b)
    x = x + _L0_ffn_ref(_L0_cond2_ref(x, cond_128, L0_cond2_weight, L0_cond2_c_weight, fside_S_0), L0_ffn_gate_w, L0_ffn_up_w, L0_ffn_down_w, L0_ffn_fc1_w, L0_ffn_fc2_w, L0_ffn_expert_w, L0_ffn_ln_gamma, L0_ffn_ln_beta)
    x = x + _L1_attn_ref(_L1_cond_ref(x, cond_128, L1_cond_W0, L1_cond_b0, L1_cond_W1, L1_cond_b1, L1_cond_W2, L1_cond_b2, L1_cond_weight, L1_cond_bias_k), L1_attn_ln_w, L1_attn_ln_b, L1_attn_Wq, L1_attn_Wk, L1_attn_Wv, L1_attn_Wo)
    x = x + _L1_ffn_ref(_L1_cond2_ref(x, cond_128, L1_cond2_W0, L1_cond2_b0, L1_cond2_W1, L1_cond2_b1, L1_cond2_W2, L1_cond2_b2, L1_cond2_weight, L1_cond2_bias_k), L1_ffn_gate_w, L1_ffn_u, L1_ffn_g, L1_ffn_d)
    return x

_drawn_inputs = setup_inputs


def setup_inputs(seed=0):
    import zlib

    import numpy as np

    out = dict(_drawn_inputs(seed))
    spreads = {'L0_cond_b0': (0.0, 0.1),
     'L0_cond_b1': (0.0, 0.1),
     'L0_cond_b2': (0.0, 0.1),
     'L0_attn_Wqk_b': (0.0, 0.1),
     'L0_attn_Wv_b': (0.0, 0.1),
     'L0_attn_Wo_b': (0.0, 0.1),
     'L0_ffn_ln_gamma': (1.0, 0.2),
     'L0_ffn_ln_beta': (0.0, 0.1),
     'L1_cond_b0': (0.0, 0.1),
     'L1_cond_b1': (0.0, 0.1),
     'L1_cond_b2': (0.0, 0.1),
     'L1_attn_ln_w': (1.0, 0.2),
     'L1_attn_ln_b': (0.0, 0.1),
     'L1_cond2_b0': (0.0, 0.1),
     'L1_cond2_b1': (0.0, 0.1),
     'L1_cond2_b2': (0.0, 0.1)}
    factors = {}
    for name, (base, spread) in spreads.items():
        noise = np.random.default_rng([zlib.crc32(name.encode()), seed]).standard_normal(out[name].shape)
        drawn = base * np.exp(spread * noise) if base else spread * noise
        out[name] = jnp.asarray(drawn.astype(out[name].dtype))
    for name, factor in factors.items():
        out[name] = (out[name] * factor).astype(out[name].dtype)
    return out
```

```python
from contextlib import ExitStack

import numpy as np

import concourse.bass as bass
from concourse import mybir

ALU = mybir.AluOpType
ACT = mybir.ActivationFunctionType
AX_X = mybir.AxisListType.X
F32 = mybir.dt.float32
F32R = mybir.dt.float32r
BF16 = mybir.dt.bfloat16

P = 128
B, C, D = 64, 32, 512
TOKENS = B * C
NT = 2
ROUND = NT * P
ROUNDS = TOKENS // ROUND
TILES = TOKENS // P
BT = P // C
Q = D // P
EMB = 128
KE = 8
CONDS = 3
H0, E0 = 8, 8
TAPS, GROUPS = 9, 4
INT, LAT, NE0 = 1024, 256, 8
KV, REP, HD = 8, 4, 16
NE1, INTER = 16, 56
EI = NE1 * INTER
M1 = EI // P
EPS = 1e-5
QB = 127.0
ROUND_MAGIC = 1.5 * 2.0**23
FAR = 3.0e38

UP, DOWN, LATENT, FC2 = 0, Q * INT, Q * INT + 8 * D, Q * INT + 8 * D + Q * LAT
CONV = FC2 + 2 * D
GATE0 = CONV + 3 * P
GW, UW, DW = 0, Q * EI, 2 * Q * EI
WCOLS = max(GATE0 + Q * NE0, DW + M1 * D)
STAGE = 1024


class Signal:

    def __init__(self, sem, per_round, unit=1):
        self.sem, self.per_round, self.unit = sem, per_round, unit

    def nth(self, s, n):
        return (s * self.per_round + n) * self.unit


def after(engine, signal, s, n):
    value = signal.nth(s, n)
    if isinstance(value, int) and value <= 0:
        return
    engine.wait_ge(signal.sem, value)


class Banks:

    def __init__(self, psum, first, count, uses, ready, free):
        self.psum, self.ready_sem, self.free_sem = psum, ready, free
        self.bank, self.turn, self.turns = {}, {}, [0] * count
        for k, use in enumerate(uses):
            self.turns[k % count] += 1
            self.bank[use], self.turn[use] = k % count, self.turns[k % count]
        self.first = first

    def __getitem__(self, use):
        return self.psum[:, self.first + self.bank[use], :]

    def claim(self, pe, s, use):
        b = self.bank[use]
        value = s * self.turns[b] + self.turn[use] - 1
        if not (isinstance(value, int) and value <= 0):
            pe.wait_ge(self.free_sem[b], value)

    def ready(self, use):
        return self.ready_sem[self.bank[use]]

    def filled(self, engine, s, use):
        b = self.bank[use]
        engine.wait_ge(self.ready_sem[b], s * self.turns[b] + self.turn[use])

    def read(self, engine, s, use):
        b = self.bank[use]
        value = s * self.turns[b] + self.turn[use]
        if not (isinstance(value, int) and value <= 0):
            engine.wait_ge(self.free_sem[b], value)

    def free(self, use):
        return self.free_sem[self.bank[use]]


def f32(ap):
    return ap.bitcast(F32)


def matmul_split(pe, out, lhs, rhs, start, stop):
    pe.matmul(out, lhs[0], rhs[0], start=start, stop=False)
    pe.matmul(out, lhs[0], rhs[1], start=False, stop=False)
    return pe.matmul(out, lhs[1], rhs[0], start=False, stop=stop)


def prepare(nc, ctx, t, sb, sem, scratch, psum, consts, weights):
    wh, wl, stage = weights
    ident, ones = consts["ident"], consts["ones"]
    embT = sb("embT", [P, B], F32)
    w0 = sb("cond_w0", [P, CONDS, P], F32)
    w1 = sb("cond_w1", [P, CONDS, P], F32)
    w2 = sb("cond_w2", [P, CONDS, KE], F32)
    b01 = sb("cond_b01", [P, CONDS, 2], F32)
    b2 = sb("cond_b2", [B, CONDS, KE], F32)
    wk = sb("cond_wk", [KE, C, BT, C], F32)
    bk = sb("cond_bk", [KE, CONDS, C], F32)
    g1 = sb("cond_g1", [P, CONDS, B], F32)
    g2 = sb("cond_g2", [P, CONDS, B], F32)
    att = sb("att", [B, CONDS, KE], F32)
    att_max = sb("att_max", [B, CONDS], F32)
    att_sum = sb("att_sum", [B, CONDS], F32)
    attT = sb("attT", [KE, CONDS, B], F32)
    mix = sb("mix", [P, TILES, 2, P], F32R)
    rows = [sb(f"rows{i}", [2 * C, TOKENS], F32R) for i in range(2)]
    row32 = sb("row32", [P, TOKENS], F32)
    cwT = sb("cwT", [P, C], F32)
    side = sb("side", [1, C], F32)
    small = sb("small_stage", [P, D], F32)
    bqk_stage = sb("bqk_stage", [2 * C, 192], F32)
    fc1T = sb("fc1T", [P, 2, D], F32)
    ew = sb("ew", [P, 2, LAT], F32)
    ones32 = sb("ones32", [P, P], F32)
    wbit = sb("bit_stage", [P, Q, 3 * P + 2 * D - P], F32)
    tern = sb("ternary_out", [P, Q, 3 * P + 2 * D - P], BF16)
    wsum, wscale = sb("weight_sum", [P, 4], F32), sb("weight_scale", [P, 4], F32)
    MATRICES = ((0, D), (D, P), (D + P, P), (D + 2 * P, D))
    kernels_in = sem("prep_kernels_in")
    bits_in = sem("prep_bits_in")
    bits_out = sem("prep_bits_out")
    bits_stored = sem("prep_bits_stored")

    loaded = sem("prep_loaded")
    loaded_small = sem("prep_small")
    staged = [sem(f"prep_staged{i}") for i in range(2)]
    high = sem("prep_high")
    low = sem("prep_low")
    zeroed = sem("prep_zeroed")
    consts_made = sem("prep_consts")
    pe_done = sem("prep_pe")
    act_done = sem("prep_act")
    dve_done = sem("prep_dve")
    mix_stored = sem("prep_mix_stored")
    rows_stored = [sem(f"prep_rows_stored{i}") for i in range(2)]

    pieces = []

    def pieces_of(first, src, chunks, width):
        per = max(1, STAGE // width)
        for c0 in range(0, chunks, per):
            n = min(per, chunks - c0)
            pieces.append((first + c0 * width, src, c0, n, width))

    qkv_h, qkv_l = consts["qkv_h"], consts["qkv_l"]
    pieces.append((None, t["qkv0"], 0, Q, 192))
    pieces_of(CONV, t["conv"], 3, P)
    pieces_of(GATE0, t["gate0"], Q, NE0)
    pieces.append(("gate1", t["gate1"], 0, Q, NE1))
    pieces_of(UP, t["up"], Q, INT)
    pieces_of(DOWN, t["down"], 8, D)
    pieces_of(FC2, t["fc2"], 2, D)

    def parts(piece):
        first, _, _, n, width = piece
        if first is None:
            return qkv_h[:, :], qkv_l[:, :]
        if first == "gate1":
            return [x[:, :] for x in consts["gate1"]]
        return wh[:, first:first + n * width], wl[:, first:first + n * width]

    ACT_GELU1, ACT_GELU2, ACT_EXP, ACT_ATT = 3, 6, 7, 8
    n_cond_loads = 11

    block = ctx.enter_context(nc.Block())

    @block.sync
    def _(sp):
        def load(dst, src):
            sp.dma_start(dst, src).then_inc(loaded, 16)

        load(embT[:, :], t["embT"])
        load(w0[:, :, :], t["cond_w0"].rearrange("(c p) n -> p c n", p=P))
        load(w1[:, :, :], t["cond_w1"].rearrange("(c p) n -> p c n", p=P))
        load(w2[:, :, :], t["cond_w2"].rearrange("(c p) n -> p c n", p=P))
        load(b01[:, :, :], t["cond_b01"].rearrange("(c p) n -> p c n", p=P))
        load(b2[:, :, :], t["cond_b2"].rearrange("(a c) n -> a c n", a=1).broadcast_to([B, CONDS, KE]))
        load(wk[:, :, :, :], t["cond_wk"][0:KE])
        load(bk[:, :, :], t["cond_bk"].rearrange("(c k) o -> k c o", k=KE))
        load(cwT[:, :], t["cwT"])
        load(side[:, :], t["side"])
        load(ew[:, :, :], t["expert"].rearrange("(c p) n -> p c n", p=P))
        sp.dma_start(wbit[:, :, :], t["bits"].rearrange("(c p) n -> p c n", p=P)).then_inc(bits_in, 16)
        sp.wait_ge(zeroed, 2)
        for r in (0, 32):
            sp.dma_start(bqk_stage[r:r + 1, :], t["bqkv0"]).then_inc(loaded_small, 16)
        sp.dma_start(small[0:64, :], t["wo0"]).then_inc(loaded_small, 16)
        for r in (64, 96):
            sp.dma_start(small[r:r + 1, :], t["bo0"]).then_inc(loaded_small, 16)
        sp.dma_start(fc1T[:, :, :], t["fc1T"].rearrange("(c p) n -> p c n", p=P)).then_inc(loaded_small, 16)
        sp.dma_start(consts["gamma"][:, :], t["gamma"].broadcast_to([P, D])).then_inc(loaded_small, 16)
        sp.dma_start(consts["beta"][:, :], t["beta"].broadcast_to([P, D])).then_inc(loaded_small, 16)
        sp.dma_start(consts["mask0"][:, :], t["mask0"]).then_inc(loaded_small, 16)
        sp.dma_start(consts["vmask0"][:, :], t["vmask0"]).then_inc(loaded_small, 16)
        sp.dma_start(consts["vsel"][:, :, :], t["vsel"]).then_inc(loaded_small, 16)
        for k, (first, src, c0, n, width) in enumerate(pieces):
            if k >= 2:
                sp.wait_ge(low, k - 1)
            sp.dma_start(stage[:, k % 2, 0:n * width].rearrange("p (c n) -> p c n", c=n),
                         src[c0 * P:(c0 + n) * P, :].rearrange("(c p) n -> p c n", p=P)).then_inc(staged[k % 2], 16)
        sp.wait_ge(mix_stored, 16 * CONDS)
        for i in range(2):
            sp.wait_ge(rows_stored[i], 16 * (CONDS + 1) // 2)
        sp.wait_ge(loaded_small, 16 * 11)
        sp.wait_ge(bits_out, len(MATRICES))
        sp.dma_start(scratch["ternary"], tern[:, :, :]).then_inc(bits_stored, 16)
        sp.wait_ge(bits_stored, 16)

    @block.gpsimd
    def _(pool):
        nc.gpsimd.memset(small[:, :], 0.0).then_inc(zeroed, 1)
        nc.gpsimd.memset(bqk_stage[:, :], 0.0).then_inc(zeroed, 1)
        nc.gpsimd.memset(ident[:, :], 0.0).then_inc(zeroed, 1)
        nc.gpsimd.memset(f32(mix[:, :, :, :]), 0.0).then_inc(zeroed, 1)
        for r in rows:
            nc.gpsimd.memset(f32(r[:, :]), 0.0).then_inc(zeroed, 1)
        for x in consts["halo"]:
            nc.gpsimd.memset(x[:, :, :], 0.0)
        nc.gpsimd.memset(f32(consts["out_b"][:, :, :]), 1.0)
        nc.gpsimd.memset(consts["minus_half"][:, :], -0.5)
        nc.gpsimd.memset(ones32[:, :], 1.0).then_inc(consts_made, 1)
        pool.wait_ge(zeroed, 6)
        nc.gpsimd.affine_select(out=ident[:, :], in_=ident[:, :], compare_op=ALU.not_equal, fill=1.0, base=0,
                                pattern=[[-1, P]], channel_multiplier=1).then_inc(consts_made, 1)
        for k, piece in enumerate(pieces):
            n = piece[3] * piece[4]
            pool.wait_ge(high, k + 1)
            hi, lo = parts(piece)
            nc.gpsimd.tensor_tensor(lo, stage[:, k % 2, 0:n], f32(hi), ALU.subtract).then_inc(low, 1)

    @block.scalar
    def _(act):
        act.wait_ge(loaded, 16 * n_cond_loads)
        for layer, g in ((0, g1), (1, g2)):
            act.wait_ge(pe_done, CONDS * (layer + 1))
            for c in range(CONDS):
                nc.scalar.activation(g[:, c, :], psum[:, layer, c * B:(c + 1) * B], ACT.Gelu,
                                     bias=b01[:, c, layer:layer + 1]).then_inc(act_done, 1)
        act.wait_ge(dve_done, 3)
        nc.scalar.activation(att[:, :, :], att[:, :, :], ACT.Exp).then_inc(act_done, 1)
        act.wait_ge(pe_done, 3 * CONDS + 1)
        nc.scalar.activation(attT[:, :, :], psum[0:KE, 3, 0:CONDS * B].rearrange("k (c b) -> k c b", c=CONDS),
                             ACT.Copy).then_inc(act_done, 1)
        assert ACT_ATT == 8
        act.wait_ge(zeroed, 6)
        for c in range(CONDS):
            act.wait_ge(pe_done, 3 * CONDS + 2 + c)
            if c + 1 < CONDS:
                act.dma_start(wk[:, :, :, :], t["cond_wk"][(c + 1) * KE:(c + 2) * KE]).then_inc(kernels_in, 16)
            if c:
                act.wait_ge(mix_stored, 16 * c)
            for r in range(BT):
                last = nc.scalar.activation(
                    mix[C * r:C * r + C, :, 0, C * r:C * r + C].rearrange("p t o -> p o t"),
                    psum[C * r:C * r + C, 4:8, :].rearrange("p k (o t r) -> p (k o) t r", r=BT, t=TILES)[:, :, :, r],
                    ACT.Copy)
            last.then_inc(consts["mix_high"], 1)
            act.wait_ge(consts["mix_high"], c + 1)
            act.wait_ge(consts["mix_low"], c + 1)
            act.dma_start(scratch["mix"][c].rearrange("t p h n -> p t h n"), f32(mix[:, :, :, :])).then_inc(mix_stored, 16)
        for k, piece in enumerate(pieces):
            act.wait_ge(staged[k % 2], 16 * (k // 2 + 1))
            n = piece[3] * piece[4]
            nc.scalar.activation(parts(piece)[0], stage[:, k % 2, 0:n], ACT.Copy).then_inc(high, 1)
            if k % 3 == 2 and k // 3 <= CONDS:
                c = k // 3
                act.wait_ge(consts["rows_low"], c + 1)
                act.dma_start(scratch["rows"][c], f32(rows[c % 2][:, :])).then_inc(rows_stored[c % 2], 16)
        assert len(pieces) >= 3 * (CONDS + 1)

    @block.vector
    def _(dve):
        count = [0]

        def done(instruction):
            count[0] += 1
            instruction.then_inc(dve_done, 1)
            dve.wait_ge(dve_done, count[0])

        dve.wait_ge(pe_done, 3 * CONDS)
        logits = psum[0:B, 2, 0:CONDS * KE].rearrange("b (c k) -> b c k", c=CONDS)
        done(nc.vector.tensor_tensor(att[:, :, :], logits, b2[:, :, :], ALU.add))
        done(nc.vector.tensor_reduce(att_max[:, :], att[:, :, :], AX_X, ALU.max))
        done(nc.vector.tensor_tensor(att[:, :, :], att[:, :, :],
                                     att_max[:, :].unsqueeze(2).broadcast_to([B, CONDS, KE]), ALU.subtract))
        dve.wait_ge(act_done, ACT_EXP)
        done(nc.vector.tensor_reduce(att_sum[:, :], att[:, :, :], AX_X, ALU.add))
        done(nc.vector.reciprocal(att_sum[:, :], att_sum[:, :]))
        done(nc.vector.tensor_tensor(att[:, :, :], att[:, :, :],
                                     att_sum[:, :].unsqueeze(2).broadcast_to([B, CONDS, KE]), ALU.mult))
        assert count[0] == 6
        for c in range(CONDS):
            dve.wait_ge(consts["mix_high"], c + 1)
            for r in range(BT):
                hi = f32(mix[C * r:C * r + C, :, 0, C * r:C * r + C]).rearrange("p t o -> p o t")
                lo = mix[C * r:C * r + C, :, 1, C * r:C * r + C].rearrange("p t o -> p o t")
                src = psum[C * r:C * r + C, 4:8, :].rearrange("p k (o t r) -> p (k o) t r", r=BT, t=TILES)[:, :, :, r]
                last = nc.vector.tensor_tensor(lo, src, hi, ALU.subtract)
            last.then_inc(consts["mix_low"], 1)
        dve.wait_ge(act_done, ACT_ATT)
        dve.wait_ge(zeroed, 6)
        for c in range(CONDS + 1):
            dst = rows[c % 2]
            if c >= 2:
                dve.wait_ge(rows_stored[c % 2], 16 * (c // 2))
            if c < CONDS:
                n = KE
                whole = row32[0:KE, :]
                done(nc.vector.tensor_tensor(whole.rearrange("k (b o) -> k b o", b=B),
                                             attT[:, c, :].unsqueeze(2).broadcast_to([KE, B, C]),
                                             bk[:, c, :].unsqueeze(1).broadcast_to([KE, B, C]), ALU.mult))
            else:
                n = 1
                done(nc.vector.tensor_tensor(row32[:, :].rearrange("k (b o) -> k b o", b=B),
                                             embT[:, :].unsqueeze(2).broadcast_to([P, B, C]),
                                             cwT[:, :].unsqueeze(1).broadcast_to([P, B, C]), ALU.mult))
                dve.wait_ge(pe_done, 4 * CONDS + 2)
                whole = row32[0:1, :]
                done(nc.vector.tensor_tensor(
                    whole.rearrange("a (k b o) -> a k b o", k=4, o=C),
                    psum[0:1, 0:4, :].rearrange("a k (b o) -> a k b o", o=C),
                    side[:, :].unsqueeze(1).unsqueeze(1).broadcast_to([1, 4, B // 4, C]), ALU.add))
            if n == 1:
                nc.vector.memset(f32(dst[0:KE, :]), 0.0)
                done(nc.vector.memset(f32(dst[32:32 + KE, :]), 0.0))
            done(nc.vector.tensor_copy(dst[0:n, :], whole))
            nc.vector.tensor_tensor(dst[32:32 + n, :], whole, f32(dst[0:n, :]), ALU.subtract)\
                .then_inc(consts["rows_low"], 1)
            dve.wait_ge(consts["rows_low"], c + 1)
        dve.wait_ge(loaded_small, 16 * 11)
        out_w = consts["out_w"]
        done(nc.vector.tensor_copy(out_w[0:64, 0, :], small[0:64, :]))
        done(nc.vector.tensor_copy(out_w[64:128, 0, :], small[0:64, :]))
        done(nc.vector.tensor_tensor(out_w[0:64, 1, :], small[0:64, :], f32(out_w[0:64, 0, :]), ALU.subtract))
        done(nc.vector.tensor_copy(out_w[64:128, 1, :], small[64:128, :]))
        done(nc.vector.tensor_tensor(out_w[96:128, 1, :], small[96:128, :], f32(out_w[96:128, 1, :]), ALU.subtract))
        bqkv = consts["bqkv"]
        done(nc.vector.tensor_copy(bqkv[:, :], bqk_stage[:, :]))
        done(nc.vector.tensor_tensor(bqkv[32:64, :], bqk_stage[32:64, :], f32(bqkv[32:64, :]), ALU.subtract))
        dve.wait_ge(consts_made, 1)
        for col in range(0, D, P):
            done(nc.vector.tensor_copy(ones[:, col:col + P], ones32[:, :]))
        dve.wait_ge(bits_in, 16)
        for k, (first, n) in enumerate(MATRICES):
            done(nc.vector.tensor_reduce(wsum[:, k:k + 1], wbit[:, :, first:first + n], mybir.AxisListType.XY, ALU.add,
                                         apply_absolute_value=True))
        dve.wait_ge(pe_done, 4 * CONDS + 3)
        dequant = consts["dequant"]
        for k, (first, n) in enumerate(MATRICES):
            done(nc.vector.tensor_scalar(dequant[:, k:k + 1], psum[:, 2, k:k + 1], 1.0 / (D * n), 1e-5,
                                         ALU.mult, ALU.max))
        done(nc.vector.reciprocal(wscale[:, :], dequant[:, :]))
        done(nc.vector.tensor_scalar(dequant[:, :], dequant[:, :], 1.0 / QB, None, ALU.mult))
        for k, (first, n) in enumerate(MATRICES):
            w = wbit[:, :, first:first + n]
            done(nc.vector.tensor_scalar(w, w, wscale[:, k:k + 1], ROUND_MAGIC, ALU.mult, ALU.add))
            done(nc.vector.tensor_scalar(w, w, -ROUND_MAGIC, 1.0, ALU.add, ALU.min))
            nc.vector.tensor_scalar(tern[:, :, first:first + n], w, -1.0, None, ALU.max).then_inc(bits_out, 1)
        dve.wait_ge(pe_done, 4 * CONDS + 4)
        for c in range(2):
            src = psum[:, 4 + c, :]
            hi = wh[:, LATENT + c * D:LATENT + c * D + D]
            lo = wl[:, LATENT + c * D:LATENT + c * D + D]
            done(nc.vector.tensor_copy(hi, src))
            done(nc.vector.tensor_tensor(lo, src, f32(hi), ALU.subtract))

    @block.tensor
    def _(pe):
        pe.wait_ge(loaded, 16 * n_cond_loads)
        for c in range(CONDS):
            nc.tensor.matmul(psum[:, 0, c * B:(c + 1) * B], w0[:, c, :], embT[:, :], start=True, stop=True)\
                .then_inc(pe_done, 1)
        for c in range(CONDS):
            pe.wait_ge(act_done, c + 1)
            nc.tensor.matmul(psum[:, 1, c * B:(c + 1) * B], w1[:, c, :], g1[:, c, :], start=True, stop=True)\
                .then_inc(pe_done, 1)
        for c in range(CONDS):
            pe.wait_ge(act_done, CONDS + c + 1)
            nc.tensor.matmul(psum[0:B, 2, c * KE:(c + 1) * KE], g2[:, c, :], w2[:, c, :], start=True, stop=True)\
                .then_inc(pe_done, 1)
        pe.wait_ge(dve_done, 6)
        pe.wait_ge(consts_made, 2)
        for c in range(CONDS):
            last = nc.tensor.transpose(psum[0:KE, 3, c * B:(c + 1) * B], att[:, c, :], ident[0:B, 0:B])
        last.then_inc(pe_done, 1)
        pe.wait_ge(act_done, ACT_ATT)
        for c in range(CONDS):
            if c:
                pe.wait_ge(consts["mix_low"], c)
                pe.wait_ge(kernels_in, 16 * c)
            for o in range(C):
                last = nc.tensor.matmul(psum[:, 4 + o // 8, (o % 8) * B:(o % 8 + 1) * B],
                                        wk[:, o, :, :].rearrange("k r i -> k (r i)"), attT[:, c, :],
                                        start=True, stop=True)
            last.then_inc(pe_done, 1)
        pe.wait_ge(consts_made, 1)
        pe.wait_ge(dve_done, 6 + 2 * CONDS + 1)
        for k in range(4):
            last = nc.tensor.matmul(psum[:, k, :], ones32[:, :], row32[:, k * D:(k + 1) * D], start=True, stop=True)
        last.then_inc(pe_done, 1)
        pe.wait_ge(dve_done, 6 + 2 * CONDS + 2 + 2 + 7 + D // P + 4)
        nc.tensor.matmul(psum[:, 2, 0:4], ones32[:, :], wsum[:, :], start=True, stop=True).then_inc(pe_done, 1)
        pe.wait_ge(loaded_small, 16 * 11)
        pe.wait_ge(consts["mix_low"], CONDS)
        for c in range(Q):
            for k in range(2):
                last = nc.tensor.matmul(psum[:, 4 + c // 2, (c % 2) * LAT:(c % 2 + 1) * LAT],
                                        fc1T[:, k, c * P:(c + 1) * P], ew[:, k, :], start=(k == 0), stop=(k == 1))
        last.then_inc(pe_done, 1)


ATTEND0 = [("split", 0), ("split", 1), ("mix", 0), ("mix", 1), ("qkv", 0), ("qkv", 1), ("scores", 0), ("scores", 1),
           ("turn", 0), ("turn", 1), ("values", 0), ("values", 1), ("out", 0), ("out", 1), ("phase", 0), ("phase", 1)]
FORWARD0 = [("carry", 0), ("conv", 0), ("conv", 1), ("gate", 0), ("up", 0), ("up", 1), ("up", 2), ("up", 3),
            ("latent", 0), ("down", 0), ("down", 1)]
BODY0 = [("F", "carry", 0), ("A", "split", 0), ("F", "conv", 0), ("F", "conv", 1), ("A", "split", 1),
         ("A", "mix", 0), ("F", "gate", 0), ("A", "mix", 1), ("F", "up", 0), ("A", "qkv", 0), ("A", "qkv", 1),
         ("F", "up", 1), ("A", "scores", 0), ("A", "scores", 1), ("F", "up", 2), ("F", "up", 3),
         ("A", "turn", 0), ("A", "turn", 1), ("F", "latent", 0), ("A", "values", 0), ("A", "values", 1),
         ("F", "down", 0), ("A", "out", 0), ("A", "out", 1), ("F", "down", 1), ("A", "phase", 0), ("A", "phase", 1)]


def layer0(nc, ctx, t, sb, sem, scratch, psum, consts, weights):
    wh, wl, _ = weights
    ident, ones, mask0, vmask0, vsel = (consts[k] for k in ("ident", "ones", "mask0", "vmask0", "vsel"))
    out_w, qkv_h, qkv_l, bqkv = (consts[k] for k in ("out_w", "qkv_h", "qkv_l", "bqkv"))
    xp = consts["halo"]
    out_b = consts["out_b"]
    x = sb("x", [P, NT, D], F32)
    xs = sb("x_split", [P, NT, 2, D], F32R)
    mix = sb("mix0", [P, NT, 2, P], F32R)
    rows = sb("bias_rows0", [2 * C, NT, P], F32R)
    crow = sb("context_rows", [2 * C, NT, P], F32R)
    ys = sb("y_split", [P, NT, 2, Q, P], F32R)
    qT = sb("qT", [H0 * E0, NT, P], F32)
    kT = sb("kT", [H0 * E0, NT, P], F32)
    km = sb("k_masked", [H0 * E0, NT, BT, H0, C], F32)
    v = sb("v", [P, NT, H0 * E0], F32)
    vb = sb("v_blocks", [P, NT, BT, H0 * E0], F32)
    prob = sb("prob", [P, NT, H0, C], F32)
    pmax = sb("prob_max", [P, NT, H0], F32)
    psums = sb("prob_sum", [P, NT, H0], F32)
    pT = sb("probT", [P, NT, 2, P], F32)
    out_a = sb("out_a", [P, NT, P], F32R)
    x1 = sb("x1", [P, NT, D], F32)
    xps = sb("phase_split", [P, NT, 2, BT, P + 2], F32R)
    hs = sb("h_split", [P, 2, Q, ROUND], F32R)
    x1b = sb("x1_plus_beta", [P, NT, D], F32)
    logit8 = sb("gate_top", [P, NT, 8], F32)
    gsum = sb("gate_sum", [P, NT], F32)
    relu = sb("relu", [P, 2, 2 * ROUND], F32)
    sq = sb("squared", [P, 2, 2 * ROUND], F32)
    gs = sb("squared_split", [P, 2, INT // P, ROUND], F32R)
    fs = sb("latent_split", [P, 2, 2, ROUND], F32R)
    routed = sb("routed", [P, D], F32)
    z = sb("ffn_out", [P, D], F32)
    stats = sb("stats", [P, 6], F32)
    mv = sb("mean_var", [P, 2], F32)
    rstd = sb("rstd", [P, 1], F32)

    def signal(name, per_round, unit=1):
        return Signal(sem("l0_" + name), per_round, unit)

    x_in = [signal(f"x_in{i}", 3, 16) for i in range(NT)]
    context_in = [signal(f"context_in{i}", 1, 16) for i in range(NT)]
    x_high, x_low = signal("x_high", NT), signal("x_low", NT)
    y_high = signal("y_high", NT)
    qk_out, k_masked = signal("qk_out", NT), signal("k_masked", NT)
    smax, expd, ssum, srecip, normed = (signal(n, NT) for n in ("max", "exp", "sum", "recip", "normed"))
    o_high = signal("o_high", 2 * NT)
    xp_in = [signal(f"xp_in{i}", Q * BT, 16) for i in range(NT)]
    xp_high, xp_low = signal("xp_high", NT), signal("xp_low", NT)
    carried = signal("carried", 1)
    h_high, gsummed = signal("h_high", NT), signal("gsummed", 1)
    relu_out, sq_high, sq_low = (signal(n, 4) for n in ("relu", "sq_high", "sq_low"))
    f_high = signal("f_high", 1)
    stats_out, mv_out, var_out, rstd_out, scaled, x2_out = (signal(n, NT) for n in (
        "stats", "mv", "var", "rstd", "scaled", "x2"))
    held = signal("held", 1)
    x2_stored = signal("x2_stored", NT, 16)

    a_uses = [(k, i) for i_k in (("mix",), ("qkv",), ("vrep",), ("scores",), ("turn",), ("values",), ("out",))
              for i in range(NT) for k in i_k]
    A = Banks(psum, 0, 4, a_uses, [sem(f"l0_a_ready{i}") for i in range(4)], [sem(f"l0_a_free{i}") for i in range(4)])
    f_uses = [("conv", 0), ("conv", 1), ("gate", 0), ("up", 0), ("up", 1), ("up", 2), ("up", 3), ("latent", 0),
              ("routed", 0), ("down", 0), ("routed", 1), ("down", 1)]
    F = Banks(psum, 4, 4, f_uses, [sem(f"l0_f_ready{i}") for i in range(4)], [sem(f"l0_f_free{i}") for i in range(4)])

    def go(steps, engine):
        for name, i in ATTEND0:
            steps("A", name, i, 0)
        for kind, name, i in BODY0:
            steps(kind, name, i, 1 if kind == "A" else 0)
        with engine.Fori(2, ROUNDS) as r:
            for kind, name, i in BODY0:
                steps(kind, name, i, r if kind == "A" else r - 1)
        for name, i in FORWARD0:
            steps("F", name, i, ROUNDS - 1)

    block = ctx.enter_context(nc.Block())

    @block.sync
    def _(sp):
        def step(kind, name, i, s):
            if name == "split":
                A.read(sp, s - 1, ("out", i))
                sp.sem_inc(held.sem, 1)
                n = x_in[i].sem
                sp.dma_start(x[:, i, :], t["x"][bass.ds(s * ROUND + i * P, P), :]).then_inc(n, 16)
                sp.dma_start(f32(mix[:, i, :, :]), scratch["mix_t"][0][bass.ds(s * ROUND + i * P, P), :, :]).then_inc(n, 16)
                sp.dma_start(f32(rows[:, i, :]), scratch["rows"][0][:, bass.ds(s * ROUND + i * P, P)]).then_inc(n, 16)
            if name == "out":
                F.read(sp, s - 1, ("conv", i))
                sp.sem_inc(held.sem, 1)
                n = context_in[i].sem
                sp.dma_start(f32(crow[:, i, :]), scratch["rows"][CONDS][:, bass.ds(s * ROUND + i * P, P)]).then_inc(n, 16)
                A.read(sp, s, ("out", i))
                sp.sem_inc(held.sem, 1)
                after(sp, xp_low, s - 1, i + 1)
                sp.sem_inc(held.sem, 1)
                for b in range(BT):
                    for q in range(Q):
                        sp.dma_start(xp[i][C * q:C * q + C, b, 1:1 + P],
                                     x1[C * b:C * b + C, i, P * q:P * q + P]).then_inc(xp_in[i].sem, 16)
            if name == "down":
                after(sp, x2_out, s, i + 1)
                sp.sem_inc(held.sem, 1)
                sp.dma_start(scratch["x2"][bass.ds(s * ROUND + i * P, P), :], z[:, :]).then_inc(x2_stored.sem, 16)

        go(step, sp)
        after(sp, x2_stored, ROUNDS - 1, NT)

    @block.scalar
    def _(act):
        copy = lambda out, in_, **k: nc.scalar.activation(out, in_, ACT.Copy, **k)

        def step(kind, name, i, s):
            if name == "split":
                after(act, x_in[i], s, 3)
                copy(xs[:, i, 0, :], x[:, i, :]).then_inc(x_high.sem, 1)
            elif name == "mix":
                A.filled(act, s, ("mix", i))
                copy(ys[:, i, 0, :, :], A[("mix", i)].rearrange("p (q n) -> p q n", q=Q)).then_inc(y_high.sem, 1)
            elif name == "qkv":
                bank = A[("qkv", i)]
                A.filled(act, s, ("qkv", i))
                copy(qT[:, i, :], bank[0:64, 0:P])
                copy(kT[:, i, :], bank[64:128, 0:P]).then_inc(qk_out.sem, 1)
                copy(v[:, i, :], bank[:, P:P + 64]).then_inc(A.free(("qkv", i)), 1)
            elif name == "scores":
                A.read(act, s, ("scores", i))
                nc.scalar.activation(prob[:, i, :, :], prob[:, i, :, :], ACT.Exp).then_inc(expd.sem, 1)
            elif name == "turn":
                A.filled(act, s, ("turn", i))
                copy(pT[:, i, :, :], A[("turn", i)][:, 0:2 * P].rearrange("p (h n) -> p h n", h=2))\
                    .then_inc(A.free(("turn", i)), 1)
            elif name == "values":
                A.filled(act, s, ("values", i))
                bank = A[("values", i)]
                copy(out_a[0:64, i, :], bank[0:64, 0:P]).then_inc(o_high.sem, 1)
                copy(out_b[0:64, i, :], bank[0:64, 0:P]).then_inc(o_high.sem, 1)
            elif name == "phase":
                after(act, xp_in[i], s, Q * BT)
                F.read(act, s - 1, ("conv", i))
                copy(xps[:, i, 0, :, :], xp[i][:, :, :]).then_inc(xp_high.sem, 1)
            elif name == "conv":
                F.filled(act, s, ("conv", i))
                after(act, f_high, s - 1, 1)
                copy(hs[:, 0, :, i * P:(i + 1) * P].rearrange("p q (b o) -> p b q o", b=BT),
                     F[("conv", i)].rearrange("p (b q o) -> p b q o", b=BT, q=Q)).then_inc(h_high.sem, 1)
            elif name == "up":
                F.filled(act, s, ("up", i))
                F.read(act, s if i >= 2 else s - 1, ("up", (i + 2) % 4))
                nc.scalar.activation(relu[:, i % 2, :], F[("up", i)], ACT.Relu).then_inc(relu_out.sem, 1)
                F.read(act, s, ("up", i))
                if i == 0:
                    F.read(act, s - 1, ("down", NT - 1))
                copy(gs[:, 0, 2 * i:2 * i + 2, :], sq[:, i % 2, :].rearrange("p (m n) -> p m n", m=2))\
                    .then_inc(sq_high.sem, 1)
            elif name == "latent":
                F.filled(act, s, ("latent", 0))
                copy(fs[:, 0, :, :], F[("latent", 0)].rearrange("p (m n) -> p m n", m=2)).then_inc(f_high.sem, 1)
            elif name == "down":
                F.filled(act, s, ("routed", i))
                after(act, gsummed, s, 1)
                F.read(act, s if i else s - 1, ("down", (i - 1) % NT))
                copy(routed[:, :], F[("routed", i)], scale=gsum[:, i:i + 1]).then_inc(F.free(("routed", i)), 1)

        go(step, act)

    @block.gpsimd
    def _(pool):
        def step(kind, name, i, s):
            if name == "split":
                after(pool, x_high, s, i + 1)
                nc.gpsimd.tensor_tensor(xs[:, i, 1, :], x[:, i, :], f32(xs[:, i, 0, :]), ALU.subtract)\
                    .then_inc(x_low.sem, 1)
            elif name == "qkv":
                after(pool, qk_out, s, i + 1)
                nc.gpsimd.tensor_tensor(
                    km[:, i, :, :, :], kT[:, i, :].rearrange("p (b k) -> p b k", b=BT).unsqueeze(2)
                    .broadcast_to([64, BT, H0, C]),
                    mask0[:, :].unsqueeze(1).unsqueeze(3).broadcast_to([64, BT, H0, C]), ALU.mult)\
                    .then_inc(k_masked.sem, 1)
            elif name == "scores":
                after(pool, srecip, s, i + 1)
                nc.gpsimd.tensor_tensor(prob[:, i, :, :], prob[:, i, :, :],
                                        psums[:, i, :].unsqueeze(2).broadcast_to([P, H0, C]), ALU.mult)\
                    .then_inc(normed.sem, 1)
            elif name == "carry":
                for j in range(NT):
                    A.read(pool, s, ("out", j))
                after(pool, x2_out, s - 1, NT)
                nc.gpsimd.tensor_tensor(x1b[:, :, :], x1[:, :, :],
                                        consts["beta"][:, :].unsqueeze(1).broadcast_to([P, NT, D]), ALU.add)\
                    .then_inc(carried.sem, 1)
            elif name == "up":
                after(pool, sq_high, s, i + 1)
                nc.gpsimd.tensor_tensor(gs[:, 1, 2 * i:2 * i + 2, :],
                                        sq[:, i % 2, :].rearrange("p (m n) -> p m n", m=2),
                                        f32(gs[:, 0, 2 * i:2 * i + 2, :]), ALU.subtract).then_inc(sq_low.sem, 1)
            elif name == "down":
                after(pool, var_out, s, i + 1)
                nc.gpsimd.tensor_tensor(rstd[:, :], mv[:, 1:2], consts["minus_half"][:, :], ALU.pow)\
                    .then_inc(rstd_out.sem, 1)

        go(step, pool)

    @block.vector
    def _(dve):
        def step(kind, name, i, s):
            if name == "mix":
                after(dve, y_high, s, i + 1)
                nc.vector.tensor_tensor(ys[:, i, 1, :, :], A[("mix", i)].rearrange("p (q n) -> p q n", q=Q),
                                        f32(ys[:, i, 0, :, :]), ALU.subtract).then_inc(A.free(("mix", i)), 1)
            elif name == "scores":
                A.filled(dve, s, ("vrep", i))
                nc.vector.tensor_tensor(
                    vb[:, i, :, :].rearrange("p b (g h e) -> p (b g) h e", g=2, e=E0),
                    A[("vrep", i)][:, 0:BT * 64].rearrange("p (b g h e) -> p (b g) h e", b=BT, g=2, e=E0),
                    vmask0[:, :].unsqueeze(1).unsqueeze(3).broadcast_to([P, 2 * BT, 4, E0]), ALU.mult)\
                    .then_inc(A.free(("vrep", i)), 1)
                A.filled(dve, s, ("scores", i))
                bank = A[("scores", i)][:, 0:H0 * C].rearrange("p (h k) -> p h k", h=H0)
                nc.vector.tensor_reduce(pmax[:, i, :], bank, AX_X, ALU.max).then_inc(smax.sem, 1)
                after(dve, smax, s, i + 1)
                nc.vector.tensor_tensor(prob[:, i, :, :], bank,
                                        pmax[:, i, :].unsqueeze(2).broadcast_to([P, H0, C]), ALU.subtract)\
                    .then_inc(A.free(("scores", i)), 1)
                after(dve, expd, s, i + 1)
                nc.vector.tensor_reduce(psums[:, i, :], prob[:, i, :, :], AX_X, ALU.add).then_inc(ssum.sem, 1)
                after(dve, ssum, s, i + 1)
                nc.vector.reciprocal(psums[:, i, :], psums[:, i, :]).then_inc(srecip.sem, 1)
            elif name == "values":
                after(dve, o_high, s, 2 * i + 2)
                nc.vector.tensor_tensor(out_a[64:128, i, :], A[("values", i)][0:64, 0:P], f32(out_a[0:64, i, :]),
                                        ALU.subtract).then_inc(A.free(("values", i)), 1)
            elif name == "out":
                A.filled(dve, s, ("out", i))
                after(dve, carried, s - 1, 1)
                after(dve, xp_in[i], s - 1, Q * BT)
                nc.vector.tensor_tensor(x1[:, i, :], A[("out", i)], x[:, i, :], ALU.add)\
                    .then_inc(A.free(("out", i)), 1)
            elif name == "phase":
                after(dve, xp_high, s, i + 1)
                nc.vector.tensor_tensor(xps[:, i, 1, :, :], xp[i][:, :, :], f32(xps[:, i, 0, :, :]), ALU.subtract)\
                    .then_inc(xp_low.sem, 1)
            elif name == "conv":
                after(dve, h_high, s, i + 1)
                nc.vector.tensor_tensor(
                    hs[:, 1, :, i * P:(i + 1) * P].rearrange("p q (b o) -> p b q o", b=BT),
                    F[("conv", i)].rearrange("p (b q o) -> p b q o", b=BT, q=Q),
                    f32(hs[:, 0, :, i * P:(i + 1) * P]).rearrange("p q (b o) -> p b q o", b=BT), ALU.subtract)\
                    .then_inc(F.free(("conv", i)), 1)
            elif name == "gate":
                F.filled(dve, s, ("gate", 0))
                F.read(dve, s - 1, ("down", NT - 1))
                dve.sem_inc(held.sem, 1)
                for j in range(NT):
                    last = nc.vector.max(logit8[:, j, :], F[("gate", 0)][:, NE0 * j:NE0 * (j + 1)])
                last.then_inc(F.free(("gate", 0)), 1)
                F.read(dve, s, ("gate", 0))
                nc.vector.tensor_tensor(gsum[:, :], logit8[:, :, 0], logit8[:, :, 1], ALU.add)\
                    .then_inc(gsummed.sem, 1)
            elif name == "up":
                after(dve, relu_out, s, i + 1)
                after(dve, sq_low, s, i - 1)
                nc.vector.tensor_tensor(sq[:, i % 2, :], F[("up", i)], relu[:, i % 2, :], ALU.mult)\
                    .then_inc(F.free(("up", i)), 1)
            elif name == "latent":
                after(dve, f_high, s, 1)
                nc.vector.tensor_tensor(fs[:, 1, :, :], F[("latent", 0)].rearrange("p (m n) -> p m n", m=2),
                                        f32(fs[:, 0, :, :]), ALU.subtract)\
                    .then_inc(F.free(("latent", 0)), 1)
            elif name == "down":
                F.filled(dve, s, ("down", i))
                F.read(dve, s, ("routed", i))
                after(dve, x2_stored, s, i)
                nc.vector.tensor_tensor(z[:, :], F[("down", i)], routed[:, :], ALU.add)\
                    .then_inc(F.free(("down", i)), 1)
                F.read(dve, s, ("down", i))
                nc.vector.bn_stats(stats[:, :], z[:, :]).then_inc(stats_out.sem, 1)
                after(dve, stats_out, s, i + 1)
                dve.sem_inc(held.sem, 1)
                nc.vector.bn_aggr(mv[:, :], stats[:, :]).then_inc(mv_out.sem, 1)
                after(dve, mv_out, s, i + 1)
                nc.vector.tensor_scalar(mv[:, 1:2], mv[:, 1:2], EPS, None, ALU.add).then_inc(var_out.sem, 1)
                nc.vector.scalar_tensor_tensor(out=z[:, :], in0=z[:, :], scalar=mv[:, 0:1],
                                               in1=consts["gamma"][:, :], op0=ALU.subtract, op1=ALU.mult)\
                    .then_inc(scaled.sem, 1)
                after(dve, scaled, s, i + 1)
                after(dve, rstd_out, s, i + 1)
                after(dve, carried, s, 1)
                nc.vector.scalar_tensor_tensor(out=z[:, :], in0=z[:, :], scalar=rstd[:, :], in1=x1b[:, i, :],
                                               op0=ALU.mult, op1=ALU.add).then_inc(x2_out.sem, 1)

        go(step, dve)

    @block.tensor
    def _(pe):
        mm = nc.tensor.matmul

        def step(kind, name, i, s):
            if name == "mix":
                use = ("mix", i)
                after(pe, x_high, s, i + 1)
                after(pe, x_low, s, i + 1)
                A.claim(pe, s, use)
                bank = A[use]
                mm(bank.rearrange("p (q n) -> p q n", q=Q), ones[0:2 * C, 0:P],
                   rows[:, i, :].unsqueeze(1).broadcast_to([2 * C, Q, P]), start=True, stop=False)
                for q in range(Q):
                    last = matmul_split(pe, bank[:, q * P:(q + 1) * P],
                                        (xs[:, i, 0, q * P:(q + 1) * P], xs[:, i, 1, q * P:(q + 1) * P]),
                                        (mix[:, i, 0, :], mix[:, i, 1, :]), False, q == Q - 1)
                last.then_inc(A.ready(use), 1)
            elif name == "qkv":
                use = ("qkv", i)
                A.read(pe, s, ("mix", i))
                A.claim(pe, s, use)
                bank = A[use]
                mm(bank[:, 0:P], bqkv[:, 0:P], ones[0:2 * C, 0:P], start=True, stop=False)
                for q in range(Q):
                    matmul_split(pe, bank[:, 0:P], (qkv_h[:, q * 192:q * 192 + P], qkv_l[:, q * 192:q * 192 + P]),
                                 (ys[:, i, 0, q, :], ys[:, i, 1, q, :]), False, q == Q - 1)
                mm(bank[:, P:P + 64], ones[0:2 * C, 0:P], bqkv[:, P:192], start=True, stop=False)
                for q in range(Q):
                    last = matmul_split(pe, bank[:, P:P + 64], (ys[:, i, 0, q, :], ys[:, i, 1, q, :]),
                                        (qkv_h[:, q * 192 + P:q * 192 + 192], qkv_l[:, q * 192 + P:q * 192 + 192]),
                                        False, q == Q - 1)
                last.then_inc(A.ready(use), 1)
            elif name == "scores":
                use = ("vrep", i)
                A.read(pe, s, ("qkv", i))
                A.claim(pe, s, use)
                for b in range(BT):
                    last = mm(A[use][:, b * 64:(b + 1) * 64], vsel[:, b, :], v[:, i, :], start=True, stop=True)
                last.then_inc(A.ready(use), 1)
                use = ("scores", i)
                after(pe, k_masked, s, i + 1)
                A.claim(pe, s, use)
                pe.sem_inc(held.sem, 1)
                for b in range(BT):
                    last = mm(A[use][C * b:C * b + C, 0:H0 * C], qT[:, i, C * b:C * b + C],
                              km[:, i, b, :, :].rearrange("p h k -> p (h k)"), start=True, stop=True)
                last.then_inc(A.ready(use), 1)
            elif name == "turn":
                use = ("turn", i)
                after(pe, normed, s, i + 1)
                A.claim(pe, s, use)
                for h in range(2):
                    last = nc.tensor.transpose(A[use][:, h * P:(h + 1) * P],
                                               prob[:, i, 4 * h:4 * h + 4, :].rearrange("p h k -> p (h k)"),
                                               ident[:, :])
                last.then_inc(A.ready(use), 1)
            elif name == "values":
                use = ("values", i)
                A.read(pe, s, ("turn", i))
                A.read(pe, s, ("vrep", i))
                A.claim(pe, s, use)
                for b in range(BT):
                    for h in range(2):
                        last = mm(A[use][C * h:C * h + C, C * b:C * b + C], vb[:, i, b, C * h:C * h + C],
                                  pT[:, i, h, C * b:C * b + C], start=True, stop=True)
                last.then_inc(A.ready(use), 1)
            elif name == "out":
                use = ("out", i)
                A.read(pe, s, ("values", i))
                A.claim(pe, s, use)
                mm(A[use], out_a[:, i, :], out_w[:, 0, :], start=True, stop=False)
                mm(A[use], out_b[:, i, :], out_w[:, 1, :], start=False, stop=True).then_inc(A.ready(use), 1)
            elif name == "conv":
                use = ("conv", i)
                after(pe, xp_low, s, i + 1)
                after(pe, context_in[i], s, 1)
                F.claim(pe, s, use)
                bank = F[use]
                mm(bank.rearrange("p (b q o) -> p b q o", b=BT, q=Q), ones[0:2 * C, 0:P],
                   crow[:, i, :].rearrange("p (b o) -> p b o", b=BT).unsqueeze(2).broadcast_to([2 * C, BT, Q, C]),
                   start=True, stop=False)
                for b in range(BT):
                    for shift in range(3):
                        w = CONV + shift * P
                        last = matmul_split(pe, bank[:, b * P:(b + 1) * P],
                                            (xps[:, i, 0, b, shift:shift + P], xps[:, i, 1, b, shift:shift + P]),
                                            (wh[:, w:w + P], wl[:, w:w + P]), False, b == BT - 1 and shift == 2)
                last.then_inc(F.ready(use), 1)
            elif name == "gate":
                use = ("gate", 0)
                for j in range(NT):
                    F.read(pe, s, ("conv", j))
                F.claim(pe, s, use)
                for j in range(NT):
                    for q in range(Q):
                        w, r = GATE0 + q * NE0, slice(j * P, (j + 1) * P)
                        last = matmul_split(pe, F[use][:, j * NE0:(j + 1) * NE0], (hs[:, 0, q, r], hs[:, 1, q, r]),
                                            (wh[:, w:w + NE0], wl[:, w:w + NE0]), q == 0, q == Q - 1)
                last.then_inc(F.ready(use), 1)
            elif name in ("up", "latent"):
                use = (name, i)
                F.claim(pe, s, use)
                for j in range(2):
                    for q in range(Q):
                        w = UP + q * INT + (2 * i + j) * P if name == "up" else LATENT + q * LAT + j * P
                        last = matmul_split(pe, F[use][:, j * ROUND:(j + 1) * ROUND],
                                            (wh[:, w:w + P], wl[:, w:w + P]),
                                            (hs[:, 0, q, :], hs[:, 1, q, :]), q == 0, q == Q - 1)
                last.then_inc(F.ready(use), 1)
            elif name == "down":
                r = slice(i * P, (i + 1) * P)
                use = ("routed", i)
                F.read(pe, s, ("latent", 0))
                F.claim(pe, s, use)
                for m in range(2):
                    w = FC2 + m * D
                    last = matmul_split(pe, F[use], (fs[:, 0, m, r], fs[:, 1, m, r]),
                                        (wh[:, w:w + D], wl[:, w:w + D]), m == 0, m == 1)
                last.then_inc(F.ready(use), 1)
                use = ("down", i)
                F.claim(pe, s, use)
                for m in range(INT // P):
                    w = DOWN + m * D
                    if m % 2 == 0:
                        after(pe, sq_low, s, m // 2 + 1)
                    last = matmul_split(pe, F[use], (gs[:, 0, m, r], gs[:, 1, m, r]),
                                        (wh[:, w:w + D], wl[:, w:w + D]), m == 0, m == INT // P - 1)
                last.then_inc(F.ready(use), 1)

        go(step, pe)


ATTEND1 = [(name, i) for name in ("split", "mix", "turnx", "qkv", "turnk", "score", "turnp", "values", "turno",
                                  "turnq", "out", "part") for i in range(NT)]
FORWARD1 = [("carry", 0), ("cmix", 0), ("cmix", 1), ("gate", 0), ("spread", 0), ("expert", 0), ("expert", 1),
            ("expert", 2), ("expert", 3), ("down", 0), ("down", 1)]
BODY1 = [("F", "carry", 0), ("F", "cmix", 0), ("F", "cmix", 1), ("A", "split", 0), ("A", "split", 1),
         ("F", "gate", 0), ("A", "mix", 0), ("A", "mix", 1), ("F", "spread", 0), ("A", "turnx", 0),
         ("F", "expert", 0), ("A", "turnx", 1), ("A", "qkv", 0), ("A", "qkv", 1), ("A", "turnk", 0),
         ("F", "expert", 1), ("A", "turnk", 1), ("A", "score", 0), ("A", "score", 1), ("F", "expert", 2),
         ("A", "turnp", 0), ("A", "turnp", 1), ("A", "values", 0), ("A", "values", 1), ("F", "expert", 3),
         ("A", "turno", 0), ("A", "turno", 1), ("F", "down", 0), ("A", "turnq", 0), ("A", "turnq", 1),
         ("A", "out", 0), ("A", "out", 1), ("F", "down", 1), ("A", "part", 0), ("A", "part", 1)]


def layer1(nc, ctx, t, sb, sem, scratch, psum, consts, weights, out):
    wh, wl, stage = weights
    ident, ones, vsel, dequant = (consts[k] for k in ("ident", "ones", "vsel", "dequant"))
    identb = sb("ident_bf16", [P, P], BF16)
    wbit = sb("ternary", [P, Q, 3 * P + 2 * D - P], BF16)
    WQ, WK, WV, WO = 0, D, D + P, D + 2 * P
    lnw, lnb = sb("ln_w", [P, D], F32), sb("ln_b", [P, D], F32)
    spread = sb("spread", [2 * C, EI], F32R)
    spread32 = sb("spread32", [2 * C, EI], F32)
    cosw, sinw = sb("rope_cos", [P, HD], F32), sb("rope_sin", [P, HD], F32)
    kmask, vmask = sb("kmask1", [P, KV], F32), sb("vmask1", [P, 4], F32)
    x = sb("x2", [P, NT, D], F32)
    mixa, mixb = sb("mix1", [P, NT, 2, P], F32R), sb("mix2", [P, NT, 2, P], F32R)
    rowa, rowb = sb("bias_rows1", [2 * C, NT, P], F32R), sb("bias_rows2", [2 * C, NT, P], F32R)
    xs = sb("x_split1", [P, NT, 2, D], F32R)
    nrm = sb("normed", [P, NT, D], F32)
    xq = sb("quantized", [P, NT, D], BF16)
    xqT = sb("quantizedT", [P, NT, Q, P], BF16)
    rot = sb("roped", [P, NT, D + P], F32)
    rot2 = sb("roped_swapped", [P, D + P], F32)
    v = sb("v1", [P, NT, P], F32)
    vb = sb("v_blocks1", [P, NT, BT, P], F32)
    qT, kT = sb("qT1", [P, NT, BT, REP, C], F32), sb("kT1", [P, NT, P], F32)
    km = sb("k_masked1", [P, NT, BT, KV, C], F32)
    prob = sb("prob1", [P, NT, BT, KV, C], F32)
    pmax, psums = sb("prob_max1", [P, NT, BT, KV], F32), sb("prob_sum1", [P, NT, BT, KV], F32)
    stats, mv, rstd = sb("stats1", [P, NT, 6], F32), sb("mv1", [P, NT, 2], F32), sb("rstd1", [P, NT], F32)
    amax, scale = sb("abs_max", [P, NT, 2], F32), sb("quant_scale", [P, NT, 2], F32)
    back = sb("dequant_scale", [P, NT, 4], F32)
    x3c = sb("x3_carried", [P, NT, D], F32)
    hs = sb("z_split", [P, 2, Q, ROUND], F32R)
    logit, top, keys = sb("logits", [P, NT, NE1], F32), sb("top8", [P, NT, 8], F32), sb("top2", [P, NT, 8], F32)
    left, share = sb("others", [P, NT, NE1], F32), sb("share", [P, NT, NE1], F32)
    esum = sb("share_sum", [P, NT], F32)
    wT = sb("shareT", [2 * C, ROUND], F32R)
    th, ga = sb("tanh", [P, 2, 2 * ROUND], F32), sb("gated", [P, 2, 2 * ROUND], F32)
    gs = sb("expert_split", [P, 2, M1, ROUND], F32R)
    z = sb("out_tile", [P, D], F32)

    def signal(name, per_round, unit=1):
        return Signal(sem("l1_" + name), per_round, unit)

    def many(names, per_round):
        return (signal(n, per_round) for n in names.split())

    x_in = [signal(f"x_in{i}", 5, 16) for i in range(NT)]
    x_high, x_low, x3_high, x3_low = many("x_high x_low x3_high x3_low", NT)
    stats_out, mv_out, var_out, rstd_out, scaled, normed, absmax, clipped, inverted, factors, rounded, quantized = many(
        "stats mv var rstd scaled normed absmax clipped inverted factors rounded quantized", NT)
    o_absmax, o_clipped, o_inverted, o_factors, o_quantized = many(
        "o_absmax o_clipped o_inverted o_factors o_quantized", NT)
    roped, added, v_out, k_masked = many("roped added v_out k_masked", NT)
    smax, expd, ssum, srecip, pnormed = many("max exp sum recip pnormed", 2 * NT)
    carried, z_high = signal("carried", 1), signal("z_high", NT)
    topped, keyed, replaced, chosen, below, exped, shares, ssumed, inv_sum, share_out = many(
        "topped keyed replaced chosen below exped shares ssumed inv_sum share_out", 1)
    wT_high = signal("wT_high", 1)
    tanh_out, gated, e_high, e_low = many("tanh gated e_high e_low", 4)
    z_added, z_stored = signal("z_added", NT), signal("z_stored", NT, 16)
    held = signal("held", 1)
    tables = sem("l1_tables")
    made = sem("l1_made")
    staged = [sem(f"l1_staged{i}") for i in range(2)]
    high, low = sem("l1_high"), sem("l1_low")

    a_uses = [(n, i) for n in ("mix", "turnx", "q", "kv", "turnq_", "turnk_", "vrep") for i in range(NT)]
    a_uses += [("score", j) for j in range(2 * NT)] + [("turnp", j) for j in range(2 * NT)]
    a_uses += [(n, i) for n in ("values", "turno", "turnq", "out") for i in range(NT)]
    A = Banks(psum, 0, 4, a_uses, [sem(f"l1_a_ready{i}") for i in range(4)], [sem(f"l1_a_free{i}") for i in range(4)])
    f_uses = [("cmix", 0), ("cmix", 1), ("gate", 0), ("spread", 0)]
    f_uses += [(n, k) for k in range(4) for n in ("g", "u", "w")] + [("down", 0), ("down", 1)]
    F = Banks(psum, 4, 4, f_uses, [sem(f"l1_f_ready{i}") for i in range(4)], [sem(f"l1_f_free{i}") for i in range(4)])

    pieces = []
    for first, name, chunks, width in ((GW, "g1", Q, EI), (UW, "u1", Q, EI), (DW, "d1", M1, D)):
        per = STAGE // width
        for c0 in range(0, chunks, per):
            pieces.append((first + c0 * width, t[name], c0, min(per, chunks - c0), width))

    def go(steps, engine):
        for name, i in ATTEND1:
            steps("A", name, i, 0)
        for kind, name, i in BODY1:
            steps(kind, name, i, 1 if kind == "A" else 0)
        with engine.Fori(2, ROUNDS) as r:
            for kind, name, i in BODY1:
                steps(kind, name, i, r if kind == "A" else r - 1)
        for name, i in FORWARD1:
            steps("F", name, i, ROUNDS - 1)

    def cols(k):
        return min(2, M1 - 2 * k) * ROUND

    block = ctx.enter_context(nc.Block())

    @block.sync
    def _(sp):
        for dst, src in ((lnw[:, :], t["ln_w"].broadcast_to([P, D])), (lnb[:, :], t["ln_b"].broadcast_to([P, D])),
                         (spread32[:, :], t["spread"]), (cosw[:, :], t["rope_cos"]), (sinw[:, :], t["rope_sin"]),
                         (kmask[:, :], t["kmask"]), (vmask[:, :], t["vmask"]), (wbit[:, :, :], scratch["ternary"])):
            sp.dma_start(dst, src).then_inc(tables, 16)

        def stage_weights():
            for k, (first, src, c0, n, width) in enumerate(pieces):
                if k >= 2:
                    sp.wait_ge(low, k - 1)
                sp.dma_start(stage[:, k % 2, 0:n * width].rearrange("p (c n) -> p c n", c=n),
                             src[c0 * P:(c0 + n) * P, :].rearrange("(c p) n -> p c n", p=P)).then_inc(staged[k % 2], 16)

        def step(kind, name, i, s):
            if name == "split":
                after(sp, carried, s - 1, 1)
                sp.sem_inc(held.sem, 1)
                after(sp, x3_low, s - 1, i + 1)
                sp.sem_inc(held.sem, 1)
                F.read(sp, s - 1, ("cmix", i))
                sp.sem_inc(held.sem, 1)
                n, r = x_in[i].sem, bass.ds(s * ROUND + i * P, P)
                sp.dma_start(x[:, i, :], scratch["x2"][r, :]).then_inc(n, 16)
                sp.dma_start(f32(mixa[:, i, :, :]), scratch["mix_t"][1][r, :, :]).then_inc(n, 16)
                sp.dma_start(f32(mixb[:, i, :, :]), scratch["mix_t"][2][r, :, :]).then_inc(n, 16)
                sp.dma_start(f32(rowa[:, i, :]), scratch["rows"][1][:, r]).then_inc(n, 16)
                sp.dma_start(f32(rowb[:, i, :]), scratch["rows"][2][:, r]).then_inc(n, 16)
                if isinstance(s, int) and s == 0 and i == NT - 1:
                    stage_weights()
            elif name == "down":
                after(sp, z_added, s, i + 1)
                sp.sem_inc(held.sem, 1)
                sp.dma_start(out[bass.ds(s * ROUND + i * P, P), :], z[:, :]).then_inc(z_stored.sem, 16)

        go(step, sp)
        after(sp, z_stored, ROUNDS - 1, NT)

    @block.scalar
    def _(act):
        copy = lambda out, in_, **k: nc.scalar.activation(out, in_, ACT.Copy, **k)

        def split_weights():
            for k, (first, _, _, n, width) in enumerate(pieces):
                act.wait_ge(staged[k % 2], 16 * (k // 2 + 1))
                copy(wh[:, first:first + n * width], stage[:, k % 2, 0:n * width]).then_inc(high, 1)

        copy(identb[:, :], ident[:, :]).then_inc(made, 1)

        def step(kind, name, i, s):
            if name == "split":
                after(act, x_in[i], s, 5)
                copy(xs[:, i, 0, :], x[:, i, :]).then_inc(x_high.sem, 1)
                if isinstance(s, int) and s == 0 and i == NT - 1:
                    split_weights()
            elif name == "turnx":
                A.filled(act, s, ("turnx", i))
                copy(xqT[:, i, :, :], turned(("turnx", i))).then_inc(A.free(("turnx", i)), 1)
            elif name == "turnk":
                A.filled(act, s, ("turnk_", i))
                copy(kT[:, i, :], A[("turnk_", i)][:, 0:P]).then_inc(A.free(("turnk_", i)), 1)
                A.filled(act, s, ("turnq_", i))
                copy(qT[:, i, :, :, :].rearrange("p b r q -> p r b q"),
                     A[("turnq_", i)].rearrange("p (r b q) -> p r b q", r=REP, b=BT))\
                    .then_inc(A.free(("turnq_", i)), 1)
            elif name == "score":
                for j in (2 * i, 2 * i + 1):
                    A.read(act, s, ("score", j))
                    h = prob[:, i, 2 * (j % 2):2 * (j % 2) + 2, :, :]
                    nc.scalar.activation(h, h, ACT.Exp, scale=float(HD) ** -0.5).then_inc(expd.sem, 1)
            elif name == "turnp":
                for j in (2 * i, 2 * i + 1):
                    A.filled(act, s, ("turnp", j))
                    copy(km[:, i, 2 * (j % 2):2 * (j % 2) + 2, :, :].rearrange("p b g k -> p (b g k)"),
                         A[("turnp", j)]).then_inc(A.free(("turnp", j)), 1)
            elif name == "values":
                A.filled(act, s, ("values", i))
                copy(nrm[:, i, :].rearrange("p (r b q) -> p b r q", r=REP, b=BT),
                     A[("values", i)].rearrange("p (b r q) -> p b r q", r=REP, b=BT))\
                    .then_inc(A.free(("values", i)), 1)
            elif name == "turnq":
                A.filled(act, s, ("turnq", i))
                copy(xqT[:, i, :, :], turned(("turnq", i))).then_inc(A.free(("turnq", i)), 1)
            elif name == "part":
                A.read(act, s, ("out", i))
                copy(xs[:, i, 0, :], x[:, i, :]).then_inc(x3_high.sem, 1)
            elif name == "cmix":
                F.filled(act, s, ("cmix", i))
                F.read(act, s - 1, ("u", 3))
                copy(hs[:, 0, :, i * P:(i + 1) * P], F[("cmix", i)].rearrange("p (q n) -> p q n", q=Q))\
                    .then_inc(z_high.sem, 1)
            elif name == "gate":
                after(act, below, s, 1)
                nc.scalar.activation(share[:, :, :], share[:, :, :], ACT.Exp).then_inc(exped.sem, 1)
            elif name == "expert":
                n = cols(i)
                F.filled(act, s, ("g", i))
                F.read(act, s if i >= 2 else s - 1, ("g", (i + 2) % 4))
                nc.scalar.activation(th[:, i % 2, 0:n], F[("g", i)][:, 0:n], ACT.Tanh, scale=0.5)\
                    .then_inc(tanh_out.sem, 1)
                F.read(act, s, ("w", i))
                if i == 0:
                    F.read(act, s - 1, ("down", NT - 1))
                copy(gs[:, 0, 2 * i:2 * i + n // ROUND, :], ga[:, i % 2, 0:n].rearrange("p (m n) -> p m n", n=ROUND))\
                    .then_inc(e_high.sem, 1)

        def turned(use):
            return A[use][:, 0:D // 2].bitcast(BF16).rearrange("p (q n) -> p q n", q=Q)

        go(step, act)

    @block.gpsimd
    def _(pool):
        nc.gpsimd.memset(keys[:, :, :], FAR)
        nc.gpsimd.memset(f32(wT[:, :]), 0.0).then_inc(made, 1)

        def split_weights():
            for k, (first, _, _, n, width) in enumerate(pieces):
                pool.wait_ge(high, k + 1)
                w = slice(first, first + n * width)
                nc.gpsimd.tensor_tensor(wl[:, w], stage[:, k % 2, 0:n * width], f32(wh[:, w]), ALU.subtract)\
                    .then_inc(low, 1)

        def step(kind, name, i, s):
            if name == "split":
                after(pool, x_high, s, i + 1)
                nc.gpsimd.tensor_tensor(xs[:, i, 1, :], x[:, i, :], f32(xs[:, i, 0, :]), ALU.subtract)\
                    .then_inc(x_low.sem, 1)
                if isinstance(s, int) and s == 0 and i == NT - 1:
                    split_weights()
            elif name == "mix":
                after(pool, var_out, s, i + 1)
                nc.gpsimd.tensor_tensor(rstd[:, i:i + 1], mv[:, i, 1:2], consts["minus_half"][:, :], ALU.pow)\
                    .then_inc(rstd_out.sem, 1)
            elif name == "qkv":
                after(pool, roped, s, i + 1)
                nc.gpsimd.tensor_tensor(rot[:, i, :], rot[:, i, :], rot2[:, :], ALU.add).then_inc(added.sem, 1)
            elif name == "turnk":
                A.read(pool, s, ("turnk_", i))
                if isinstance(s, int) and s == 0:
                    pool.wait_ge(tables, 16 * 8)
                nc.gpsimd.tensor_tensor(
                    km[:, i, :, :, :],
                    kT[:, i, :].rearrange("p (b k) -> p b k", b=BT).unsqueeze(2).broadcast_to([P, BT, KV, C]),
                    kmask[:, :].unsqueeze(1).unsqueeze(3).broadcast_to([P, BT, KV, C]), ALU.mult)\
                    .then_inc(k_masked.sem, 1)
            elif name == "score":
                for j in (0, 1):
                    after(pool, srecip, s, 2 * i + j + 1)
                    h = prob[:, i, 2 * j:2 * j + 2, :, :].rearrange("p b g k -> p (b g) k")
                    nc.gpsimd.tensor_tensor(
                        h, h, psums[:, i, 2 * j:2 * j + 2, :].rearrange("p b g -> p (b g)").unsqueeze(2)
                        .broadcast_to([P, 2 * KV, C]), ALU.mult).then_inc(pnormed.sem, 1)
            elif name == "part":
                after(pool, x3_high, s, i + 1)
                nc.gpsimd.tensor_tensor(xs[:, i, 1, :], x[:, i, :], f32(xs[:, i, 0, :]), ALU.subtract)\
                    .then_inc(x3_low.sem, 1)
            elif name == "carry":
                for j in range(NT):
                    A.read(pool, s, ("out", j))
                after(pool, z_added, s - 1, NT)
                pool.sem_inc(held.sem, 1)
                nc.gpsimd.tensor_copy(x3c[:, :, :], x[:, :, :]).then_inc(carried.sem, 1)
            elif name == "expert":
                m = cols(i) // ROUND
                after(pool, e_high, s, i + 1)
                nc.gpsimd.tensor_tensor(gs[:, 1, 2 * i:2 * i + m, :],
                                        ga[:, i % 2, 0:m * ROUND].rearrange("p (m n) -> p m n", m=m),
                                        f32(gs[:, 0, 2 * i:2 * i + m, :]), ALU.subtract).then_inc(e_low.sem, 1)

        go(step, pool)

    @block.vector
    def _(dve):
        dve.wait_ge(tables, 16 * 8)
        nc.vector.tensor_copy(spread[:, :], spread32[:, :]).then_inc(made, 1)

        def quantize(src, i, which, s, done, clip, inv, fac, last):
            nc.vector.tensor_reduce(amax[:, i, which:which + 1], src, AX_X, ALU.max, apply_absolute_value=True)\
                .then_inc(done.sem, 1)
            after(dve, done, s, i + 1)
            a = amax[:, i, which:which + 1]
            nc.vector.tensor_scalar(a, a, 1e-5, None, ALU.max).then_inc(clip.sem, 1)
            after(dve, clip, s, i + 1)
            nc.vector.reciprocal(scale[:, i, which:which + 1], a).then_inc(inv.sem, 1)
            r = (0, 3) if which == 0 else (3, 4)
            nc.vector.tensor_scalar(back[:, i, r[0]:r[1]], dequant[:, r[0]:r[1]], a, None, ALU.mult)
            after(dve, inv, s, i + 1)
            nc.vector.tensor_scalar(scale[:, i, which:which + 1], scale[:, i, which:which + 1], QB, None, ALU.mult)\
                .then_inc(fac.sem, 1)
            after(dve, fac, s, i + 1)
            tmp = nrm[:, i, :] if which == 0 else rot[:, i, 0:D]
            nc.vector.tensor_scalar(tmp, src, scale[:, i, which:which + 1], ROUND_MAGIC, ALU.mult, ALU.add)\
                .then_inc(last, 1)

        def step(kind, name, i, s):
            if name == "mix":
                use = ("mix", i)
                A.filled(dve, s, use)
                nc.vector.bn_stats(stats[:, i, :], A[use]).then_inc(stats_out.sem, 1)
                after(dve, stats_out, s, i + 1)
                dve.sem_inc(held.sem, 1)
                nc.vector.bn_aggr(mv[:, i, :], stats[:, i, :]).then_inc(mv_out.sem, 1)
                after(dve, mv_out, s, i + 1)
                nc.vector.tensor_scalar(mv[:, i, 1:2], mv[:, i, 1:2], EPS, None, ALU.add).then_inc(var_out.sem, 1)
                nc.vector.scalar_tensor_tensor(out=nrm[:, i, :], in0=A[use], scalar=mv[:, i, 0:1], in1=lnw[:, :],
                                               op0=ALU.subtract, op1=ALU.mult).then_inc(A.free(use), 1)
                A.read(dve, s, use)
                after(dve, rstd_out, s, i + 1)
                nc.vector.scalar_tensor_tensor(out=nrm[:, i, :], in0=nrm[:, i, :], scalar=rstd[:, i:i + 1],
                                               in1=lnb[:, :], op0=ALU.mult, op1=ALU.add).then_inc(normed.sem, 1)
                after(dve, normed, s, i + 1)
                quantize(nrm[:, i, :], i, 0, s, absmax, clipped, inverted, factors, rounded.sem)
                after(dve, rounded, s, i + 1)
                nc.vector.tensor_scalar(xq[:, i, :], nrm[:, i, :], -ROUND_MAGIC, QB, ALU.add, ALU.min)\
                    .then_inc(quantized.sem, 1)
            elif name == "qkv":
                A.filled(dve, s, ("q", i))
                after(dve, added, s, i)
                for src, first, heads, which in ((A[("q", i)], 0, KV * REP, 0), (A[("kv", i)][:, 0:P], D, KV, 1)):
                    if which:
                        A.filled(dve, s, ("kv", i))
                    half = HD // 2
                    sv = src.rearrange("p (h d) -> p h d", d=HD)
                    o1 = rot[:, i, first:first + heads * HD].rearrange("p (h d) -> p h d", d=HD)
                    o2 = rot2[:, first:first + heads * HD].rearrange("p (h d) -> p h d", d=HD)
                    a = back[:, i, which:which + 1]

                    def table(w, lo, hi):
                        return w[:, lo:hi].unsqueeze(1).broadcast_to([P, heads, hi - lo])

                    nc.vector.scalar_tensor_tensor(out=o1, in0=sv, scalar=a, in1=table(cosw, 0, HD),
                                                   op0=ALU.mult, op1=ALU.mult)
                    nc.vector.scalar_tensor_tensor(out=o2[:, :, 0:half], in0=sv[:, :, half:HD], scalar=a,
                                                   in1=table(sinw, 0, half), op0=ALU.mult, op1=ALU.mult)
                    last = nc.vector.scalar_tensor_tensor(out=o2[:, :, half:HD], in0=sv[:, :, 0:half], scalar=a,
                                                          in1=table(sinw, half, HD), op0=ALU.mult, op1=ALU.mult)
                    if which == 0:
                        last.then_inc(A.free(("q", i)), 1)
                    else:
                        last.then_inc(roped.sem, 1)
                nc.vector.tensor_scalar(v[:, i, :], A[("kv", i)][:, P:2 * P], back[:, i, 2:3], None, ALU.mult)\
                    .then_inc(A.free(("kv", i)), 1)
            elif name == "turnk":
                A.filled(dve, s, ("vrep", i))
                nc.vector.tensor_tensor(
                    vb[:, i, :, :].rearrange("p b (g h e) -> p (b g) h e", g=2, e=HD),
                    A[("vrep", i)].rearrange("p (b g h e) -> p (b g) h e", b=BT, g=2, e=HD),
                    vmask[:, :].unsqueeze(1).unsqueeze(3).broadcast_to([P, 2 * BT, 4, HD]), ALU.mult)\
                    .then_inc(A.free(("vrep", i)), 1)
            elif name == "score":
                for j in (0, 1):
                    n = 2 * i + j
                    A.filled(dve, s, ("score", n))
                    bank = A[("score", n)].rearrange("p (b k) -> p b k", k=C)
                    m = pmax[:, i, 2 * j:2 * j + 2, :].rearrange("p b g -> p (b g)")
                    nc.vector.tensor_reduce(m, bank, AX_X, ALU.max).then_inc(smax.sem, 1)
                    after(dve, smax, s, n + 1)
                    nc.vector.tensor_tensor(prob[:, i, 2 * j:2 * j + 2, :, :].rearrange("p b g k -> p (b g) k"), bank,
                                            m.unsqueeze(2).broadcast_to([P, 2 * KV, C]), ALU.subtract)\
                        .then_inc(A.free(("score", n)), 1)
                for j in (0, 1):
                    n = 2 * i + j
                    after(dve, expd, s, n + 1)
                    m = psums[:, i, 2 * j:2 * j + 2, :].rearrange("p b g -> p (b g)")
                    nc.vector.tensor_reduce(m, prob[:, i, 2 * j:2 * j + 2, :, :].rearrange("p b g k -> p (b g) k"),
                                            AX_X, ALU.add).then_inc(ssum.sem, 1)
                    after(dve, ssum, s, n + 1)
                    nc.vector.reciprocal(m, m).then_inc(srecip.sem, 1)
            elif name == "turno":
                use = ("turno", i)
                A.filled(dve, s, use)
                quantize(A[use], i, 1, s, o_absmax, o_clipped, o_inverted, o_factors, A.free(use))
                A.read(dve, s, use)
                nc.vector.tensor_scalar(xq[:, i, :], rot[:, i, 0:D], -ROUND_MAGIC, QB, ALU.add, ALU.min)\
                    .then_inc(o_quantized.sem, 1)
            elif name == "out":
                A.filled(dve, s, ("out", i))
                nc.vector.scalar_tensor_tensor(out=x[:, i, :], in0=A[("out", i)], scalar=back[:, i, 3:4],
                                               in1=x[:, i, :], op0=ALU.mult, op1=ALU.add)\
                    .then_inc(A.free(("out", i)), 1)
            elif name == "cmix":
                after(dve, z_high, s, i + 1)
                nc.vector.tensor_tensor(hs[:, 1, :, i * P:(i + 1) * P], F[("cmix", i)].rearrange("p (q n) -> p q n", q=Q),
                                        f32(hs[:, 0, :, i * P:(i + 1) * P]), ALU.subtract)\
                    .then_inc(F.free(("cmix", i)), 1)
            elif name == "gate":
                F.filled(dve, s, ("gate", 0))
                nc.vector.tensor_copy(logit[:, :, :], F[("gate", 0)][:, 0:NT * NE1].rearrange("p (j e) -> p j e", j=NT))\
                    .then_inc(F.free(("gate", 0)), 1)
                F.read(dve, s, ("gate", 0))
                dve.sem_inc(held.sem, 1)
                for j in range(NT):
                    last = nc.vector.max(top[:, j, :], logit[:, j, :])
                last.then_inc(topped.sem, 1)
                after(dve, topped, s, 1)
                nc.vector.tensor_copy(keys[:, :, 0:2], top[:, :, 0:2]).then_inc(keyed.sem, 1)
                nc.vector.tensor_tensor(share[:, :, :], logit[:, :, :], top[:, :, 0:1].broadcast_to([P, NT, NE1]),
                                        ALU.subtract).then_inc(below.sem, 1)
                after(dve, keyed, s, 1)
                dve.sem_inc(held.sem, 1)
                for j in range(NT):
                    last = nc.vector.match_replace(left[:, j, :], keys[:, j, :], logit[:, j, :], -FAR)
                last.then_inc(replaced.sem, 1)
                after(dve, replaced, s, 1)
                nc.vector.tensor_tensor(left[:, :, :], left[:, :, :], logit[:, :, :], ALU.not_equal)\
                    .then_inc(chosen.sem, 1)
                after(dve, chosen, s, 1)
                after(dve, exped, s, 1)
                nc.vector.tensor_tensor(share[:, :, :], share[:, :, :], left[:, :, :], ALU.mult).then_inc(shares.sem, 1)
                after(dve, shares, s, 1)
                nc.vector.tensor_reduce(esum[:, :], share[:, :, :], AX_X, ALU.add).then_inc(ssumed.sem, 1)
                after(dve, ssumed, s, 1)
                nc.vector.reciprocal(esum[:, :], esum[:, :]).then_inc(inv_sum.sem, 1)
                after(dve, inv_sum, s, 1)
                nc.vector.scalar_tensor_tensor(out=share[:, :, :], in0=share[:, :, :], scalar=0.5,
                                               in1=esum[:, :].unsqueeze(2).broadcast_to([P, NT, NE1]),
                                               op0=ALU.mult, op1=ALU.mult).then_inc(share_out.sem, 1)
            elif name == "spread":
                use = ("spread", 0)
                F.filled(dve, s, use)
                F.read(dve, s - 1, ("w", 3))
                nc.vector.tensor_copy(wT[0:NE1, :], F[use][0:NE1, 0:ROUND]).then_inc(wT_high.sem, 1)
                after(dve, wT_high, s, 1)
                nc.vector.tensor_tensor(wT[C:C + NE1, :], F[use][0:NE1, 0:ROUND], f32(wT[0:NE1, :]), ALU.subtract)\
                    .then_inc(F.free(use), 1)
            elif name == "expert":
                n = cols(i)
                a = ga[:, i % 2, 0:n]
                after(dve, tanh_out, s, i + 1)
                after(dve, e_low, s, i - 1)
                nc.vector.scalar_tensor_tensor(out=a, in0=th[:, i % 2, 0:n], scalar=1.0, in1=F[("g", i)][:, 0:n],
                                               op0=ALU.add, op1=ALU.mult).then_inc(F.free(("g", i)), 1)
                F.read(dve, s, ("g", i))
                F.filled(dve, s, ("u", i))
                nc.vector.tensor_tensor(a, a, F[("u", i)][:, 0:n], ALU.mult).then_inc(F.free(("u", i)), 1)
                F.read(dve, s, ("u", i))
                F.filled(dve, s, ("w", i))
                nc.vector.tensor_tensor(a, a, F[("w", i)][:, 0:n], ALU.mult).then_inc(F.free(("w", i)), 1)
            elif name == "down":
                F.filled(dve, s, ("down", i))
                after(dve, carried, s, 1)
                after(dve, z_stored, s, i)
                nc.vector.tensor_tensor(z[:, :], F[("down", i)], x3c[:, i, :], ALU.add)\
                    .then_inc(z_added.sem, 1)
                after(dve, z_added, s, i + 1)
                dve.sem_inc(F.free(("down", i)), 1)

        go(step, dve)

    @block.tensor
    def _(pe):
        mm = nc.tensor.matmul

        def turn_bf16(use, src):
            bank = A[use][:, 0:D // 2].bitcast(BF16)
            for q in range(Q):
                last = nc.tensor.transpose(bank[:, q * P:(q + 1) * P], src[:, q * P:(q + 1) * P], identb[:, :])
            last.then_inc(A.ready(use), 1)

        pe.wait_ge(tables, 16 * 8)
        pe.wait_ge(made, 3)

        def step(kind, name, i, s):
            r = slice(i * P, (i + 1) * P)
            if name == "mix":
                use = ("mix", i)
                after(pe, x_low, s, i + 1)
                A.claim(pe, s, use)
                mm(A[use], rowa[:, i, :], ones[0:2 * C, :], start=True, stop=False)
                matmul_split(pe, A[use], (mixa[:, i, 0, :], mixa[:, i, 1, :]), (xs[:, i, 0, :], xs[:, i, 1, :]),
                             False, True).then_inc(A.ready(use), 1)
            elif name == "turnx":
                after(pe, quantized, s, i + 1)
                A.claim(pe, s, ("turnx", i))
                turn_bf16(("turnx", i), xq[:, i, :])
            elif name == "qkv":
                A.read(pe, s, ("turnx", i))
                for use, first, n in ((("q", i), WQ, D), (("kv", i), WK, 2 * P)):
                    A.claim(pe, s, use)
                    for q in range(Q):
                        last = mm(A[use][:, 0:n], xqT[:, i, q, :], wbit[:, q, first:first + n],
                                  start=(q == 0), stop=(q == Q - 1))
                    last.then_inc(A.ready(use), 1)
            elif name == "turnk":
                after(pe, added, s, i + 1)
                A.claim(pe, s, ("turnk_", i))
                nc.tensor.transpose(A[("turnk_", i)][:, 0:P], rot[:, i, D:D + P], ident[:, :])\
                    .then_inc(A.ready(("turnk_", i)), 1)
                A.claim(pe, s, ("turnq_", i))
                for k in range(REP):
                    last = nc.tensor.transpose(A[("turnq_", i)][:, k * P:(k + 1) * P], rot[:, i, k * P:(k + 1) * P],
                                               ident[:, :])
                last.then_inc(A.ready(("turnq_", i)), 1)
                A.read(pe, s, ("kv", i))
                A.claim(pe, s, ("vrep", i))
                for b in range(BT):
                    last = mm(A[("vrep", i)][:, b * P:(b + 1) * P], vsel[:, b, :], v[:, i, :], start=True, stop=True)
                last.then_inc(A.ready(("vrep", i)), 1)
            elif name == "score":
                after(pe, k_masked, s, i + 1)
                A.read(pe, s, ("turnq_", i))
                for j in (0, 1):
                    use = ("score", 2 * i + j)
                    A.claim(pe, s, use)
                    for b in (2 * j, 2 * j + 1):
                        last = mm(A[use][:, (b % 2) * 256:(b % 2 + 1) * 256],
                                  qT[:, i, b, :, :].rearrange("p r q -> p (r q)"),
                                  km[:, i, b, :, :].rearrange("p g k -> p (g k)"), start=True, stop=True)
                    last.then_inc(A.ready(use), 1)
            elif name == "turnp":
                for j in (0, 1):
                    use = ("turnp", 2 * i + j)
                    after(pe, pnormed, s, 2 * i + j + 1)
                    A.claim(pe, s, use)
                    for k in range(4):
                        b, h = 2 * j + k // 2, k % 2
                        last = nc.tensor.transpose(A[use][:, k * P:(k + 1) * P],
                                                   prob[:, i, b, 4 * h:4 * h + 4, :].rearrange("p g k -> p (g k)"),
                                                   ident[:, :])
                    last.then_inc(A.ready(use), 1)
            elif name == "values":
                use = ("values", i)
                A.read(pe, s, ("turnp", 2 * i + 1))
                A.read(pe, s, ("vrep", i))
                A.claim(pe, s, use)
                for b in range(BT):
                    for h in range(2):
                        last = mm(A[use][64 * h:64 * h + 64, b * P:(b + 1) * P], vb[:, i, b, 64 * h:64 * h + 64],
                                  km[:, i, b, 4 * h:4 * h + 4, :].rearrange("p g k -> p (g k)"), start=True, stop=True)
                last.then_inc(A.ready(use), 1)
            elif name == "turno":
                use = ("turno", i)
                A.read(pe, s, ("values", i))
                A.claim(pe, s, use)
                for k in range(REP):
                    last = nc.tensor.transpose(A[use][:, k * P:(k + 1) * P], nrm[:, i, k * P:(k + 1) * P], ident[:, :])
                last.then_inc(A.ready(use), 1)
            elif name == "turnq":
                after(pe, o_quantized, s, i + 1)
                A.claim(pe, s, ("turnq", i))
                turn_bf16(("turnq", i), xq[:, i, :])
            elif name == "out":
                use = ("out", i)
                A.read(pe, s, ("turnq", i))
                A.claim(pe, s, use)
                for q in range(Q):
                    last = mm(A[use], xqT[:, i, q, :], wbit[:, q, WO:WO + D], start=(q == 0), stop=(q == Q - 1))
                last.then_inc(A.ready(use), 1)
            elif name == "cmix":
                use = ("cmix", i)
                after(pe, x3_low, s, i + 1)
                F.claim(pe, s, use)
                bank = F[use]
                mm(bank.rearrange("p (q n) -> p q n", q=Q), ones[0:2 * C, 0:P],
                   rowb[:, i, :].unsqueeze(1).broadcast_to([2 * C, Q, P]), start=True, stop=False)
                for q in range(Q):
                    w = slice(q * P, (q + 1) * P)
                    last = matmul_split(pe, bank[:, w], (xs[:, i, 0, w], xs[:, i, 1, w]),
                                        (mixb[:, i, 0, :], mixb[:, i, 1, :]), False, q == Q - 1)
                last.then_inc(F.ready(use), 1)
            elif name == "gate":
                use = ("gate", 0)
                for j in range(NT):
                    F.read(pe, s, ("cmix", j))
                F.claim(pe, s, use)
                gate_h, gate_l = consts["gate1"]
                for j in range(NT):
                    for q in range(Q):
                        n, w = slice(j * P, (j + 1) * P), slice(q * NE1, (q + 1) * NE1)
                        last = matmul_split(pe, F[use][:, j * NE1:(j + 1) * NE1], (hs[:, 0, q, n], hs[:, 1, q, n]),
                                            (gate_h[:, w], gate_l[:, w]), q == 0, q == Q - 1)
                last.then_inc(F.ready(use), 1)
            elif name == "spread":
                use = ("spread", 0)
                after(pe, share_out, s, 1)
                F.claim(pe, s, use)
                for j in range(NT):
                    last = nc.tensor.transpose(F[use][0:NE1, j * P:(j + 1) * P], share[:, j, :], ident[:, :])
                last.then_inc(F.ready(use), 1)
            elif name == "expert":
                if isinstance(s, int) and s == 0 and i == 0:
                    pe.wait_ge(low, len(pieces))
                for n, first in (("g", GW), ("u", UW)):
                    use = (n, i)
                    F.claim(pe, s, use)
                    for m in range(2 * i, min(2 * i + 2, M1)):
                        for q in range(Q):
                            w = slice(first + q * EI + m * P, first + q * EI + (m + 1) * P)
                            last = matmul_split(pe, F[use][:, (m % 2) * ROUND:(m % 2 + 1) * ROUND],
                                                (wh[:, w], wl[:, w]), (hs[:, 0, q, :], hs[:, 1, q, :]),
                                                q == 0, q == Q - 1)
                    last.then_inc(F.ready(use), 1)
                use = ("w", i)
                F.read(pe, s, ("spread", 0))
                F.claim(pe, s, use)
                for m in range(2 * i, min(2 * i + 2, M1)):
                    last = mm(F[use][:, (m % 2) * ROUND:(m % 2 + 1) * ROUND], spread[:, m * P:(m + 1) * P], wT[:, :],
                              start=True, stop=True)
                last.then_inc(F.ready(use), 1)
            elif name == "down":
                use = ("down", i)
                F.claim(pe, s, use)
                for m in range(M1):
                    if m % 2 == 0:
                        after(pe, e_low, s, m // 2 + 1)
                    w = slice(DW + m * D, DW + (m + 1) * D)
                    last = matmul_split(pe, F[use], (gs[:, 0, m, r], gs[:, 1, m, r]), (wh[:, w], wl[:, w]),
                                        m == 0, m == M1 - 1)
                last.then_inc(F.ready(use), 1)

        go(step, pe)


_TENSORS = ["x", "embT", "cond_w0", "cond_w1", "cond_w2", "cond_b01", "cond_b2", "cond_wk", "cond_bk", "cwT", "side",
            "expert", "bqkv0", "wo0", "bo0", "fc1T", "gamma", "beta", "mask0", "vmask0", "vsel", "qkv0", "conv",
            "gate0", "up", "down", "fc2", "bits", "gate1", "g1", "u1", "d1", "ln_w", "ln_b", "spread", "rope_cos",
            "rope_sin", "kmask", "vmask"]


def program(nc, t, out):
    scratch_mix = nc.dram_tensor("scratch_mix", (CONDS, TILES, P, 2, P), F32, kind="Internal").ap()
    scratch = {
        "mix": [scratch_mix[c] for c in range(CONDS)],
        "mix_t": [scratch_mix[c].rearrange("t p h n -> (t p) h n") for c in range(CONDS)],
        "ternary": nc.dram_tensor("scratch_ternary", (P, Q, 2 * D + 2 * P), BF16, kind="Internal").ap(),
        "rows": [nc.dram_tensor(f"scratch_rows{c}", (2 * C, TOKENS), F32, kind="Internal").ap()
                 for c in range(CONDS + 1)],
        "x2": nc.dram_tensor("scratch_x2", (TOKENS, D), F32, kind="Internal").ap(),
    }
    with ExitStack() as ctx:
        def sem(name):
            return ctx.enter_context(nc.semaphore(name))

        def tensors(scope):
            return lambda name, shape, dtype: scope.enter_context(nc.sbuf_tensor(name, shape, dtype))

        sb = tensors(ctx)
        psum = ctx.enter_context(nc.psum_tensor("psum", [P, 8, 512], F32))
        weights = (sb("w_high", [P, WCOLS], F32R), sb("w_low", [P, WCOLS], F32R), sb("stage", [P, 2, STAGE], F32))
        consts = {
            "ident": sb("ident", [P, P], F32),
            "ones": sb("ones", [P, D], F32R),
            "gate1": [sb(f"gate1_{n}", [P, Q * NE1], F32R) for n in ("high", "low")],
            "dequant": sb("dequant", [P, 4], F32),
            "minus_half": sb("minus_half", [P, 1], F32),
            "vsel": sb("vsel", [P, BT, P], F32),
            "mix_high": sem("prep_mix_high"), "mix_low": sem("prep_mix_low"), "rows_low": sem("prep_rows_low"),
        }
        with ExitStack() as layer:
            sb0 = tensors(layer)
            consts.update({
                "qkv_h": sb0("qkv_high", [P, Q * 192], F32R), "qkv_l": sb0("qkv_low", [P, Q * 192], F32R),
                "bqkv": sb0("bqkv", [2 * C, 192], F32R),
                "out_w": sb0("out_w", [P, 2, D], F32R),
                "out_b": sb0("out_b", [P, NT, P], F32R),
                "halo": [sb0(f"x1_phase{i}", [P, BT, P + 2], F32) for i in range(NT)],
                "gamma": sb0("gamma", [P, D], F32), "beta": sb0("beta", [P, D], F32),
                "mask0": sb0("mask0", [H0 * E0, H0], F32), "vmask0": sb0("vmask0", [P, 4], F32),
            })
            with ExitStack() as scope:
                prepare(nc, scope, t, tensors(scope), sem, scratch, psum, consts, weights)
            with ExitStack() as scope:
                layer0(nc, scope, t, tensors(scope), sem, scratch, psum, consts, weights)
        with ExitStack() as scope:
            layer1(nc, scope, t, tensors(scope), sem, scratch, psum, consts, weights, out)


def _layouts(a):
    n = {k: np.ascontiguousarray(v) for k, v in a.items()}
    zero = np.zeros

    def rows(w):
        return np.ascontiguousarray(w.reshape(P, Q, -1).transpose(1, 0, 2).reshape(D, -1))

    def cols(w):
        w = w.reshape(-1, D)
        return np.ascontiguousarray(w.reshape(-1, P, Q).transpose(0, 2, 1).reshape(-1, D))

    conds = ["L0_cond", "L1_cond", "L1_cond2"]
    stack = lambda f: np.concatenate([np.ascontiguousarray(f(n, c)) for c in conds], axis=0)
    t = {
        "x": cols(n["x"]),
        "embT": np.ascontiguousarray(n["cond_128"].T),
        "cond_w0": stack(lambda n, c: n[c + "_W0"]),
        "cond_w1": stack(lambda n, c: n[c + "_W1"]),
        "cond_w2": stack(lambda n, c: n[c + "_W2"]),
        "cond_b01": stack(lambda n, c: np.stack([n[c + "_b0"], n[c + "_b1"]], axis=1)),
        "cond_b2": stack(lambda n, c: n[c + "_b2"][None]),
        "cond_wk": stack(lambda n, c: np.repeat(n[c + "_weight"][:, :, None, :, 0], BT, axis=2)),
        "cond_bk": stack(lambda n, c: n[c + "_bias_k"]),
        "cwT": np.ascontiguousarray(n["L0_cond2_c_weight"].T),
        "side": n["fside_S_0"][None],
        "expert": n["L0_ffn_expert_w"],
    }
    wqk, bqk = n["L0_attn_Wqk_w"], n["L0_attn_Wqk_b"]
    t["qkv0"] = rows(np.concatenate([wqk[0::2], wqk[1::2], n["L0_attn_Wv_w"]], axis=0).T)
    t["bqkv0"] = np.concatenate([bqk[0::2], bqk[1::2], n["L0_attn_Wv_b"]])[None]
    t["wo0"] = cols(np.ascontiguousarray(n["L0_attn_Wo_w"].T))
    t["bo0"] = cols(n["L0_attn_Wo_b"])
    t["fc1T"] = np.ascontiguousarray(rows(n["L0_ffn_fc1_w"]).T)
    t["gamma"], t["beta"] = cols(n["L0_ffn_ln_gamma"]), cols(n["L0_ffn_ln_beta"])
    w = n["L0_cond2_weight"]
    per = C // GROUPS
    conv = zero((3, Q, C, Q, C), np.float32)
    for shift in range(3):
        for p in range(Q):
            for q in range(Q):
                tap = 4 * shift + p - q
                if 0 <= tap < TAPS:
                    for g in range(GROUPS):
                        r = slice(g * per, (g + 1) * per)
                        conv[shift, p, r, q, r] = w[r, :, tap].T
    t["conv"] = conv.reshape(3 * P, P)
    t["gate0"] = rows(n["L0_ffn_gate_w"])
    t["up"] = rows(n["L0_ffn_up_w"])
    t["down"] = cols(n["L0_ffn_down_w"])
    t["fc2"] = cols(n["L0_ffn_fc2_w"])
    t["mask0"] = np.repeat(np.eye(H0, dtype=np.float32), E0, axis=0)
    t["vmask0"] = np.repeat(np.eye(4, dtype=np.float32), C, axis=0) * np.float32((H0 * E0) ** -0.5)
    def heads(w):
        return w.reshape(KV, REP, HD, -1).transpose(1, 0, 2, 3).reshape(D, -1)

    qkv = np.concatenate([heads(n["L1_attn_Wq"]), n["L1_attn_Wk"], n["L1_attn_Wv"]], axis=0)
    wo = heads(np.ascontiguousarray(n["L1_attn_Wo"].T))
    t["bits"] = np.concatenate([rows(np.ascontiguousarray(qkv.T)), cols(wo)], axis=1)
    t["gate1"] = rows(np.ascontiguousarray(n["L1_ffn_gate_w"].T))
    t["g1"] = rows(np.ascontiguousarray(n["L1_ffn_g"].T))
    t["u1"] = rows(np.ascontiguousarray(n["L1_ffn_u"].T))
    t["d1"] = cols(np.ascontiguousarray(n["L1_ffn_d"].T))
    t["ln_w"], t["ln_b"] = cols(n["L1_attn_ln_w"]), cols(n["L1_attn_ln_b"])
    spread = zero((2 * C, EI), np.float32)
    for e in range(NE1):
        spread[[e, C + e], e * INTER:(e + 1) * INTER] = 1.0
    t["spread"] = spread
    inv = (1.0 / np.float32(10000.0) ** (np.arange(0, HD, 2, dtype=np.float32) / np.float32(HD))).astype(np.float32)
    angle = np.tile(np.arange(C, dtype=np.float32)[:, None] * inv[None, :], (BT, 2))
    t["rope_cos"] = np.cos(angle).astype(np.float32)
    t["rope_sin"] = (np.sin(angle) * np.repeat([-1.0, 1.0], HD // 2)).astype(np.float32)
    t["kmask"] = np.repeat(np.eye(KV, dtype=np.float32), HD, axis=0)
    t["vmask"] = np.repeat(np.eye(4, dtype=np.float32), C, axis=0)
    sel = zero((BT, C, BT, 4, C), np.float32)
    for b in range(BT):
        for k in range(4):
            sel[b, :, b, k, :] = np.eye(C, dtype=np.float32)
    t["vsel"] = sel.reshape(P, BT, P)
    return t


def kernel(**inputs):
    import concourse.bacc as _bacc
    from concourse import mybir as _mybir
    from concourse.bass_utils import run_bass_kernel_spmd as _run

    nc = _bacc.Bacc("TRN2", target_bir_lowering=False, num_devices=1, dynamic_dma_scratch_size=1024)
    laid = _layouts({k: np.asarray(v) for k, v in inputs.items()})
    arrays, t = {}, {}
    for name in _TENSORS:
        a = np.ascontiguousarray(laid[name])
        arrays["in_" + name] = a
        t[name] = nc.dram_tensor("in_" + name, a.shape, _mybir.dt.from_np(a.dtype), kind="ExternalInput").ap()
    out = nc.dram_tensor("out_dram", (TOKENS, D), F32, kind="ExternalOutput").ap()
    program(nc, t, out)
    r = _run(nc, [arrays], core_ids=[0])
    got = r.results[0]["out_dram"]
    return np.ascontiguousarray(got.reshape(B, C, Q, P).transpose(0, 1, 3, 2)).reshape(B, C, D)
```

```python
from contextlib import ExitStack

import numpy as np

import concourse.bass as bass
from concourse import mybir

ALU = mybir.AluOpType
ACT = mybir.ActivationFunctionType
AX_X = mybir.AxisListType.X
F32 = mybir.dt.float32
F32R = mybir.dt.float32r
BF16 = mybir.dt.bfloat16

P = 128
B, C, D = 64, 32, 512
TOKENS = B * C
NT = 2
ROUND = NT * P
ROUNDS = TOKENS // ROUND
TILES = TOKENS // P
BT = P // C
Q = D // P
KE = 8
CONDS = 3
H0, E0 = 8, 8
TAPS, GROUPS = 9, 4
INT, LAT, NE0 = 1024, 256, 8
KV, REP, HD = 8, 4, 16
NE1, INTER = 16, 56
EI = NE1 * INTER
M1 = EI // P
EPS = 1e-5
QB = 127.0
ROUND_MAGIC = 1.5 * 2.0**23
FAR = 3.0e38

UP, DOWN, LATENT, FC2 = 0, Q * INT, Q * INT + 8 * D, Q * INT + 8 * D + Q * LAT
CONV = FC2 + 2 * D
GATE0 = CONV + 3 * P
GW, UW, DW = 0, Q * EI, 2 * Q * EI
WCOLS = max(GATE0 + Q * NE0, DW + M1 * D)
STAGE = 1024


class Signal:

    def __init__(self, sem, per_round, unit=1):
        self.sem, self.per_round, self.unit = sem, per_round, unit

    def nth(self, s, n):
        return (s * self.per_round + n) * self.unit


class Link:

    def __init__(self, sem, order, name):
        self.sem, self.order, self.name = sem, order, name

    def nth(self, s, n):
        return s * len(self.order) + self.order.index((self.name, n)) + 1


def chain(sem, names, groups, each=1):
    order = []
    for g in range(groups):
        for entry in names.split():
            order += [(name, g * each + k + 1) for k in range(each) for name in entry.split(",")]
    return [Link(sem, order, name) for name in names.replace(",", " ").split()]


def after(engine, signal, s, n):
    value = signal.nth(s, n)
    if isinstance(value, int) and value <= 0:
        return
    engine.wait_ge(signal.sem, value)


class Banks:

    def __init__(self, psum, first, count, uses, ready, free, held):
        self.held = held
        self.psum, self.ready_sem, self.free_sem = psum, ready, free
        self.bank, self.turn, self.turns = {}, {}, [0] * count
        for k, use in enumerate(uses):
            self.turns[k % count] += 1
            self.bank[use], self.turn[use] = k % count, self.turns[k % count]
        self.first = first

    def __getitem__(self, use):
        return self.psum[:, self.first + self.bank[use], :]

    def claim(self, pe, s, use):
        b = self.bank[use]
        value = s * self.turns[b] + self.turn[use] - 1
        if not (isinstance(value, int) and value <= 0):
            pe.wait_ge(self.free_sem[b], value)

    def ready(self, use):
        return self.ready_sem[self.bank[use]]

    def filled(self, engine, s, use):
        b = self.bank[use]
        engine.wait_ge(self.ready_sem[b], s * self.turns[b] + self.turn[use])

    def read(self, engine, s, *uses, claim=None):
        waited = []
        for use in uses:
            b = self.bank[use]
            value = s * self.turns[b] + self.turn[use]
            if not (isinstance(value, int) and value <= 0):
                if b in waited:
                    engine.sem_inc(self.held, 1)
                waited.append(b)
                engine.wait_ge(self.free_sem[b], value)
        if claim is not None:
            if self.bank[claim] in waited:
                engine.sem_inc(self.held, 1)
            self.claim(engine, s, claim)

    def free(self, use):
        return self.free_sem[self.bank[use]]


def f32(ap):
    return ap.bitcast(F32)


def matmul_split(pe, out, lhs, rhs, start, stop):
    pe.matmul(out, lhs[0], rhs[0], start=start, stop=False)
    pe.matmul(out, lhs[0], rhs[1], start=False, stop=False)
    return pe.matmul(out, lhs[1], rhs[0], start=False, stop=stop)


def stage_pieces(sources):
    pieces = []
    for first, src, chunks, width in sources:
        per = max(1, STAGE // width)
        for c0 in range(0, chunks, per):
            pieces.append((first + c0 * width, src, c0, min(per, chunks - c0), width))
    return pieces


class Staging:

    def __init__(self, sem, name, pieces, buffers, wh, wl, steps=1, first=0, last=1):
        self.pieces, self.buffers, self.wh, self.wl = pieces, buffers, wh, wl
        self.arrived = [sem(f"{name}_arrived{i}") for i in range(len(buffers))]
        self.high, self.low = sem(name + "_high"), [sem(f"{name}_low{i}") for i in range(2)]
        due = [min(max(n + 1 - first, 0), last - first) * len(pieces) // (last - first) for n in range(-1, steps)]
        self.after_step = [range(a, b) for a, b in zip(due, due[1:])]

    def lows(self, engine, count):
        for i in range(2):
            if (count + 1 - i) // 2:
                engine.wait_ge(self.low[i], (count + 1 - i) // 2)

    def load(self, sp, k):
        _, src, c0, n, width = self.pieces[k]
        b = k % len(self.buffers)
        if k >= len(self.buffers):
            sp.wait_ge(self.low[(k - len(self.buffers)) % 2], (k - len(self.buffers)) // 2 + 1)
        sp.dma_start(self.buffers[b][:, 0:n * width].rearrange("p (c n) -> p c n", c=n),
                     src[c0 * P:(c0 + n) * P, :].rearrange("(c p) n -> p c n", p=P)).then_inc(self.arrived[b], 16)

    def cut(self, k):
        first, _, _, n, width = self.pieces[k]
        b, w = k % len(self.buffers), slice(first, first + n * width)
        return self.buffers[b][:, 0:n * width], self.wh[:, w], self.wl[:, w]

    def split_high(self, nc, act, k):
        src, high, _ = self.cut(k)
        act.wait_ge(self.arrived[k % len(self.buffers)], 16 * (k // len(self.buffers) + 1))
        nc.scalar.activation(high, src, ACT.Copy).then_inc(self.high, 1)

    def split_low(self, nc_engine, engine, k):
        src, high, low = self.cut(k)
        engine.wait_ge(self.high, k + 1)
        nc_engine.tensor_tensor(low, src, f32(high), ALU.subtract).then_inc(self.low[k % 2], 1)


def prepare(nc, ctx, t, sb, sem, scratch, psum, consts, weights):
    wh, wl, stage = weights
    ident, ones = consts["ident"], consts["ones"]
    embT = sb("embT", [P, B], F32)
    w0 = sb("cond_w0", [P, CONDS, P], F32)
    w1 = sb("cond_w1", [P, CONDS, P], F32)
    w2 = sb("cond_w2", [P, CONDS, KE], F32)
    b01 = sb("cond_b01", [P, CONDS, 2], F32)
    b2 = sb("cond_b2", [B, CONDS, KE], F32)
    wk = sb("cond_wk", [KE, CONDS, C * C], F32)
    bk = sb("cond_bk", [KE, CONDS, C], F32)
    g1 = sb("cond_g1", [P, CONDS, B], F32)
    g2 = sb("cond_g2", [P, CONDS, B], F32)
    att = sb("att", [B, CONDS, KE], F32)
    att_max = sb("att_max", [B, CONDS], F32)
    att_sum = sb("att_sum", [B, CONDS], F32)
    attT = sb("attT", [KE, CONDS, B], F32)
    mixed = sb("mixed_kernels", [B, CONDS, C, 2, C], F32R)
    bias = sb("mixed_bias", [B, CONDS, 2, C], F32R)
    cwT = sb("cwT", [P, P], F32)
    side = sb("side", [P, 1], F32)
    context = sb("context_all", [P, B], F32)
    small = sb("small_stage", [P, D], F32)
    bqk_stage = sb("bqk_stage", [2 * C, 192], F32)
    fc1T = sb("fc1T", [P, 2, D], F32)
    ew = sb("ew", [P, 2, LAT], F32)
    ones32 = sb("ones32", [P, D], F32)
    wbit = sb("bit_stage", [P, Q, 3 * P + 2 * D - P], F32)
    tern = sb("ternary_out", [P, Q, 3 * P + 2 * D - P], BF16)
    wsum, wscale = sb("weight_sum", [P, 4], F32), sb("weight_scale", [P, 4], F32)
    minus_magic = sb("minus_magic", [P, 1], F32)
    qkv_stage = sb("qkv_stage", [P, Q * 192], F32)
    conv_stage = sb("conv_stage", [P, 3 * P], F32)
    gate_stage = [sb(f"gate_stage{i}", [P, Q * n], F32) for i, n in enumerate((NE0, NE1))]
    MATRICES = ((0, D), (D, P), (D + P, P), (D + 2 * P, D))

    first_in, cond_in = sem("prep_first_in"), sem("prep_cond_in")
    kernels_in = sem("prep_kernels_in")
    bits_in = sem("prep_bits_in")
    rows_in = sem("prep_rows_in")
    latent_in = sem("prep_latent_in")
    weights_in = sem("prep_weights_in")
    tables_in = sem("prep_tables_in")
    zeroed, consts_made = sem("prep_zeroed"), sem("prep_consts")
    hidden = sem("prep_hidden")
    gelu = sem("prep_gelu")
    logits_out, below, exped, shared = (sem("prep_" + n) for n in ("logits", "below", "exp", "shares"))
    turned, attT_out = sem("prep_turned"), sem("prep_attT")
    agg, agg_high, agg_low = sem("prep_agg"), sem("prep_agg_high"), sem("prep_agg_low")
    bias_ready, bias_high, bias_low = sem("prep_bias"), sem("prep_bias_high"), sem("prep_bias_low")
    context_ready, context_out = sem("prep_context"), sem("prep_context_out")
    magnitudes, totals = sem("prep_magnitudes"), sem("prep_totals")
    bits_rounded = sem("prep_bits_rounded")
    bits_out, latent_ready, latent_high = sem("prep_bits_out"), sem("prep_latent"), sem("prep_latent_high")
    high, low = sem("prep_high"), sem("prep_low")
    step_done = sem("prep_step_done")
    stored = [sem(f"prep_stored{i}") for i in range(2)]

    smalls = [(qkv_stage, t["qkv0"], consts["qkv_h"][:, :], consts["qkv_l"][:, :]),
              (conv_stage, t["conv"], wh[:, CONV:CONV + 3 * P], wl[:, CONV:CONV + 3 * P]),
              (gate_stage[0], t["gate0"], wh[:, GATE0:GATE0 + Q * NE0], wl[:, GATE0:GATE0 + Q * NE0]),
              (gate_stage[1], t["gate1"], consts["gate1"][0][:, :], consts["gate1"][1][:, :])]

    spare = sb("spare_stage", [P, 2, STAGE], F32)
    up = Staging(sem, "prep_up", stage_pieces(((UP, t["up"], Q, INT),)),
                 [stage[:, 0, :], stage[:, 1, :], spare[:, 0, :], spare[:, 1, :]], wh, wl)

    AGG = (4, 6, 0)
    LATENT_BANK, BIAS_BANK, CONTEXT_BANK = 4, 2, 3

    block = ctx.enter_context(nc.Block())

    @block.sync
    def _(sp):
        for dst, src in ((embT[:, :], t["embT"]), (w0[:, :, :], t["cond_w0"].rearrange("(c p) n -> p c n", p=P)),
                         (b01[:, :, :], t["cond_b01"].rearrange("(c p) n -> p c n", p=P))):
            sp.dma_start(dst, src).then_inc(first_in, 16)
        for dst, src in ((w1[:, :, :], t["cond_w1"].rearrange("(c p) n -> p c n", p=P)),
                         (w2[:, :, :], t["cond_w2"].rearrange("(c p) n -> p c n", p=P)),
                         (b2[:, :, :], t["cond_b2"].rearrange("(a c) n -> a c n", a=1).broadcast_to([B, CONDS, KE]))):
            sp.dma_start(dst, src).then_inc(cond_in, 16)
        sp.dma_start(wbit[:, :, :], t["bits"].rearrange("(c p) n -> p c n", p=P)).then_inc(bits_in, 16)
        sp.wait_ge(zeroed, 2)
        for r in (0, 32):
            sp.dma_start(bqk_stage[r:r + 1, :], t["bqkv0"]).then_inc(rows_in, 16)
        sp.dma_start(small[0:64, :], t["wo0"]).then_inc(rows_in, 16)
        for r in (64, 96):
            sp.dma_start(small[r:r + 1, :], t["bo0"]).then_inc(rows_in, 16)
        for buf, src, _, _ in smalls:
            n = src.shape[0] // P
            sp.dma_start(buf[:, :].rearrange("p (c n) -> p c n", c=n), src.rearrange("(c p) n -> p c n", p=P))\
                .then_inc(weights_in, 16)
        for dst, src in ((consts["gamma"][:, :], t["gamma"].broadcast_to([P, D])),
                         (consts["beta"][:, :], t["beta"].broadcast_to([P, D])),
                         (consts["mask0"][:, :], t["mask0"]), (consts["vmask0"][:, :], t["vmask0"]),
                         (consts["vsel"][:, :, :], t["vsel"]),
                         (consts["lnw"][:, :], t["ln_w"].broadcast_to([P, D])),
                         (consts["lnb"][:, :], t["ln_b"].broadcast_to([P, D])),
                         (consts["cosw"][:, :], t["rope_cos"]), (consts["sinw"][:, :], t["rope_sin"]),
                         (consts["kmask1"][:, :], t["kmask"]), (consts["vmask1"][:, :], t["vmask"])):
            sp.dma_start(dst, src).then_inc(tables_in, 16)
        for k in range(len(up.pieces)):
            up.load(sp, k)
        for c in range(CONDS):
            sp.wait_ge(agg_low, c + 1)
            for r in range(BT):
                sp.dma_start(scratch["mix"][c, r].rearrange("i t n -> t i n"),
                              f32(mixed[r:B:BT, c, :, :, :]).rearrange("t i h o -> t i (h o)")).then_inc(stored[0], 16)
        sp.wait_ge(bias_low, 1)
        sp.dma_start(scratch["rows"].rearrange("c (b o) -> b c o", b=B),
                      f32(bias[:, :, :, :]).rearrange("b c h o -> b (c h) o")).then_inc(stored[0], 16)
        sp.wait_ge(stored[0], 16 * (CONDS * BT + 1))
        sp.wait_ge(tables_in, 16 * 11)

    @block.gpsimd
    def _(pool):
        nc.gpsimd.memset(small[:, :], 0.0).then_inc(zeroed, 1)
        nc.gpsimd.memset(bqk_stage[:, :], 0.0).then_inc(zeroed, 1)
        nc.gpsimd.memset(ident[:, :], 0.0).then_inc(zeroed, 1)
        nc.gpsimd.memset(ones32[:, :], 1.0).then_inc(consts_made, 1)
        pool.wait_ge(zeroed, 3)
        nc.gpsimd.affine_select(out=ident[:, :], in_=ident[:, :], compare_op=ALU.not_equal, fill=1.0, base=0,
                                pattern=[[-1, P]], channel_multiplier=1).then_inc(consts_made, 1)
        nc.gpsimd.memset(minus_magic[:, :], -ROUND_MAGIC).then_inc(consts_made, 1)
        nc.gpsimd.memset(consts["halo"][:, :, :], 0.0)
        nc.gpsimd.memset(f32(consts["out_b"][:, :, :]), 1.0)
        nc.gpsimd.memset(consts["minus_half"][:, :], -0.5)
        for k, (buf, _, hi, lo) in enumerate(smalls):
            pool.wait_ge(high, k + 1)
            nc.gpsimd.tensor_tensor(lo, buf[:, :], f32(hi), ALU.subtract).then_inc(low, 1)
        for k in range(0, len(up.pieces), 2):
            up.split_low(nc.gpsimd, pool, k)
        pool.wait_ge(low, len(smalls))

    @block.scalar
    def _(act):
        for dst, src in ((wk[:, :, :], t["cond_wk"].rearrange("(c k) n -> k c n", k=KE)),
                         (bk[:, :, :], t["cond_bk"].rearrange("(c k) o -> k c o", k=KE)),
                         (cwT[:, :], t["cwT"]), (side[:, :], t["side"])):
            act.dma_start(dst, src).then_inc(kernels_in, 16)
        for dst, src in ((fc1T[:, :, :], t["fc1T"].rearrange("(c p) n -> p c n", p=P)),
                         (ew[:, :, :], t["expert"].rearrange("(c p) n -> p c n", p=P))):
            act.dma_start(dst, src).then_inc(latent_in, 16)
        act.wait_ge(first_in, 16 * 3)
        for layer, g in ((0, g1), (1, g2)):
            act.wait_ge(hidden, CONDS * (layer + 1))
            for c in range(CONDS):
                nc.scalar.activation(g[:, c, :], psum[:, layer, c * B:(c + 1) * B], ACT.Gelu,
                                     bias=b01[:, c, layer:layer + 1]).then_inc(gelu, 1)
        act.wait_ge(below, 1)
        nc.scalar.activation(att[:, :, :], att[:, :, :], ACT.Exp).then_inc(exped, 1)
        act.wait_ge(turned, 1)
        nc.scalar.activation(attT[:, :, :], psum[0:KE, 3, 0:CONDS * B].rearrange("k (c b) -> k c b", c=CONDS),
                             ACT.Copy).then_inc(attT_out, 1)
        act.wait_ge(bias_ready, 1)
        nc.scalar.activation(bias[:, :, 0, :], psum[0:B, BIAS_BANK, 0:CONDS * C].rearrange("b (c o) -> b c o", c=CONDS),
                             ACT.Copy).then_inc(bias_high, 1)
        act.wait_ge(context_ready, 1)
        nc.scalar.activation(context[:, :], psum[:, CONTEXT_BANK, 0:B], ACT.Identity, bias=side[:, 0:1])\
            .then_inc(context_out, 1)
        act.wait_ge(context_out, 1)
        act.dma_start(scratch["context"], context[:, :]).then_inc(stored[1], 16)
        for k, (buf, _, hi, _) in enumerate(smalls):
            act.wait_ge(weights_in, 16 * len(smalls))
            nc.scalar.activation(hi, buf[:, :], ACT.Copy).then_inc(high, 1)
        act.wait_ge(rows_in, 16 * 5)
        out_w = consts["out_w"]
        for dst, src in ((out_w[0:64, 0, :], small[0:64, :]), (out_w[64:128, 0, :], small[0:64, :]),
                         (out_w[64:128, 1, :], small[64:128, :]), (consts["bqkv"][:, :], bqk_stage[:, :])):
            last = nc.scalar.activation(dst, src, ACT.Copy)
        last.then_inc(high, 1)
        act.wait_ge(consts_made, 3)
        nc.scalar.activation(ones[:, :], ones32[:, :], ACT.Copy)
        for c in range(CONDS):
            act.wait_ge(agg, c + 1)
            nc.scalar.activation(mixed[:, c, :, 0, :],
                                 psum[0:B, AGG[c]:AGG[c] + 2, :].rearrange("b k (i o) -> b (k i) o", o=C), ACT.Copy)\
                .then_inc(agg_high, 1)
        for k in range(len(up.pieces)):
            up.split_high(nc, act, k)
        act.wait_ge(latent_ready, 1)
        nc.scalar.activation(wh[:, LATENT:LATENT + 2 * D].rearrange("p (k n) -> p k n", k=2),
                             psum[:, LATENT_BANK:LATENT_BANK + 2, :], ACT.Copy).then_inc(latent_high, 1)
        for k, (first, n) in enumerate(MATRICES[:-1]):
            act.wait_ge(bits_rounded, k + 1)
            nc.scalar.activation(tern[:, :, first:first + n], wbit[:, :, first:first + n], ACT.Identity,
                                 bias=minus_magic[:, 0:1]).then_inc(bits_out, 1)
        act.wait_ge(bits_out, len(MATRICES))
        act.dma_start(scratch["ternary"], tern[:, :, :]).then_inc(stored[1], 16)
        act.wait_ge(stored[1], 16 * 2)

    @block.vector
    def _(dve):
        count = [0]

        def done(instruction):
            count[0] += 1
            instruction.then_inc(step_done, 1)
            dve.wait_ge(step_done, count[0])

        dve.wait_ge(logits_out, 1)
        dve.wait_ge(cond_in, 16 * 3)
        logits = psum[0:B, 2, 0:CONDS * KE].rearrange("b (c k) -> b c k", c=CONDS)
        done(nc.vector.tensor_tensor(att[:, :, :], logits, b2[:, :, :], ALU.add))
        done(nc.vector.tensor_reduce(att_max[:, :], att[:, :, :], AX_X, ALU.max))
        nc.vector.tensor_tensor(att[:, :, :], att[:, :, :], att_max[:, :].unsqueeze(2).broadcast_to([B, CONDS, KE]),
                                ALU.subtract).then_inc(below, 1)
        dve.wait_ge(exped, 1)
        done(nc.vector.tensor_reduce(att_sum[:, :], att[:, :, :], AX_X, ALU.add))
        done(nc.vector.reciprocal(att_sum[:, :], att_sum[:, :]))
        nc.vector.tensor_tensor(att[:, :, :], att[:, :, :], att_sum[:, :].unsqueeze(2).broadcast_to([B, CONDS, KE]),
                                ALU.mult).then_inc(shared, 1)
        dve.wait_ge(bits_in, 16)
        for k, (first, n) in enumerate(MATRICES):
            last = nc.vector.tensor_reduce(wsum[:, k:k + 1], wbit[:, :, first:first + n], mybir.AxisListType.XY,
                                           ALU.add, apply_absolute_value=True)
        last.then_inc(magnitudes, 1)
        dve.wait_ge(bias_high, 1)
        nc.vector.tensor_tensor(bias[:, :, 1, :],
                                psum[0:B, BIAS_BANK, 0:CONDS * C].rearrange("b (c o) -> b c o", c=CONDS),
                                f32(bias[:, :, 0, :]), ALU.subtract).then_inc(bias_low, 1)

        out_w, bqkv = consts["out_w"], consts["bqkv"]
        dve.wait_ge(high, len(smalls) + 1)
        nc.vector.tensor_tensor(out_w[0:64, 1, :], small[0:64, :], f32(out_w[0:64, 0, :]), ALU.subtract)
        nc.vector.tensor_tensor(out_w[96:128, 1, :], small[96:128, :], f32(out_w[96:128, 1, :]), ALU.subtract)
        nc.vector.tensor_tensor(bqkv[32:64, :], bqk_stage[32:64, :], f32(bqkv[32:64, :]), ALU.subtract)

        def low_kernels(c):
            dve.wait_ge(agg_high, c + 1)
            nc.vector.tensor_tensor(mixed[:, c, :, 1, :],
                                    psum[0:B, AGG[c]:AGG[c] + 2, :].rearrange("b k (i o) -> b (k i) o", o=C),
                                    f32(mixed[:, c, :, 0, :]), ALU.subtract).then_inc(agg_low, 1)

        for c in range(CONDS):
            low_kernels(c)
        dve.wait_ge(totals, 1)
        dequant = consts["dequant"]
        for k, (first, n) in enumerate(MATRICES):
            last = nc.vector.tensor_scalar(dequant[:, k:k + 1], psum[:, 3, k:k + 1], 1.0 / (D * n), 1e-5,
                                           ALU.mult, ALU.max)
        done(last)
        done(nc.vector.reciprocal(wscale[:, :], dequant[:, :]))
        nc.vector.tensor_scalar(dequant[:, :], dequant[:, :], 1.0 / QB, None, ALU.mult)
        for k, (first, n) in enumerate(MATRICES):
            w = wbit[:, :, first:first + n]
            last = nc.vector.tensor_scalar(w, w, wscale[:, k:k + 1], 1.0, ALU.mult, ALU.min)
        done(last)
        for k, (first, n) in enumerate(MATRICES):
            w = wbit[:, :, first:first + n]
            nc.vector.tensor_scalar(w, w, -1.0, ROUND_MAGIC, ALU.max, ALU.add).then_inc(bits_rounded, 1)
        first, n = MATRICES[-1]
        dve.wait_ge(bits_rounded, len(MATRICES))
        nc.vector.tensor_scalar(tern[:, :, first:first + n], wbit[:, :, first:first + n], -ROUND_MAGIC, None, ALU.add)\
            .then_inc(bits_out, 1)
        dve.wait_ge(latent_high, 1)
        for c in range(2):
            w = slice(LATENT + c * D, LATENT + c * D + D)
            nc.vector.tensor_tensor(wl[:, w], psum[:, LATENT_BANK + c, :], f32(wh[:, w]), ALU.subtract)
        for k in range(1, len(up.pieces), 2):
            up.split_low(nc.vector, dve, k)

    @block.tensor
    def _(pe):
        pe.wait_ge(first_in, 16 * 3)
        for layer, w, rhs in ((0, w0, None), (1, w1, g1)):
            if layer:
                pe.wait_ge(cond_in, 16 * 3)
            for c in range(CONDS):
                if layer:
                    pe.wait_ge(gelu, c + 1)
                nc.tensor.matmul(psum[:, layer, c * B:(c + 1) * B], w[:, c, :], rhs[:, c, :] if layer else embT[:, :],
                                 start=True, stop=True).then_inc(hidden, 1)
        for c in range(CONDS):
            pe.wait_ge(gelu, CONDS + c + 1)
            last = nc.tensor.matmul(psum[0:B, 2, c * KE:(c + 1) * KE], g2[:, c, :], w2[:, c, :], start=True, stop=True)
        last.then_inc(logits_out, 1)
        pe.wait_ge(shared, 1)
        pe.wait_ge(consts_made, 2)
        for c in range(CONDS):
            last = nc.tensor.transpose(psum[0:KE, 3, c * B:(c + 1) * B], att[:, c, :], ident[0:B, 0:B])
        last.then_inc(turned, 1)
        pe.wait_ge(attT_out, 1)
        pe.wait_ge(kernels_in, 16 * 4)
        for c in range(CONDS):
            last = nc.tensor.matmul(psum[0:B, BIAS_BANK, c * C:(c + 1) * C], attT[:, c, :], bk[:, c, :],
                                    start=True, stop=True)
        last.then_inc(bias_ready, 1)
        nc.tensor.matmul(psum[:, CONTEXT_BANK, 0:B], cwT[:, :], embT[:, :], start=True, stop=True)\
            .then_inc(context_ready, 1)
        for c in range(CONDS):
            for k in range(2):
                last = nc.tensor.matmul(psum[0:B, AGG[c] + k, :], attT[:, c, :], wk[:, c, k * D:(k + 1) * D],
                                        start=True, stop=True)
            last.then_inc(agg, 1)
        pe.wait_ge(magnitudes, 1)
        pe.wait_ge(context_out, 1)
        nc.tensor.matmul(psum[:, 3, 0:4], ones32[:, 0:P], wsum[:, :], start=True, stop=True).then_inc(totals, 1)
        pe.wait_ge(latent_in, 16 * 2)
        pe.wait_ge(agg_low, 1)
        for c in range(Q):
            for k in range(2):
                last = nc.tensor.matmul(psum[:, LATENT_BANK + c // 2, (c % 2) * LAT:(c % 2 + 1) * LAT],
                                        fc1T[:, k, c * P:(c + 1) * P], ew[:, k, :], start=(k == 0), stop=(k == 1))
        last.then_inc(latent_ready, 1)


BODY0 = [("F", "conv", 0), ("A", "split", 0), ("F", "conv", 1), ("F", "hturn", 0), ("F", "hturn", 1),
         ("A", "split", 1), ("A", "mix", 0), ("F", "gate", 0), ("A", "mix", 1), ("F", "up", 0), ("A", "qkv", 0),
         ("F", "up", 1), ("A", "vrep", 0), ("A", "scores", 0), ("A", "scores", 1), ("F", "latent", 0),
         ("F", "square", 0), ("F", "carry", 0), ("A", "turn", 0), ("F", "up", 2), ("A", "values", 0),
         ("A", "turn", 1), ("F", "square", 1), ("F", "square", 2), ("F", "gturn", 0), ("F", "send", 0),
         ("F", "up", 3), ("A", "values", 1), ("A", "out", 0), ("F", "square", 3), ("A", "out", 1),
         ("F", "routed", 0), ("A", "phase", 0), ("F", "down", 0), ("A", "phase", 1), ("F", "routed", 1),
         ("F", "down", 1)]
ATTEND0 = [(name, i) for kind, name, i in BODY0 if kind == "A"]
FORWARD0 = [(name, i) for kind, name, i in BODY0 if kind == "F"]


def load_mix(engine, mix, rows, scratch, which, s, arrived):
    for r in range(BT):
        d = slice(C * r, C * r + C)
        engine.dma_start(mix[d, :, :, d].rearrange("p i h o -> p (i h) o"),
                         scratch["mix"][which, r, :, bass.ds(s * NT, NT), :].rearrange("p i (h o) -> p (i h) o", h=2))\
            .then_inc(arrived, 16)
    engine.dma_start(rows, scratch["rows"][2 * which:2 * which + 2, bass.ds(s * ROUND, ROUND)]).then_inc(arrived, 16)


def layer0(nc, ctx, t, sb, sem, scratch, psum, consts, weights):
    wh, wl, stage = weights
    ident, ones, mask0, vmask0 = (consts[k] for k in ("ident", "ones", "mask0", "vmask0"))
    out_w, qkv_h, qkv_l, bqkv = (consts[k] for k in ("out_w", "qkv_h", "qkv_l", "bqkv"))
    xp = consts["halo"]
    out_b = consts["out_b"]
    x = sb("x", [P, NT, D], F32)
    xs = sb("x_split", [P, NT, 2, D], F32R)
    mix = sb("mix0", [P, NT, 2, P], F32R)
    rows = sb("bias_rows0", [2, ROUND], F32R)
    context = sb("context", [P, NT, BT], F32)
    ys = sb("y_split", [P, NT, 2, Q, P], F32R)
    qT = sb("qT", [H0 * E0, NT, P], F32)
    vT = sb("vT", [H0 * E0, NT * BT, 4, C], F32)
    km = sb("k_masked", [H0 * E0, NT, BT, H0, C], F32)
    vb = sb("v_blocks", [P, NT, BT, H0 * E0], F32)
    prob = sb("prob", [P, NT, H0, C], F32)
    pmax = sb("prob_max", [P, NT, H0], F32)
    psums = sb("prob_sum", [P, NT, H0], F32)
    pT = sb("probT", [P, NT, 2, P], F32)
    out_a = sb("out_a", [P, NT, P], F32R)
    x1 = sb("x1", [P, NT, D], F32)
    xps = sb("phase_split", [P, NT, 2, BT, P + 2], F32R)
    hp = sb("h_phase", [P, NT, BT, P], F32)
    hs = sb("h_split", [P, 2, Q, ROUND], F32R)
    x1b = sb("x1_plus_beta", [P, NT, D], F32)
    logitT = sb("gate_logitsT", [NE0, ROUND], F32)
    logit8 = sb("gate_top", [P, NT, 8], F32)
    gsum = sb("gate_sum", [P, NT], F32)
    relu = sb("relu", [P, 2, 2 * ROUND], F32)
    sq = sb("squared", [P, 2, 2 * ROUND], F32)
    gs = sb("squared_split", [P, 2, INT // P, ROUND], F32R)
    fs = sb("latent_split", [P, 2, 2, ROUND], F32R)
    z, routed = stage[:, :, 0:D], stage[:, 0, D:2 * D]
    stats = sb("stats", [P, 6], F32)
    mv = sb("mean_var", [P, 2], F32)
    rstd = sb("rstd", [P, 1], F32)

    def signal(name, per_round, unit=1):
        return Signal(sem("l0_" + name), per_round, unit)

    x_in = [signal(f"x_in{i}", 1, 16) for i in range(NT)]
    mix_in, zeroed = signal("mix_in", BT + 1, 16), sem("l0_zeroed")
    context_in = signal("context_in", 1, 16)
    x_high, x_low = signal("x_high", NT), signal("x_low", NT)
    y_high = signal("y_high", NT)
    q_out, v_out = signal("q_out", 1), signal("v_out", 1)
    smax, ssum, srecip = chain(sem("l0_softmax"), "max sum recip", NT)
    expd, normed = signal("exp", NT), signal("normed", NT)
    o_high = signal("o_high", 2 * NT)
    x1_sent = [signal(f"x1_sent{i}", 1, 16) for i in range(NT)]
    xp_in = signal("xp_in", Q, 16)
    conv_out, logits_out = signal("conv_out", NT), signal("logits_out", 1)
    xp_high, xp_low = signal("xp_high", NT), signal("xp_low", NT)
    carried = signal("carried", 1)
    h_high, gsummed = signal("h_high", NT), signal("gsummed", 1)
    squared, sq_high, sq_low = (signal(n, 4) for n in ("squared", "sq_high", "sq_low"))
    f_high = signal("f_high", 1)
    stats_out, mv_out, var_out, scaled, x2_out = chain(sem("l0_norm"), "stats mv var scaled x2", NT)
    rstd_out = signal("rstd", NT)
    held = signal("held", 1)
    x2_stored = [signal(f"x2_stored{i}", 1, 16) for i in range(NT)]

    a_uses = [(name, i) for name, i in ATTEND0 if name not in ("split", "phase")]
    A = Banks(psum, 0, 4, a_uses, [sem(f"l0_a_ready{i}") for i in range(4)],
              [sem(f"l0_a_free{i}") for i in range(4)], held.sem)
    f_uses = [(name, i) for name, i in FORWARD0 if name not in ("carry", "square", "send")]
    F = Banks(psum, 4, 4, f_uses, [sem(f"l0_f_ready{i}") for i in range(4)],
              [sem(f"l0_f_free{i}") for i in range(4)], held.sem)

    buffers = [stage[:, 0, :], stage[:, 1, :], sq.rearrange("p a n -> p (a n)"), relu.rearrange("p a n -> p (a n)"),
               hp.rearrange("p i b n -> p (i b n)"), x1b.rearrange("p i n -> p (i n)")]
    staging = Staging(sem, "l0_weights", stage_pieces(((FC2, t["fc2"], 2, D), (DOWN, t["down"], INT // P, D))),
                      buffers, wh, wl, len(ATTEND0),
                      ATTEND0.index(("mix", 0)), ATTEND0.index(("values", 1)))

    def go(steps, engine, weigh=None):
        for n, (name, i) in enumerate(ATTEND0):
            steps("A", name, i, 0)
            if engine is nc.sync:
                pieces = range(len(staging.pieces)) if (name, i) == ("split", NT - 1) else ()
            else:
                pieces = staging.after_step[n]
            for k in pieces if weigh else ():
                weigh(k)
        if weigh and engine is not nc.sync:
            staging.lows(engine, len(staging.pieces))
        for kind, name, i in BODY0:
            steps(kind, name, i, 1 if kind == "A" else 0)
        with engine.Fori(2, ROUNDS) as r:
            for kind, name, i in BODY0:
                steps(kind, name, i, r if kind == "A" else r - 1)
        for name, i in FORWARD0:
            steps("F", name, i, ROUNDS - 1)

    block = ctx.enter_context(nc.Block())

    @block.sync
    def _(sp):
        def step(kind, name, i, s):
            if name == "split":
                A.read(sp, s - 1, ("out", i))
                sp.sem_inc(held.sem, 1)
                sp.dma_start(x[:, i, :], t["x"][bass.ds(s * ROUND + i * P, P), :]).then_inc(x_in[i].sem, 16)
                if i == NT - 1:
                    A.read(sp, s - 1, *[("mix", j) for j in range(NT)])
                    sp.sem_inc(held.sem, 1)
                    if isinstance(s, int) and s == 0:
                        sp.wait_ge(zeroed, 1)
                    load_mix(sp, f32(mix[:, :, :, :]), f32(rows[:, :]), scratch, 0, s, mix_in.sem)
            elif name == "out":
                A.read(sp, s, ("out", i))
                sp.sem_inc(held.sem, 1)
                sp.dma_start(scratch["x1"][bass.ds(s * ROUND + i * P, P), :], x1[:, i, :]).then_inc(x1_sent[i].sem, 16)
            elif name == "phase" and i == 0:
                after(sp, conv_out, s - 1, NT)
                sp.sem_inc(held.sem, 1)
                sp.dma_start(context[:, :, :].rearrange("p i b -> p (i b)"),
                             scratch["context"][:, bass.ds(s * NT * BT, NT * BT)]).then_inc(context_in.sem, 16)
                after(sp, xp_low, s - 1, NT)
                sp.sem_inc(held.sem, 1)
                for j in range(NT):
                    after(sp, x1_sent[j], s, 1)
                    sp.sem_inc(held.sem, 1)
                for q in range(Q):
                    sp.dma_start(xp[C * q:C * q + C, :, 1:1 + P],
                                 scratch["x1"][bass.ds(s * ROUND, ROUND), P * q:P * q + P]
                                 .rearrange("(b c) j -> c b j", c=C)).then_inc(xp_in.sem, 16)
            elif name == "down" and i == 0:
                send(s, 0)
            elif name == "send" and not (isinstance(s, int) and s == 0):
                send(s - 1, 1)

        def send(s, i):
            after(sp, x2_out, s, i + 1)
            sp.sem_inc(held.sem, 1)
            sp.dma_start(scratch["x2"][bass.ds(s * ROUND + i * P, P), :], z[:, i, :]).then_inc(x2_stored[i].sem, 16)

        go(step, sp, lambda k: staging.load(sp, k))
        send(ROUNDS - 1, 1)

    @block.scalar
    def _(act):
        copy = lambda out, in_, **k: nc.scalar.activation(out, in_, ACT.Copy, **k)

        def step(kind, name, i, s):
            if name == "split":
                after(act, x_in[i], s, 1)
                copy(xs[:, i, 0, :], x[:, i, :]).then_inc(x_high.sem, 1)
            elif name == "mix":
                A.filled(act, s, ("mix", i))
                copy(ys[:, i, 0, :, :], A[("mix", i)].rearrange("p (q n) -> p q n", q=Q)).then_inc(y_high.sem, 1)
            elif name == "qkv":
                bank = A[("qkv", 0)]
                A.filled(act, s, ("qkv", 0))
                copy(qT[:, :, :], bank[0:64, 0:ROUND].rearrange("p (i n) -> p i n", i=NT)).then_inc(q_out.sem, 1)
                copy(vT[:, :, :, :], bank[0:64, ROUND:2 * ROUND].rearrange("p (b k) -> p b k", k=C).unsqueeze(2)
                     .broadcast_to([64, NT * BT, 4, C])).then_inc(v_out.sem, 1)
            elif name == "scores":
                A.read(act, s, ("scores", i))
                nc.scalar.activation(prob[:, i, :, :], prob[:, i, :, :], ACT.Exp).then_inc(expd.sem, 1)
            elif name == "turn":
                A.filled(act, s, ("turn", i))
                copy(pT[:, i, :, :], A[("turn", i)][:, 0:2 * P].rearrange("p (h n) -> p h n", h=2))\
                    .then_inc(A.free(("turn", i)), 1)
            elif name == "values":
                A.filled(act, s, ("values", i))
                bank = A[("values", i)]
                copy(out_a[0:64, i, :], bank[0:64, 0:P]).then_inc(o_high.sem, 1)
                copy(out_b[0:64, i, :], bank[0:64, 0:P]).then_inc(o_high.sem, 1)
            elif name == "phase":
                after(act, xp_in, s, Q)
                F.read(act, s - 1, ("conv", i))
                copy(xps[:, i, 0, :, :], xp[:, i * BT:(i + 1) * BT, :]).then_inc(xp_high.sem, 1)
            elif name == "conv":
                F.filled(act, s, ("conv", i))
                after(act, context_in, s, 1)
                for b in range(BT):
                    last = nc.scalar.activation(hp[:, i, b, :], F[("conv", i)][:, b * P:(b + 1) * P], ACT.Identity,
                                                bias=context[:, i, b:b + 1])
                last.then_inc(F.free(("conv", i)), 1)
                F.read(act, s, ("conv", i))
                act.sem_inc(conv_out.sem, 1)
            elif name == "hturn":
                F.filled(act, s, ("hturn", i))
                after(act, f_high, s - 1, 1)
                copy(hs[:, 0, :, i * P:(i + 1) * P].rearrange("p q (b o) -> p b q o", b=BT),
                     F[("hturn", i)].rearrange("p (b q o) -> p b q o", b=BT, q=Q)).then_inc(h_high.sem, 1)
            elif name == "gate":
                F.filled(act, s, ("gate", 0))
                copy(logitT[:, :], F[("gate", 0)][0:NE0, 0:ROUND]).then_inc(F.free(("gate", 0)), 1)
            elif name == "up":
                F.filled(act, s, ("up", i))
                after(act, squared, s, i - 1)
                nc.scalar.activation(relu[:, i % 2, :], F[("up", i)], ACT.Relu).then_inc(F.free(("up", i)), 1)
            elif name == "square":
                after(act, squared, s, i + 1)
                if i == 0:
                    F.read(act, s - 1, ("down", NT - 1))
                copy(gs[:, 0, 2 * i:2 * i + 2, :], sq[:, i % 2, :].rearrange("p (m n) -> p m n", m=2))\
                    .then_inc(sq_high.sem, 1)
            elif name == "latent":
                F.filled(act, s, ("latent", 0))
                copy(fs[:, 0, :, :], F[("latent", 0)].rearrange("p (m n) -> p m n", m=2)).then_inc(f_high.sem, 1)
            elif name == "routed":
                F.filled(act, s, ("routed", i))
                after(act, gsummed, s, 1)
                F.read(act, s if i else s - 1, ("down", (i - 1) % NT))
                copy(routed, F[("routed", i)], scale=gsum[:, i:i + 1]).then_inc(F.free(("routed", i)), 1)

        go(step, act, lambda k: staging.split_high(nc, act, k))

    @block.gpsimd
    def _(pool):
        nc.gpsimd.memset(f32(mix[:, :, :, :]), 0.0).then_inc(zeroed, 1)

        def step(kind, name, i, s):
            if name == "split":
                after(pool, x_high, s, i + 1)
                nc.gpsimd.tensor_tensor(xs[:, i, 1, :], x[:, i, :], f32(xs[:, i, 0, :]), ALU.subtract)\
                    .then_inc(x_low.sem, 1)
            elif name == "scores":
                after(pool, srecip, s, i + 1)
                nc.gpsimd.tensor_tensor(prob[:, i, :, :], prob[:, i, :, :],
                                        psums[:, i, :].unsqueeze(2).broadcast_to([P, H0, C]), ALU.mult)\
                    .then_inc(normed.sem, 1)
            elif name == "carry":
                for j in range(NT):
                    A.read(pool, s, ("out", j))
                after(pool, x2_out, s - 1, NT)
                nc.gpsimd.tensor_tensor(x1b[:, :, :], x1[:, :, :],
                                        consts["beta"][:, :].unsqueeze(1).broadcast_to([P, NT, D]), ALU.add)\
                    .then_inc(carried.sem, 1)
            elif name == "square":
                after(pool, sq_high, s, i + 1)
                nc.gpsimd.tensor_tensor(gs[:, 1, 2 * i:2 * i + 2, :],
                                        sq[:, i % 2, :].rearrange("p (m n) -> p m n", m=2),
                                        f32(gs[:, 0, 2 * i:2 * i + 2, :]), ALU.subtract).then_inc(sq_low.sem, 1)
            elif name == "down":
                after(pool, var_out, s, i + 1)
                nc.gpsimd.tensor_tensor(rstd[:, :], mv[:, 1:2], consts["minus_half"][:, :], ALU.pow)\
                    .then_inc(rstd_out.sem, 1)

        go(step, pool, lambda k: None if k % 2 else staging.split_low(nc.gpsimd, pool, k))

    @block.vector
    def _(dve):
        def step(kind, name, i, s):
            if name == "mix":
                after(dve, y_high, s, i + 1)
                nc.vector.tensor_tensor(ys[:, i, 1, :, :], A[("mix", i)].rearrange("p (q n) -> p q n", q=Q),
                                        f32(ys[:, i, 0, :, :]), ALU.subtract).then_inc(A.free(("mix", i)), 1)
            elif name == "qkv":
                after(dve, v_out, s, 1)
                for j in range(NT):
                    last = nc.vector.tensor_tensor(
                        km[:, j, :, :, :],
                        A[("qkv", 0)][64:128, j * P:(j + 1) * P].rearrange("p (b k) -> p b k", b=BT).unsqueeze(2)
                        .broadcast_to([64, BT, H0, C]),
                        mask0[:, :].unsqueeze(1).unsqueeze(3).broadcast_to([64, BT, H0, C]), ALU.mult)
                last.then_inc(A.free(("qkv", 0)), 1)
            elif name == "vrep":
                A.filled(dve, s, ("vrep", 0))
                nc.vector.tensor_tensor(
                    vb[:, :, :, :].rearrange("p i b (g h e) -> p (i b g) h e", g=2, e=E0),
                    A[("vrep", 0)].rearrange("p (b h e) -> p b h e", h=4, e=E0),
                    vmask0[:, :].unsqueeze(1).unsqueeze(3).broadcast_to([P, 2 * NT * BT, 4, E0]), ALU.mult)\
                    .then_inc(A.free(("vrep", 0)), 1)
            elif name == "scores":
                A.filled(dve, s, ("scores", i))
                bank = A[("scores", i)][:, 0:H0 * C].rearrange("p (h k) -> p h k", h=H0)
                nc.vector.tensor_reduce(pmax[:, i, :], bank, AX_X, ALU.max).then_inc(smax.sem, 1)
                after(dve, smax, s, i + 1)
                nc.vector.tensor_tensor(prob[:, i, :, :], bank,
                                        pmax[:, i, :].unsqueeze(2).broadcast_to([P, H0, C]), ALU.subtract)\
                    .then_inc(A.free(("scores", i)), 1)
                after(dve, expd, s, i + 1)
                nc.vector.tensor_reduce(psums[:, i, :], prob[:, i, :, :], AX_X, ALU.add).then_inc(ssum.sem, 1)
                after(dve, ssum, s, i + 1)
                nc.vector.reciprocal(psums[:, i, :], psums[:, i, :]).then_inc(srecip.sem, 1)
            elif name == "values":
                after(dve, o_high, s, 2 * i + 2)
                nc.vector.tensor_tensor(out_a[64:128, i, :], A[("values", i)][0:64, 0:P], f32(out_a[0:64, i, :]),
                                        ALU.subtract).then_inc(A.free(("values", i)), 1)
            elif name == "out":
                A.filled(dve, s, ("out", i))
                after(dve, carried, s - 1, 1)
                after(dve, x1_sent[i], s - 1, 1)
                nc.vector.tensor_tensor(x1[:, i, :], A[("out", i)], x[:, i, :], ALU.add)\
                    .then_inc(A.free(("out", i)), 1)
            elif name == "phase":
                after(dve, xp_high, s, i + 1)
                nc.vector.tensor_tensor(xps[:, i, 1, :, :], xp[:, i * BT:(i + 1) * BT, :],
                                        f32(xps[:, i, 0, :, :]), ALU.subtract)\
                    .then_inc(xp_low.sem, 1)
            elif name == "hturn":
                after(dve, h_high, s, i + 1)
                nc.vector.tensor_tensor(
                    hs[:, 1, :, i * P:(i + 1) * P].rearrange("p q (b o) -> p b q o", b=BT),
                    F[("hturn", i)].rearrange("p (b q o) -> p b q o", b=BT, q=Q),
                    f32(hs[:, 0, :, i * P:(i + 1) * P]).rearrange("p q (b o) -> p b q o", b=BT), ALU.subtract)\
                    .then_inc(F.free(("hturn", i)), 1)
            elif name == "gturn":
                F.filled(dve, s, ("gturn", 0))
                F.read(dve, s - 1, ("down", NT - 1))
                dve.sem_inc(held.sem, 1)
                for j in range(NT):
                    last = nc.vector.max(logit8[:, j, :], F[("gturn", 0)][:, NE0 * j:NE0 * (j + 1)])
                last.then_inc(F.free(("gturn", 0)), 1)
                F.read(dve, s, ("gturn", 0))
                nc.vector.tensor_tensor(gsum[:, :], logit8[:, :, 0], logit8[:, :, 1], ALU.add)\
                    .then_inc(gsummed.sem, 1)
            elif name == "up":
                F.read(dve, s, ("up", i))
                after(dve, sq_low, s, i - 1)
                nc.vector.tensor_tensor(sq[:, i % 2, :], relu[:, i % 2, :], relu[:, i % 2, :], ALU.mult)\
                    .then_inc(squared.sem, 1)
            elif name == "latent":
                after(dve, f_high, s, 1)
                nc.vector.tensor_tensor(fs[:, 1, :, :], F[("latent", 0)].rearrange("p (m n) -> p m n", m=2),
                                        f32(fs[:, 0, :, :]), ALU.subtract)\
                    .then_inc(F.free(("latent", 0)), 1)
            elif name == "down":
                F.filled(dve, s, ("down", i))
                F.read(dve, s, ("routed", i))
                after(dve, x2_stored[i], s - 1, 1)
                nc.vector.tensor_tensor(z[:, i, :], F[("down", i)], routed, ALU.add)\
                    .then_inc(F.free(("down", i)), 1)
                F.read(dve, s, ("down", i))
                nc.vector.bn_stats(stats[:, :], z[:, i, :]).then_inc(stats_out.sem, 1)
                after(dve, stats_out, s, i + 1)
                dve.sem_inc(held.sem, 1)
                nc.vector.bn_aggr(mv[:, :], stats[:, :]).then_inc(mv_out.sem, 1)
                after(dve, mv_out, s, i + 1)
                nc.vector.tensor_scalar(mv[:, 1:2], mv[:, 1:2], EPS, None, ALU.add).then_inc(var_out.sem, 1)
                nc.vector.scalar_tensor_tensor(out=z[:, i, :], in0=z[:, i, :], scalar=mv[:, 0:1],
                                               in1=consts["gamma"][:, :], op0=ALU.subtract, op1=ALU.mult)\
                    .then_inc(scaled.sem, 1)
                after(dve, scaled, s, i + 1)
                after(dve, rstd_out, s, i + 1)
                after(dve, carried, s, 1)
                nc.vector.scalar_tensor_tensor(out=z[:, i, :], in0=z[:, i, :], scalar=rstd[:, :], in1=x1b[:, i, :],
                                               op0=ALU.mult, op1=ALU.add).then_inc(x2_out.sem, 1)

        go(step, dve, lambda k: staging.split_low(nc.vector, dve, k) if k % 2 else None)

    @block.tensor
    def _(pe):
        mm = nc.tensor.matmul

        def step(kind, name, i, s):
            if name == "mix":
                use = ("mix", i)
                after(pe, x_high, s, i + 1)
                after(pe, x_low, s, i + 1)
                after(pe, mix_in, s, BT + 1)
                A.claim(pe, s, use)
                bank = A[use]
                mm(bank.rearrange("p (q n) -> p q n", q=Q), ones[0:2, 0:P],
                   rows[:, i * P:(i + 1) * P].unsqueeze(1).broadcast_to([2, Q, P]), start=True, stop=False)
                for q in range(Q):
                    last = matmul_split(pe, bank[:, q * P:(q + 1) * P],
                                        (xs[:, i, 0, q * P:(q + 1) * P], xs[:, i, 1, q * P:(q + 1) * P]),
                                        (mix[:, i, 0, :], mix[:, i, 1, :]), False, q == Q - 1)
                last.then_inc(A.ready(use), 1)
            elif name == "qkv":
                use = ("qkv", 0)
                A.read(pe, s, *[("mix", j) for j in range(NT)], claim=use)
                for first, n, out in ((0, P, A[use][:, 0:ROUND]), (P, 64, A[use][0:64, ROUND:2 * ROUND])):
                    mm(out, bqkv[:, first:first + n], ones[0:2 * C, 0:ROUND], start=True, stop=False)
                    for q in range(Q):
                        w = slice(q * 192 + first, q * 192 + first + n)
                        last = matmul_split(pe, out.rearrange("p (i n) -> p i n", i=NT), (qkv_h[:, w], qkv_l[:, w]),
                                            (ys[:, :, 0, q, :], ys[:, :, 1, q, :]), False, q == Q - 1)
                last.then_inc(A.ready(use), 1)
            elif name == "vrep":
                use = ("vrep", 0)
                after(pe, v_out, s, 1)
                A.claim(pe, s, use)
                pe.sem_inc(held.sem, 1)
                for b in range(NT * BT):
                    last = nc.tensor.transpose(A[use][:, b * 64:(b + 1) * 64],
                                               vT[:, b, :, :].rearrange("p k n -> p (k n)"), ident[0:64, 0:64])
                last.then_inc(A.ready(use), 1)
            elif name == "scores":
                use = ("scores", i)
                A.read(pe, s, ("qkv", 0), claim=use)
                pe.sem_inc(held.sem, 1)
                for b in range(BT):
                    last = mm(A[use][C * b:C * b + C, 0:H0 * C], qT[:, i, C * b:C * b + C],
                              km[:, i, b, :, :].rearrange("p h k -> p (h k)"), start=True, stop=True)
                last.then_inc(A.ready(use), 1)
            elif name == "turn":
                use = ("turn", i)
                after(pe, normed, s, i + 1)
                A.claim(pe, s, use)
                for h in range(2):
                    last = nc.tensor.transpose(A[use][:, h * P:(h + 1) * P],
                                               prob[:, i, 4 * h:4 * h + 4, :].rearrange("p h k -> p (h k)"),
                                               ident[:, :])
                last.then_inc(A.ready(use), 1)
            elif name == "values":
                use = ("values", i)
                A.read(pe, s, ("turn", i), ("vrep", 0), claim=use)
                for b in range(BT):
                    for h in range(2):
                        last = mm(A[use][C * h:C * h + C, C * b:C * b + C], vb[:, i, b, C * h:C * h + C],
                                  pT[:, i, h, C * b:C * b + C], start=True, stop=True)
                last.then_inc(A.ready(use), 1)
            elif name == "out":
                use = ("out", i)
                A.read(pe, s, ("values", i), claim=use)
                mm(A[use], out_a[:, i, :], out_w[:, 0, :], start=True, stop=False)
                mm(A[use], out_b[:, i, :], out_w[:, 1, :], start=False, stop=True).then_inc(A.ready(use), 1)
            elif name == "conv":
                use = ("conv", i)
                after(pe, xp_low, s, i + 1)
                F.claim(pe, s, use)
                for shift in range(3):
                    w = slice(CONV + shift * P, CONV + (shift + 1) * P)
                    last = matmul_split(pe, F[use].rearrange("p (b j) -> p b j", b=BT), (wh[:, w], wl[:, w]),
                                        (xps[:, i, 0, :, shift:shift + P], xps[:, i, 1, :, shift:shift + P]),
                                        shift == 0, shift == 2)
                last.then_inc(F.ready(use), 1)
            elif name == "hturn":
                use = ("hturn", i)
                F.read(pe, s, ("conv", i), claim=use)
                for b in range(BT):
                    last = nc.tensor.transpose(F[use][:, b * P:(b + 1) * P], hp[:, i, b, :], ident[:, :])
                last.then_inc(F.ready(use), 1)
            elif name == "gate":
                use = ("gate", 0)
                F.read(pe, s, *[("hturn", j) for j in range(NT)], claim=use)
                for q in range(Q):
                    w = slice(GATE0 + q * NE0, GATE0 + (q + 1) * NE0)
                    last = matmul_split(pe, F[use][0:NE0, 0:ROUND], (wh[:, w], wl[:, w]),
                                        (hs[:, 0, q, :], hs[:, 1, q, :]), q == 0, q == Q - 1)
                last.then_inc(F.ready(use), 1)
            elif name == "gturn":
                use = ("gturn", 0)
                F.read(pe, s, ("gate", 0), claim=use)
                pe.sem_inc(held.sem, 1)
                for j in range(NT):
                    last = nc.tensor.transpose(F[use][:, j * NE0:(j + 1) * NE0], logitT[:, j * P:(j + 1) * P],
                                               ident[0:NE0, 0:NE0])
                last.then_inc(F.ready(use), 1)
            elif name in ("up", "latent"):
                use = (name, i)
                F.read(pe, s, *[("hturn", j) for j in range(NT)], claim=use)
                for j in range(2):
                    for q in range(Q):
                        w = UP + q * INT + (2 * i + j) * P if name == "up" else LATENT + q * LAT + j * P
                        last = matmul_split(pe, F[use][:, j * ROUND:(j + 1) * ROUND],
                                            (wh[:, w:w + P], wl[:, w:w + P]),
                                            (hs[:, 0, q, :], hs[:, 1, q, :]), q == 0, q == Q - 1)
                last.then_inc(F.ready(use), 1)
            elif name == "routed":
                use, r = ("routed", i), slice(i * P, (i + 1) * P)
                if isinstance(s, int) and s == 0 and i == 0:
                    staging.lows(pe, len(staging.pieces))
                F.read(pe, s, ("latent", 0), claim=use)
                for m in range(2):
                    w = FC2 + m * D
                    last = matmul_split(pe, F[use], (fs[:, 0, m, r], fs[:, 1, m, r]),
                                        (wh[:, w:w + D], wl[:, w:w + D]), m == 0, m == 1)
                last.then_inc(F.ready(use), 1)
            elif name == "down":
                use, r = ("down", i), slice(i * P, (i + 1) * P)
                F.claim(pe, s, use)
                for m in range(INT // P):
                    w = DOWN + m * D
                    if m % 2 == 0:
                        after(pe, sq_low, s, m // 2 + 1)
                    last = matmul_split(pe, F[use], (gs[:, 0, m, r], gs[:, 1, m, r]),
                                        (wh[:, w:w + D], wl[:, w:w + D]), m == 0, m == INT // P - 1)
                last.then_inc(F.ready(use), 1)

        go(step, pe)
    return x2_stored


BODY1 = [("A", "load", 0), ("A", "load", 1), ("A", "split", 0), ("A", "split", 1), ("F", "cmix", 0),
         ("F", "cmix", 1), ("A", "mix", 0), ("F", "gate", 0), ("A", "quant", 0), ("A", "mix", 1), ("A", "quant", 1),
         ("F", "carry", 1), ("F", "g", 0), ("A", "turnx", 0), ("A", "qkv", 0), ("F", "carry", 0), ("F", "g", 1),
         ("A", "turnx", 1), ("F", "gturn", 0), ("A", "load2", 0), ("A", "qkv", 1), ("F", "u", 0), ("F", "send", 0),
         ("A", "turnk", 0), ("F", "spread", 0), ("F", "u", 1), ("A", "vrep", 0), ("F", "weigh", 0), ("A", "vrep", 1),
         ("A", "turnk", 1), ("F", "weigh", 1), ("A", "score", 0), ("F", "g", 2), ("A", "score", 1), ("F", "u", 2),
         ("A", "turnp", 0), ("F", "g", 3), ("F", "u", 3), ("A", "turnp", 1), ("A", "values", 0), ("A", "values", 1),
         ("F", "weigh", 2), ("F", "weigh", 3), ("A", "turno", 0), ("A", "turno", 1), ("F", "down", 0),
         ("A", "turnq", 0), ("A", "out", 0), ("A", "turnq", 1), ("A", "out", 1), ("A", "part", 0), ("F", "down", 1),
         ("A", "part", 1)]
ATTEND1 = [(name, i) for kind, name, i in BODY1 if kind == "A"]
FORWARD1 = [(name, i) for kind, name, i in BODY1 if kind == "F"]


def layer1(nc, ctx, t, sb, sem, scratch, psum, consts, weights, x2_stored, out):
    wh, wl, stage = weights
    ident, ones, vsel, dequant = (consts[k] for k in ("ident", "ones", "vsel", "dequant"))
    identb = sb("ident_bf16", [P, P], BF16)
    wbit = sb("ternary", [P, Q, 3 * P + 2 * D - P], BF16)
    WQ, WK, WO = 0, D, D + 2 * P
    lnw, lnb, cosw, sinw, kmask, vmask = (consts[k] for k in ("lnw", "lnb", "cosw", "sinw", "kmask1", "vmask1"))
    spread = sb("spread", [2 * C, EI], F32R)
    x2, x3 = stage[:, :, D:2 * D], sb("x3", [P, NT, D], F32)
    mixa, mixb = sb("mix1", [P, NT, 2, P], F32R), sb("mix2", [P, NT, 2, P], F32R)
    rowa, rowb = sb("bias_rows1", [2, ROUND], F32R), sb("bias_rows2", [2, ROUND], F32R)
    xs, xs3 = sb("x2_split", [P, NT, 2, D], F32R), sb("x3_split", [P, NT, 2, D], F32R)
    nrm = sb("normed", [P, NT, D], F32)
    xq = sb("quantized", [P, NT, D], BF16)
    xqT = sb("quantizedT", [P, NT, Q, P], BF16)
    rot = sb("roped", [P, NT, D + P], F32)
    rot2 = sb("roped_swapped", [P, D + P], F32)
    v = sb("v1", [P, NT, P], F32)
    vb = sb("v_blocks1", [P, NT, BT, P], F32)
    qT, kT = sb("qT1", [P, NT, BT, REP, C], F32), sb("kT1", [P, NT, P], F32)
    km = sb("k_masked1", [P, NT, BT, KV, C], F32)
    prob = sb("prob1", [P, NT, BT, KV, C], F32)
    spread32 = prob.rearrange("p i b g k -> p (i b g k)")[0:2 * C, 0:EI]
    pmax, psums = sb("prob_max1", [P, NT, BT, KV], F32), sb("prob_sum1", [P, NT, BT, KV], F32)
    stats, mv, rstd = sb("stats1", [P, NT, 6], F32), sb("mv1", [P, NT, 2], F32), sb("rstd1", [P, NT], F32)
    amax, scale = sb("abs_max", [P, NT, 2], F32), sb("quant_scale", [P, NT, 2], F32)
    back = sb("dequant_scale", [P, NT, 4], F32)
    x3c = sb("x3_carried", [P, NT, D], F32)
    hs = sb("z_split", [P, 2, Q, ROUND], F32R)
    logit, top, keys = sb("logits", [P, NT, NE1], F32), sb("top8", [P, NT, 8], F32), sb("top2", [P, NT, 8], F32)
    logitT = sb("logitsT", [NE1, ROUND], F32)
    left, share = sb("others", [P, NT, NE1], F32), sb("share", [P, NT, NE1], F32)
    esum = sb("share_sum", [P, NT], F32)
    wT = sb("shareT", [2 * C, ROUND], F32R)
    th, ga = sb("tanh", [P, 2, 2 * ROUND], F32), sb("gated", [P, 2, 2 * ROUND], F32)
    gs = sb("expert_split", [P, 2, M1, ROUND], F32R)
    z = sb("out_tile", [P, D], F32)

    def signal(name, per_round, unit=1):
        return Signal(sem("l1_" + name), per_round, unit)

    def many(names, per_round):
        return (signal(n, per_round) for n in names.split())

    x_in = [signal(f"x_in{i}", 1, 16) for i in range(NT)]
    mixa_in, mixb_in, zeroed = signal("mix1_in", BT + 1, 16), signal("mix2_in", BT + 1, 16), sem("l1_zeroed")
    x_high, x_low, x3_high, x3_low = many("x_high x_low x3_high x3_low", NT)
    stats_out, mv_out, var_out, normed = chain(sem("l1_norm"), "stats mv var normed", NT)
    absmax, clipped, inverted, factors, rounded, quantized = chain(
        sem("l1_quantize"), "absmax clipped inverted factors rounded quantized", NT)
    rstd_out = signal("rstd", NT)
    o_absmax, o_clipped, o_inverted, o_factors, o_quantized = chain(
        sem("l1_o_quantize"), "absmax clipped inverted factors quantized", NT)
    roped, added, k_masked = many("roped added k_masked", NT)
    smax, ssum, srecip = chain(sem("l1_softmax"), "max sum,recip", NT, 2)
    expd, pnormed = many("exp pnormed", 2 * NT)
    carried, z_high = signal("carried", NT), signal("z_high", NT)
    topped, keyed, below, replaced, chosen, shares, ssumed, inv_sum, share_out = chain(
        sem("l1_choice"), "topped keyed below replaced chosen shares summed inverted share", 1)
    exped = signal("choice_exp", 1)
    wT_high = signal("wT_high", 1)
    tanh_out, e_high, e_low = many("tanh e_high e_low", 4)
    z_added, z_stored = signal("z_added", NT), signal("z_stored", NT, 16)
    held = signal("held", 1)
    spread_in = sem("l1_spread_in")
    ternary_in = sem("l1_ternary_in")
    made = sem("l1_made")

    def uses(name, i):
        if name in ("load", "load2", "split", "quant", "part", "carry", "send"):
            return []
        if name in ("score", "turnp"):
            return [(name, 2 * i), (name, 2 * i + 1)]
        return [(n, i) for n in {"qkv": ("q", "kv"), "turnk": ("turnk_", "turnq_")}.get(name, (name,))]

    a_uses = [use for step in ATTEND1 for use in uses(*step)]
    f_uses = [use for step in FORWARD1 for use in uses(*step)]
    A = Banks(psum, 0, 4, a_uses, [sem(f"l1_a_ready{i}") for i in range(4)],
              [sem(f"l1_a_free{i}") for i in range(4)], held.sem)
    F = Banks(psum, 4, 4, f_uses, [sem(f"l1_f_ready{i}") for i in range(4)],
              [sem(f"l1_f_free{i}") for i in range(4)], held.sem)

    G_PIECES = Q * EI // (STAGE // EI * EI)
    buffers = [b.rearrange("p a n -> p (a n)") for b in (th, ga, x3c)]
    staging = Staging(sem, "l1_weights", stage_pieces(((GW, t["g1"], Q, EI), (UW, t["u1"], Q, EI),
                                                       (DW, t["d1"], M1, D))), buffers, wh, wl, len(ATTEND1),
                      ATTEND1.index(("mix", 0)), ATTEND1.index(("values", 1)))

    def go(steps, engine, weigh=None):
        for n, (name, i) in enumerate(ATTEND1):
            steps("A", name, i, 0)
            if engine is nc.sync:
                pieces = range(len(staging.pieces)) if name == "load2" else ()
            else:
                pieces = staging.after_step[n]
            for k in pieces if weigh else ():
                weigh(k)
        if weigh and engine is not nc.sync:
            staging.lows(engine, len(staging.pieces))
        for kind, name, i in BODY1:
            steps(kind, name, i, 1 if kind == "A" else 0)
        with engine.Fori(2, ROUNDS) as r:
            for kind, name, i in BODY1:
                steps(kind, name, i, r if kind == "A" else r - 1)
        for name, i in FORWARD1:
            steps("F", name, i, ROUNDS - 1)

    def cols(k):
        return min(2, M1 - 2 * k) * ROUND

    block = ctx.enter_context(nc.Block())

    @block.sync
    def _(sp):
        def step(kind, name, i, s):
            if name == "load":
                A.read(sp, s - 1, ("out", i))
                sp.sem_inc(held.sem, 1)
                sp.dma_start(x2[:, i, :], scratch["x2"][bass.ds(s * ROUND + i * P, P), :]).then_inc(x_in[i].sem, 16)
                if i == NT - 1:
                    A.read(sp, s - 1, *[("mix", j) for j in range(NT)])
                    sp.sem_inc(held.sem, 1)
                    if isinstance(s, int) and s == 0:
                        sp.wait_ge(zeroed, 1)
                    load_mix(sp, f32(mixa[:, :, :, :]), f32(rowa[:, :]), scratch, 1, s, mixa_in.sem)
                    if isinstance(s, int) and s == 0:
                        sp.dma_start(wbit[:, :, :], scratch["ternary"]).then_inc(ternary_in, 16)
                        sp.dma_start(spread32, t["spread"]).then_inc(spread_in, 16)
            elif name == "load2":
                F.read(sp, s - 1, *[("cmix", j) for j in range(NT)])
                sp.sem_inc(held.sem, 1)
                if isinstance(s, int) and s == 0:
                    sp.wait_ge(zeroed, 2)
                    for j in range(NT):
                        after(sp, x2_stored[j], ROUNDS - 1, 1)
                load_mix(sp, f32(mixb[:, :, :, :]), f32(rowb[:, :]), scratch, 2, s, mixb_in.sem)
            elif name == "down" and i == 0:
                send(s, 0)
            elif name == "send" and not (isinstance(s, int) and s == 0):
                send(s - 1, 1)

        def send(s, i):
            after(sp, z_added, s, i + 1)
            sp.sem_inc(held.sem, 1)
            sp.dma_start(out[bass.ds(s * ROUND + i * P, P), :], z[:, :]).then_inc(z_stored.sem, 16)

        go(step, sp, lambda k: staging.load(sp, k))
        send(ROUNDS - 1, 1)
        after(sp, z_stored, ROUNDS - 1, NT)

    @block.scalar
    def _(act):
        copy = lambda out, in_, **k: nc.scalar.activation(out, in_, ACT.Copy, **k)

        copy(identb[:, :], ident[:, :]).then_inc(made, 1)

        def step(kind, name, i, s):
            if name == "split":
                after(act, x_in[i], s, 1)
                A.read(act, s - 1, ("mix", i))
                copy(xs[:, i, 0, :], x2[:, i, :]).then_inc(x_high.sem, 1)
            elif name == "turnx":
                A.filled(act, s, ("turnx", i))
                copy(xqT[:, i, :, :], turned(("turnx", i))).then_inc(A.free(("turnx", i)), 1)
            elif name == "turnk":
                A.filled(act, s, ("turnk_", i))
                copy(kT[:, i, :], A[("turnk_", i)][:, 0:P]).then_inc(A.free(("turnk_", i)), 1)
                A.filled(act, s, ("turnq_", i))
                copy(qT[:, i, :, :, :].rearrange("p b r q -> p r b q"),
                     A[("turnq_", i)].rearrange("p (r b q) -> p r b q", r=REP, b=BT))\
                    .then_inc(A.free(("turnq_", i)), 1)
            elif name == "score":
                for j in (2 * i, 2 * i + 1):
                    A.read(act, s, ("score", j))
                    h = prob[:, i, 2 * (j % 2):2 * (j % 2) + 2, :, :]
                    nc.scalar.activation(h, h, ACT.Exp, scale=float(HD) ** -0.5).then_inc(expd.sem, 1)
            elif name == "turnp":
                for j in (2 * i, 2 * i + 1):
                    A.filled(act, s, ("turnp", j))
                    copy(km[:, i, 2 * (j % 2):2 * (j % 2) + 2, :, :].rearrange("p b g k -> p (b g k)"),
                         A[("turnp", j)]).then_inc(A.free(("turnp", j)), 1)
            elif name == "values":
                A.filled(act, s, ("values", i))
                copy(nrm[:, i, :].rearrange("p (r b q) -> p b r q", r=REP, b=BT),
                     A[("values", i)].rearrange("p (b r q) -> p b r q", r=REP, b=BT))\
                    .then_inc(A.free(("values", i)), 1)
            elif name == "turnq":
                A.filled(act, s, ("turnq", i))
                copy(xqT[:, i, :, :], turned(("turnq", i))).then_inc(A.free(("turnq", i)), 1)
            elif name == "carry":
                A.read(act, s, ("out", i))
                after(act, z_added, s - 1, i + 1)
                copy(x3c[:, i, :], x3[:, i, :]).then_inc(carried.sem, 1)
            elif name == "part":
                A.read(act, s, ("out", i))
                F.read(act, s - 1, ("cmix", i))
                copy(xs3[:, i, 0, :], x3[:, i, :]).then_inc(x3_high.sem, 1)
            elif name == "cmix":
                F.filled(act, s, ("cmix", i))
                F.read(act, s - 1, ("u", 3))
                copy(hs[:, 0, :, i * P:(i + 1) * P], F[("cmix", i)].rearrange("p (q n) -> p q n", q=Q))\
                    .then_inc(z_high.sem, 1)
            elif name == "gate":
                F.filled(act, s, ("gate", 0))
                copy(logitT[:, :], F[("gate", 0)][0:NE1, 0:ROUND]).then_inc(F.free(("gate", 0)), 1)
            elif name == "gturn":
                after(act, below, s, 1)
                nc.scalar.activation(share[:, :, :], share[:, :, :], ACT.Exp).then_inc(exped.sem, 1)
            elif name == "g":
                n = cols(i)
                F.filled(act, s, ("g", i))
                F.read(act, s if i >= 2 else s - 1, ("g", (i + 2) % 4))
                nc.scalar.activation(th[:, i % 2, 0:n], F[("g", i)][:, 0:n], ACT.Tanh, scale=0.5)\
                    .then_inc(tanh_out.sem, 1)
            elif name == "weigh":
                n = cols(i)
                F.read(act, s, ("weigh", i))
                if i == 0:
                    act.sem_inc(held.sem, 1)
                    F.read(act, s - 1, ("down", NT - 1))
                copy(gs[:, 0, 2 * i:2 * i + n // ROUND, :], ga[:, i % 2, 0:n].rearrange("p (m n) -> p m n", n=ROUND))\
                    .then_inc(e_high.sem, 1)

        def turned(use):
            return A[use][:, 0:D // 2].bitcast(BF16).rearrange("p (q n) -> p q n", q=Q)

        go(step, act, lambda k: staging.split_high(nc, act, k))

    @block.gpsimd
    def _(pool):
        nc.gpsimd.memset(f32(mixa[:, :, :, :]), 0.0).then_inc(zeroed, 1)
        nc.gpsimd.memset(f32(mixb[:, :, :, :]), 0.0).then_inc(zeroed, 1)
        nc.gpsimd.memset(keys[:, :, :], FAR)
        nc.gpsimd.memset(f32(wT[:, :]), 0.0).then_inc(made, 1)

        def step(kind, name, i, s):
            if name == "split":
                after(pool, x_high, s, i + 1)
                nc.gpsimd.tensor_tensor(xs[:, i, 1, :], x2[:, i, :], f32(xs[:, i, 0, :]), ALU.subtract)\
                    .then_inc(x_low.sem, 1)
            elif name == "mix":
                after(pool, var_out, s, i + 1)
                nc.gpsimd.tensor_tensor(rstd[:, i:i + 1], mv[:, i, 1:2], consts["minus_half"][:, :], ALU.pow)\
                    .then_inc(rstd_out.sem, 1)
            elif name == "qkv":
                after(pool, roped, s, i + 1)
                nc.gpsimd.tensor_tensor(rot[:, i, :], rot[:, i, :], rot2[:, :], ALU.add).then_inc(added.sem, 1)
            elif name == "turnk":
                A.read(pool, s, ("turnk_", i))
                nc.gpsimd.tensor_tensor(
                    km[:, i, :, :, :],
                    kT[:, i, :].rearrange("p (b k) -> p b k", b=BT).unsqueeze(2).broadcast_to([P, BT, KV, C]),
                    kmask[:, :].unsqueeze(1).unsqueeze(3).broadcast_to([P, BT, KV, C]), ALU.mult)\
                    .then_inc(k_masked.sem, 1)
            elif name == "score":
                for j in (0, 1):
                    after(pool, srecip, s, 2 * i + j + 1)
                    h = prob[:, i, 2 * j:2 * j + 2, :, :].rearrange("p b g k -> p (b g) k")
                    nc.gpsimd.tensor_tensor(
                        h, h, psums[:, i, 2 * j:2 * j + 2, :].rearrange("p b g -> p (b g)").unsqueeze(2)
                        .broadcast_to([P, 2 * KV, C]), ALU.mult).then_inc(pnormed.sem, 1)
            elif name == "part":
                after(pool, x3_high, s, i + 1)
                nc.gpsimd.tensor_tensor(xs3[:, i, 1, :], x3[:, i, :], f32(xs3[:, i, 0, :]), ALU.subtract)\
                    .then_inc(x3_low.sem, 1)
            elif name == "weigh":
                m = cols(i) // ROUND
                after(pool, e_high, s, i + 1)
                nc.gpsimd.tensor_tensor(gs[:, 1, 2 * i:2 * i + m, :],
                                        ga[:, i % 2, 0:m * ROUND].rearrange("p (m n) -> p m n", m=m),
                                        f32(gs[:, 0, 2 * i:2 * i + m, :]), ALU.subtract).then_inc(e_low.sem, 1)

        go(step, pool, lambda k: None if k % 2 else staging.split_low(nc.gpsimd, pool, k))

    @block.vector
    def _(dve):
        def quantize(src, i, which, s, done, clip, inv, fac, last):
            nc.vector.tensor_reduce(amax[:, i, which:which + 1], src, AX_X, ALU.max, apply_absolute_value=True)\
                .then_inc(done.sem, 1)
            after(dve, done, s, i + 1)
            a = amax[:, i, which:which + 1]
            nc.vector.tensor_scalar(a, a, 1e-5, None, ALU.max).then_inc(clip.sem, 1)
            after(dve, clip, s, i + 1)
            nc.vector.reciprocal(scale[:, i, which:which + 1], a).then_inc(inv.sem, 1)
            r = (0, 3) if which == 0 else (3, 4)
            nc.vector.tensor_scalar(back[:, i, r[0]:r[1]], dequant[:, r[0]:r[1]], a, None, ALU.mult)
            after(dve, inv, s, i + 1)
            nc.vector.tensor_scalar(scale[:, i, which:which + 1], scale[:, i, which:which + 1], QB, None, ALU.mult)\
                .then_inc(fac.sem, 1)
            after(dve, fac, s, i + 1)
            tmp = nrm[:, i, :] if which == 0 else rot[:, i, 0:D]
            nc.vector.tensor_scalar(tmp, src, scale[:, i, which:which + 1], ROUND_MAGIC, ALU.mult, ALU.add)\
                .then_inc(last, 1)

        def step(kind, name, i, s):
            if name == "mix":
                use = ("mix", i)
                A.filled(dve, s, use)
                nc.vector.bn_stats(stats[:, i, :], A[use]).then_inc(stats_out.sem, 1)
                after(dve, stats_out, s, i + 1)
                dve.sem_inc(held.sem, 1)
                nc.vector.bn_aggr(mv[:, i, :], stats[:, i, :]).then_inc(mv_out.sem, 1)
                after(dve, mv_out, s, i + 1)
                nc.vector.tensor_scalar(mv[:, i, 1:2], mv[:, i, 1:2], EPS, None, ALU.add).then_inc(var_out.sem, 1)
                if isinstance(s, int) and s == 0 and i == NT - 1:
                    dve.wait_ge(spread_in, 16)
                    nc.vector.tensor_copy(spread[:, :], spread32)
                nc.vector.scalar_tensor_tensor(out=nrm[:, i, :], in0=A[use], scalar=mv[:, i, 0:1], in1=lnw[:, :],
                                               op0=ALU.subtract, op1=ALU.mult).then_inc(A.free(use), 1)
                A.read(dve, s, use)
                after(dve, rstd_out, s, i + 1)
                nc.vector.scalar_tensor_tensor(out=nrm[:, i, :], in0=nrm[:, i, :], scalar=rstd[:, i:i + 1],
                                               in1=lnb[:, :], op0=ALU.mult, op1=ALU.add).then_inc(normed.sem, 1)
            elif name == "quant":
                after(dve, normed, s, i + 1)
                quantize(nrm[:, i, :], i, 0, s, absmax, clipped, inverted, factors, rounded.sem)
                after(dve, rounded, s, i + 1)
                nc.vector.tensor_scalar(xq[:, i, :], nrm[:, i, :], -ROUND_MAGIC, QB, ALU.add, ALU.min)\
                    .then_inc(quantized.sem, 1)
            elif name == "qkv":
                A.filled(dve, s, ("q", i))
                after(dve, added, s, i)
                for src, first, heads, which in ((A[("q", i)], 0, KV * REP, 0), (A[("kv", i)][:, 0:P], D, KV, 1)):
                    if which:
                        A.filled(dve, s, ("kv", i))
                    half = HD // 2
                    sv = src.rearrange("p (h d) -> p h d", d=HD)
                    o1 = rot[:, i, first:first + heads * HD].rearrange("p (h d) -> p h d", d=HD)
                    o2 = rot2[:, first:first + heads * HD].rearrange("p (h d) -> p h d", d=HD)
                    a = back[:, i, which:which + 1]

                    def table(w, lo, hi):
                        return w[:, lo:hi].unsqueeze(1).broadcast_to([P, heads, hi - lo])

                    nc.vector.scalar_tensor_tensor(out=o1, in0=sv, scalar=a, in1=table(cosw, 0, HD),
                                                   op0=ALU.mult, op1=ALU.mult)
                    nc.vector.scalar_tensor_tensor(out=o2[:, :, 0:half], in0=sv[:, :, half:HD], scalar=a,
                                                   in1=table(sinw, 0, half), op0=ALU.mult, op1=ALU.mult)
                    last = nc.vector.scalar_tensor_tensor(out=o2[:, :, half:HD], in0=sv[:, :, 0:half], scalar=a,
                                                          in1=table(sinw, half, HD), op0=ALU.mult, op1=ALU.mult)
                    if which == 0:
                        last.then_inc(A.free(("q", i)), 1)
                    else:
                        last.then_inc(roped.sem, 1)
                nc.vector.tensor_scalar(v[:, i, :], A[("kv", i)][:, P:2 * P], back[:, i, 2:3], None, ALU.mult)\
                    .then_inc(A.free(("kv", i)), 1)
            elif name == "vrep":
                A.filled(dve, s, ("vrep", i))
                nc.vector.tensor_tensor(
                    vb[:, i, :, :].rearrange("p b (g h e) -> p (b g) h e", g=2, e=HD),
                    A[("vrep", i)].rearrange("p (b g h e) -> p (b g) h e", b=BT, g=2, e=HD),
                    vmask[:, :].unsqueeze(1).unsqueeze(3).broadcast_to([P, 2 * BT, 4, HD]), ALU.mult)\
                    .then_inc(A.free(("vrep", i)), 1)
            elif name == "score":
                for j in (0, 1):
                    n = 2 * i + j
                    A.filled(dve, s, ("score", n))
                    bank = A[("score", n)].rearrange("p (b k) -> p b k", k=C)
                    m = pmax[:, i, 2 * j:2 * j + 2, :].rearrange("p b g -> p (b g)")
                    nc.vector.tensor_reduce(m, bank, AX_X, ALU.max).then_inc(smax.sem, 1)
                    after(dve, smax, s, n + 1)
                    nc.vector.tensor_tensor(prob[:, i, 2 * j:2 * j + 2, :, :].rearrange("p b g k -> p (b g) k"), bank,
                                            m.unsqueeze(2).broadcast_to([P, 2 * KV, C]), ALU.subtract)\
                        .then_inc(A.free(("score", n)), 1)
                for j in (0, 1):
                    n = 2 * i + j
                    after(dve, expd, s, n + 1)
                    m = psums[:, i, 2 * j:2 * j + 2, :].rearrange("p b g -> p (b g)")
                    nc.vector.tensor_reduce(m, prob[:, i, 2 * j:2 * j + 2, :, :].rearrange("p b g k -> p (b g) k"),
                                            AX_X, ALU.add).then_inc(ssum.sem, 1)
                    after(dve, ssum, s, n + 1)
                    nc.vector.reciprocal(m, m).then_inc(srecip.sem, 1)
            elif name == "turno":
                use = ("turno", i)
                A.filled(dve, s, use)
                quantize(A[use], i, 1, s, o_absmax, o_clipped, o_inverted, o_factors, A.free(use))
                A.read(dve, s, use)
                nc.vector.tensor_scalar(xq[:, i, :], rot[:, i, 0:D], -ROUND_MAGIC, QB, ALU.add, ALU.min)\
                    .then_inc(o_quantized.sem, 1)
            elif name == "out":
                A.filled(dve, s, ("out", i))
                after(dve, carried, s - 1, i + 1)
                after(dve, x3_low, s - 1, i + 1)
                nc.vector.scalar_tensor_tensor(out=x3[:, i, :], in0=A[("out", i)], scalar=back[:, i, 3:4],
                                               in1=x2[:, i, :], op0=ALU.mult, op1=ALU.add)\
                    .then_inc(A.free(("out", i)), 1)
            elif name == "cmix":
                after(dve, z_high, s, i + 1)
                nc.vector.tensor_tensor(hs[:, 1, :, i * P:(i + 1) * P],
                                        F[("cmix", i)].rearrange("p (q n) -> p q n", q=Q),
                                        f32(hs[:, 0, :, i * P:(i + 1) * P]), ALU.subtract)\
                    .then_inc(F.free(("cmix", i)), 1)
            elif name == "gturn":
                F.filled(dve, s, ("gturn", 0))
                nc.vector.tensor_copy(logit[:, :, :],
                                      F[("gturn", 0)][:, 0:NT * NE1].rearrange("p (j e) -> p j e", j=NT))\
                    .then_inc(F.free(("gturn", 0)), 1)
                F.read(dve, s, ("gturn", 0))
                dve.sem_inc(held.sem, 1)
                for j in range(NT):
                    last = nc.vector.max(top[:, j, :], logit[:, j, :])
                last.then_inc(topped.sem, 1)
                after(dve, topped, s, 1)
                nc.vector.tensor_copy(keys[:, :, 0:2], top[:, :, 0:2]).then_inc(keyed.sem, 1)
                nc.vector.tensor_tensor(share[:, :, :], logit[:, :, :], top[:, :, 0:1].broadcast_to([P, NT, NE1]),
                                        ALU.subtract).then_inc(below.sem, 1)
                after(dve, keyed, s, 1)
                dve.sem_inc(held.sem, 1)
                for j in range(NT):
                    last = nc.vector.match_replace(left[:, j, :], keys[:, j, :], logit[:, j, :], -FAR)
                last.then_inc(replaced.sem, 1)
                after(dve, replaced, s, 1)
                nc.vector.tensor_tensor(left[:, :, :], left[:, :, :], logit[:, :, :], ALU.not_equal)\
                    .then_inc(chosen.sem, 1)
                after(dve, chosen, s, 1)
                after(dve, exped, s, 1)
                nc.vector.tensor_tensor(share[:, :, :], share[:, :, :], left[:, :, :], ALU.mult).then_inc(shares.sem, 1)
                after(dve, shares, s, 1)
                nc.vector.tensor_reduce(esum[:, :], share[:, :, :], AX_X, ALU.add).then_inc(ssumed.sem, 1)
                after(dve, ssumed, s, 1)
                nc.vector.reciprocal(esum[:, :], esum[:, :]).then_inc(inv_sum.sem, 1)
                after(dve, inv_sum, s, 1)
                nc.vector.scalar_tensor_tensor(out=share[:, :, :], in0=share[:, :, :], scalar=0.5,
                                               in1=esum[:, :].unsqueeze(2).broadcast_to([P, NT, NE1]),
                                               op0=ALU.mult, op1=ALU.mult).then_inc(share_out.sem, 1)
            elif name == "spread":
                use = ("spread", 0)
                F.filled(dve, s, use)
                F.read(dve, s - 1, ("weigh", 3))
                nc.vector.tensor_copy(wT[0:NE1, :], F[use][0:NE1, 0:ROUND]).then_inc(wT_high.sem, 1)
                after(dve, wT_high, s, 1)
                nc.vector.tensor_tensor(wT[C:C + NE1, :], F[use][0:NE1, 0:ROUND], f32(wT[0:NE1, :]), ALU.subtract)\
                    .then_inc(F.free(use), 1)
            elif name == "g":
                n = cols(i)
                a = ga[:, i % 2, 0:n]
                after(dve, tanh_out, s, i + 1)
                after(dve, e_low, s, i - 1)
                nc.vector.scalar_tensor_tensor(out=a, in0=th[:, i % 2, 0:n], scalar=1.0, in1=F[("g", i)][:, 0:n],
                                               op0=ALU.add, op1=ALU.mult).then_inc(F.free(("g", i)), 1)
            elif name == "u":
                n = cols(i)
                a = ga[:, i % 2, 0:n]
                F.read(dve, s, ("g", i))
                F.filled(dve, s, ("u", i))
                nc.vector.tensor_tensor(a, a, F[("u", i)][:, 0:n], ALU.mult).then_inc(F.free(("u", i)), 1)
            elif name == "weigh":
                n = cols(i)
                a = ga[:, i % 2, 0:n]
                F.read(dve, s, ("u", i))
                F.filled(dve, s, ("weigh", i))
                nc.vector.tensor_tensor(a, a, F[("weigh", i)][:, 0:n], ALU.mult).then_inc(F.free(("weigh", i)), 1)
            elif name == "down":
                F.filled(dve, s, ("down", i))
                after(dve, carried, s, i + 1)
                after(dve, z_stored, s, i)
                nc.vector.tensor_tensor(z[:, :], F[("down", i)], x3c[:, i, :], ALU.add)\
                    .then_inc(z_added.sem, 1)
                after(dve, z_added, s, i + 1)
                dve.sem_inc(F.free(("down", i)), 1)

        go(step, dve, lambda k: staging.split_low(nc.vector, dve, k) if k % 2 else None)

    @block.tensor
    def _(pe):
        mm = nc.tensor.matmul

        def turn_bf16(use, src):
            bank = A[use][:, 0:D // 2].bitcast(BF16)
            for q in range(Q):
                last = nc.tensor.transpose(bank[:, q * P:(q + 1) * P], src[:, q * P:(q + 1) * P], identb[:, :])
            last.then_inc(A.ready(use), 1)

        def step(kind, name, i, s):
            r = slice(i * P, (i + 1) * P)
            if isinstance(s, int) and s == 0 and (name, i) == ("turnx", 0):
                pe.wait_ge(ternary_in, 16)
                pe.wait_ge(made, 2)
            if name == "mix":
                use = ("mix", i)
                after(pe, x_low, s, i + 1)
                A.claim(pe, s, use)
                after(pe, mixa_in, s, BT + 1)
                mm(A[use], rowa[:, r], ones[0:2, :], start=True, stop=False)
                matmul_split(pe, A[use], (mixa[:, i, 0, :], mixa[:, i, 1, :]), (xs[:, i, 0, :], xs[:, i, 1, :]),
                             False, True).then_inc(A.ready(use), 1)
            elif name == "turnx":
                after(pe, quantized, s, i + 1)
                A.claim(pe, s, ("turnx", i))
                turn_bf16(("turnx", i), xq[:, i, :])
            elif name == "qkv":
                for use, first, n in ((("q", i), WQ, D), (("kv", i), WK, 2 * P)):
                    A.read(pe, s, ("turnx", i), claim=use)
                    for q in range(Q):
                        last = mm(A[use][:, 0:n], xqT[:, i, q, :], wbit[:, q, first:first + n],
                                  start=(q == 0), stop=(q == Q - 1))
                    last.then_inc(A.ready(use), 1)
            elif name == "turnk":
                after(pe, added, s, i + 1)
                A.claim(pe, s, ("turnk_", i))
                nc.tensor.transpose(A[("turnk_", i)][:, 0:P], rot[:, i, D:D + P], ident[:, :])\
                    .then_inc(A.ready(("turnk_", i)), 1)
                A.claim(pe, s, ("turnq_", i))
                for k in range(REP):
                    last = nc.tensor.transpose(A[("turnq_", i)][:, k * P:(k + 1) * P], rot[:, i, k * P:(k + 1) * P],
                                               ident[:, :])
                last.then_inc(A.ready(("turnq_", i)), 1)
            elif name == "vrep":
                A.read(pe, s, ("kv", i), claim=("vrep", i))
                for b in range(BT):
                    last = mm(A[("vrep", i)][:, b * P:(b + 1) * P], vsel[:, b, :], v[:, i, :], start=True, stop=True)
                last.then_inc(A.ready(("vrep", i)), 1)
            elif name == "score":
                after(pe, k_masked, s, i + 1)
                for j in (0, 1):
                    use = ("score", 2 * i + j)
                    A.read(pe, s, ("turnq_", i), claim=use)
                    for b in (2 * j, 2 * j + 1):
                        last = mm(A[use][:, (b % 2) * 256:(b % 2 + 1) * 256],
                                  qT[:, i, b, :, :].rearrange("p r q -> p (r q)"),
                                  km[:, i, b, :, :].rearrange("p g k -> p (g k)"), start=True, stop=True)
                    last.then_inc(A.ready(use), 1)
            elif name == "turnp":
                for j in (0, 1):
                    use = ("turnp", 2 * i + j)
                    after(pe, pnormed, s, 2 * i + j + 1)
                    A.claim(pe, s, use)
                    for k in range(4):
                        b, h = 2 * j + k // 2, k % 2
                        last = nc.tensor.transpose(A[use][:, k * P:(k + 1) * P],
                                                   prob[:, i, b, 4 * h:4 * h + 4, :].rearrange("p g k -> p (g k)"),
                                                   ident[:, :])
                    last.then_inc(A.ready(use), 1)
            elif name == "values":
                use = ("values", i)
                A.read(pe, s, ("turnp", 2 * i + 1), ("vrep", i), claim=use)
                for b in range(BT):
                    for h in range(2):
                        last = mm(A[use][64 * h:64 * h + 64, b * P:(b + 1) * P], vb[:, i, b, 64 * h:64 * h + 64],
                                  km[:, i, b, 4 * h:4 * h + 4, :].rearrange("p g k -> p (g k)"), start=True, stop=True)
                last.then_inc(A.ready(use), 1)
            elif name == "turno":
                use = ("turno", i)
                A.read(pe, s, ("values", i), claim=use)
                for k in range(REP):
                    last = nc.tensor.transpose(A[use][:, k * P:(k + 1) * P], nrm[:, i, k * P:(k + 1) * P], ident[:, :])
                last.then_inc(A.ready(use), 1)
            elif name == "turnq":
                after(pe, o_quantized, s, i + 1)
                A.claim(pe, s, ("turnq", i))
                turn_bf16(("turnq", i), xq[:, i, :])
            elif name == "out":
                use = ("out", i)
                A.read(pe, s, ("turnq", i), claim=use)
                for q in range(Q):
                    last = mm(A[use], xqT[:, i, q, :], wbit[:, q, WO:WO + D], start=(q == 0), stop=(q == Q - 1))
                last.then_inc(A.ready(use), 1)
            elif name == "cmix":
                use = ("cmix", i)
                after(pe, x3_low, s, i + 1)
                after(pe, mixb_in, s, BT + 1)
                F.claim(pe, s, use)
                bank = F[use]
                mm(bank.rearrange("p (q n) -> p q n", q=Q), ones[0:2, 0:P],
                   rowb[:, r].unsqueeze(1).broadcast_to([2, Q, P]), start=True, stop=False)
                for q in range(Q):
                    w = slice(q * P, (q + 1) * P)
                    last = matmul_split(pe, bank[:, w], (xs3[:, i, 0, w], xs3[:, i, 1, w]),
                                        (mixb[:, i, 0, :], mixb[:, i, 1, :]), False, q == Q - 1)
                last.then_inc(F.ready(use), 1)
            elif name == "gate":
                use = ("gate", 0)
                F.read(pe, s, *[("cmix", j) for j in range(NT)], claim=use)
                gate_h, gate_l = consts["gate1"]
                for q in range(Q):
                    w = slice(q * NE1, (q + 1) * NE1)
                    last = matmul_split(pe, F[use][0:NE1, 0:ROUND], (gate_h[:, w], gate_l[:, w]),
                                        (hs[:, 0, q, :], hs[:, 1, q, :]), q == 0, q == Q - 1)
                last.then_inc(F.ready(use), 1)
            elif name == "gturn":
                use = ("gturn", 0)
                F.read(pe, s, ("gate", 0), claim=use)
                pe.sem_inc(held.sem, 1)
                for j in range(NT):
                    last = nc.tensor.transpose(F[use][:, j * NE1:(j + 1) * NE1], logitT[:, j * P:(j + 1) * P],
                                               ident[0:NE1, 0:NE1])
                last.then_inc(F.ready(use), 1)
            elif name == "spread":
                use = ("spread", 0)
                after(pe, share_out, s, 1)
                F.claim(pe, s, use)
                for j in range(NT):
                    last = nc.tensor.transpose(F[use][0:NE1, j * P:(j + 1) * P], share[:, j, :], ident[:, :])
                last.then_inc(F.ready(use), 1)
            elif name in ("g", "u"):
                if isinstance(s, int) and s == 0 and i == 0:
                    staging.lows(pe, G_PIECES if name == "g" else 2 * G_PIECES)
                use, first = (name, i), GW if name == "g" else UW
                F.read(pe, s, *[("cmix", j) for j in range(NT)], claim=use)
                for m in range(2 * i, min(2 * i + 2, M1)):
                    for q in range(Q):
                        w = slice(first + q * EI + m * P, first + q * EI + (m + 1) * P)
                        last = matmul_split(pe, F[use][:, (m % 2) * ROUND:(m % 2 + 1) * ROUND],
                                            (wh[:, w], wl[:, w]), (hs[:, 0, q, :], hs[:, 1, q, :]),
                                            q == 0, q == Q - 1)
                last.then_inc(F.ready(use), 1)
            elif name == "weigh":
                use = ("weigh", i)
                F.read(pe, s, ("spread", 0), claim=use)
                for m in range(2 * i, min(2 * i + 2, M1)):
                    last = mm(F[use][:, (m % 2) * ROUND:(m % 2 + 1) * ROUND], spread[:, m * P:(m + 1) * P], wT[:, :],
                              start=True, stop=True)
                last.then_inc(F.ready(use), 1)
            elif name == "down":
                use = ("down", i)
                if isinstance(s, int) and s == 0 and i == 0:
                    staging.lows(pe, len(staging.pieces))
                F.claim(pe, s, use)
                for m in range(M1):
                    if m % 2 == 0:
                        after(pe, e_low, s, m // 2 + 1)
                    w = slice(DW + m * D, DW + (m + 1) * D)
                    last = matmul_split(pe, F[use], (gs[:, 0, m, r], gs[:, 1, m, r]), (wh[:, w], wl[:, w]),
                                        m == 0, m == M1 - 1)
                last.then_inc(F.ready(use), 1)

        go(step, pe)


_TENSORS = ["x", "embT", "cond_w0", "cond_w1", "cond_w2", "cond_b01", "cond_b2", "cond_wk", "cond_bk", "cwT", "side",
            "expert", "bqkv0", "wo0", "bo0", "fc1T", "gamma", "beta", "mask0", "vmask0", "vsel", "qkv0", "conv",
            "gate0", "up", "down", "fc2", "bits", "gate1", "g1", "u1", "d1", "ln_w", "ln_b", "spread", "rope_cos",
            "rope_sin", "kmask", "vmask"]


def program(nc, t, out):
    scratch = {
        "mix": nc.dram_tensor("scratch_mix", (CONDS, BT, C, TILES, 2 * C), F32, kind="Internal").ap(),
        "ternary": nc.dram_tensor("scratch_ternary", (P, Q, 2 * D + 2 * P), BF16, kind="Internal").ap(),
        "rows": nc.dram_tensor("scratch_rows", (CONDS * 2, TOKENS), F32, kind="Internal").ap(),
        "context": nc.dram_tensor("scratch_context", (P, B), F32, kind="Internal").ap(),
        "x1": nc.dram_tensor("scratch_x1", (TOKENS, D), F32, kind="Internal").ap(),
        "x2": nc.dram_tensor("scratch_x2", (TOKENS, D), F32, kind="Internal").ap(),
    }
    with ExitStack() as ctx:
        def sem(name):
            return ctx.enter_context(nc.semaphore(name))

        def tensors(scope):
            return lambda name, shape, dtype: scope.enter_context(nc.sbuf_tensor(name, shape, dtype))

        sb = tensors(ctx)
        psum = ctx.enter_context(nc.psum_tensor("psum", [P, 8, 512], F32))
        weights = (sb("w_high", [P, WCOLS], F32R), sb("w_low", [P, WCOLS], F32R), sb("stage", [P, 2, STAGE], F32))
        consts = {
            "ident": sb("ident", [P, P], F32),
            "ones": sb("ones", [P, D], F32R),
            "gate1": [sb(f"gate1_{n}", [P, Q * NE1], F32R) for n in ("high", "low")],
            "dequant": sb("dequant", [P, 4], F32),
            "minus_half": sb("minus_half", [P, 1], F32),
            "vsel": sb("vsel", [P, BT, P], F32),
            "lnw": sb("ln_w", [P, D], F32), "lnb": sb("ln_b", [P, D], F32),
            "cosw": sb("rope_cos", [P, HD], F32), "sinw": sb("rope_sin", [P, HD], F32),
            "kmask1": sb("kmask1", [P, KV], F32), "vmask1": sb("vmask1", [P, 4], F32),
        }
        with ExitStack() as layer:
            sb0 = tensors(layer)
            consts.update({
                "qkv_h": sb0("qkv_high", [P, Q * 192], F32R), "qkv_l": sb0("qkv_low", [P, Q * 192], F32R),
                "bqkv": sb0("bqkv", [2 * C, 192], F32R),
                "out_w": sb0("out_w", [P, 2, D], F32R),
                "out_b": sb0("out_b", [P, NT, P], F32R),
                "halo": sb0("x1_phase", [P, NT * BT, P + 2], F32),
                "gamma": sb0("gamma", [P, D], F32), "beta": sb0("beta", [P, D], F32),
                "mask0": sb0("mask0", [H0 * E0, H0], F32), "vmask0": sb0("vmask0", [P, 4], F32),
            })
            with ExitStack() as scope:
                prepare(nc, scope, t, tensors(scope), sem, scratch, psum, consts, weights)
            with ExitStack() as scope:
                x2_stored = layer0(nc, scope, t, tensors(scope), sem, scratch, psum, consts, weights)
        with ExitStack() as scope:
            layer1(nc, scope, t, tensors(scope), sem, scratch, psum, consts, weights, x2_stored, out)


def _layouts(a):
    n = {k: np.ascontiguousarray(v) for k, v in a.items()}
    zero = np.zeros

    def rows(w):
        return np.ascontiguousarray(w.reshape(P, Q, -1).transpose(1, 0, 2).reshape(D, -1))

    def cols(w):
        w = w.reshape(-1, D)
        return np.ascontiguousarray(w.reshape(-1, P, Q).transpose(0, 2, 1).reshape(-1, D))

    conds = ["L0_cond", "L1_cond", "L1_cond2"]
    stack = lambda f: np.concatenate([np.ascontiguousarray(f(n, c)) for c in conds], axis=0)
    t = {
        "x": cols(n["x"]),
        "embT": np.ascontiguousarray(n["cond_128"].T),
        "cond_w0": stack(lambda n, c: n[c + "_W0"]),
        "cond_w1": stack(lambda n, c: n[c + "_W1"]),
        "cond_w2": stack(lambda n, c: n[c + "_W2"]),
        "cond_b01": stack(lambda n, c: np.stack([n[c + "_b0"], n[c + "_b1"]], axis=1)),
        "cond_b2": stack(lambda n, c: n[c + "_b2"][None]),
        "cond_wk": stack(lambda n, c: n[c + "_weight"][..., 0].transpose(0, 2, 1).reshape(KE, C * C)),
        "cond_bk": stack(lambda n, c: n[c + "_bias_k"]),
        "cwT": np.tile(n["L0_cond2_c_weight"].T, (1, Q)),
        "side": np.tile(n["fside_S_0"], Q)[:, None],
        "expert": n["L0_ffn_expert_w"],
    }
    wqk, bqk = n["L0_attn_Wqk_w"], n["L0_attn_Wqk_b"]
    t["qkv0"] = rows(np.concatenate([wqk[0::2], wqk[1::2], n["L0_attn_Wv_w"]], axis=0).T)
    t["bqkv0"] = np.concatenate([bqk[0::2], bqk[1::2], n["L0_attn_Wv_b"]])[None]
    t["wo0"] = cols(np.ascontiguousarray(n["L0_attn_Wo_w"].T))
    t["bo0"] = cols(n["L0_attn_Wo_b"])
    t["fc1T"] = np.ascontiguousarray(rows(n["L0_ffn_fc1_w"]).T)
    t["gamma"], t["beta"] = cols(n["L0_ffn_ln_gamma"]), cols(n["L0_ffn_ln_beta"])
    w = n["L0_cond2_weight"]
    per = C // GROUPS
    conv = zero((3, Q, C, Q, C), np.float32)
    for shift in range(3):
        for p in range(Q):
            for q in range(Q):
                tap = 4 * shift + p - q
                if 0 <= tap < TAPS:
                    for g in range(GROUPS):
                        r = slice(g * per, (g + 1) * per)
                        conv[shift, p, r, q, r] = w[r, :, tap].T
    t["conv"] = conv.reshape(3 * P, P)
    t["gate0"] = rows(n["L0_ffn_gate_w"])
    t["up"] = rows(n["L0_ffn_up_w"])
    t["down"] = cols(n["L0_ffn_down_w"])
    t["fc2"] = cols(n["L0_ffn_fc2_w"])
    t["mask0"] = np.repeat(np.eye(H0, dtype=np.float32), E0, axis=0)
    t["vmask0"] = np.repeat(np.eye(4, dtype=np.float32), C, axis=0) * np.float32((H0 * E0) ** -0.5)
    def heads(w):
        return w.reshape(KV, REP, HD, -1).transpose(1, 0, 2, 3).reshape(D, -1)

    qkv = np.concatenate([heads(n["L1_attn_Wq"]), n["L1_attn_Wk"], n["L1_attn_Wv"]], axis=0)
    wo = heads(np.ascontiguousarray(n["L1_attn_Wo"].T))
    t["bits"] = np.concatenate([rows(np.ascontiguousarray(qkv.T)), cols(wo)], axis=1)
    t["gate1"] = rows(np.ascontiguousarray(n["L1_ffn_gate_w"].T))
    t["g1"] = rows(np.ascontiguousarray(n["L1_ffn_g"].T))
    t["u1"] = rows(np.ascontiguousarray(n["L1_ffn_u"].T))
    t["d1"] = cols(np.ascontiguousarray(n["L1_ffn_d"].T))
    t["ln_w"], t["ln_b"] = cols(n["L1_attn_ln_w"]), cols(n["L1_attn_ln_b"])
    spread = zero((2 * C, EI), np.float32)
    for e in range(NE1):
        spread[[e, C + e], e * INTER:(e + 1) * INTER] = 1.0
    t["spread"] = spread
    inv = (1.0 / np.float32(10000.0) ** (np.arange(0, HD, 2, dtype=np.float32) / np.float32(HD))).astype(np.float32)
    angle = np.tile(np.arange(C, dtype=np.float32)[:, None] * inv[None, :], (BT, 2))
    t["rope_cos"] = np.cos(angle).astype(np.float32)
    t["rope_sin"] = (np.sin(angle) * np.repeat([-1.0, 1.0], HD // 2)).astype(np.float32)
    t["kmask"] = np.repeat(np.eye(KV, dtype=np.float32), HD, axis=0)
    t["vmask"] = np.repeat(np.eye(4, dtype=np.float32), C, axis=0)
    sel = zero((BT, C, BT, 4, C), np.float32)
    for b in range(BT):
        for k in range(4):
            sel[b, :, b, k, :] = np.eye(C, dtype=np.float32)
    t["vsel"] = sel.reshape(P, BT, P)
    return t


def kernel(**inputs):
    import concourse.bacc as _bacc
    from concourse import mybir as _mybir
    from concourse.bass_utils import run_bass_kernel_spmd as _run

    nc = _bacc.Bacc("TRN2", target_bir_lowering=False, num_devices=1, dynamic_dma_scratch_size=1024)
    laid = _layouts({k: np.asarray(v) for k, v in inputs.items()})
    arrays, t = {}, {}
    for name in _TENSORS:
        a = np.ascontiguousarray(laid[name])
        arrays["in_" + name] = a
        t[name] = nc.dram_tensor("in_" + name, a.shape, _mybir.dt.from_np(a.dtype), kind="ExternalInput").ap()
    out = nc.dram_tensor("out_dram", (TOKENS, D), F32, kind="ExternalOutput").ap()
    program(nc, t, out)
    r = _run(nc, [arrays], core_ids=[0])
    got = r.results[0]["out_dram"]
    return np.ascontiguousarray(got.reshape(B, C, Q, P).transpose(0, 1, 3, 2)).reshape(B, C, D)
```
